# Optimizing a Trainium2 kernel written in Bass

```python
import numpy as np
import jax
import jax.numpy as jnp

def _softmax(x, axis=-1):
    return jax.nn.softmax(x, axis=axis)

def _gelu(x):
    return jax.nn.gelu(x, approximate=True)

def _silu(x):
    return jax.nn.silu(x)

def _sigmoid(x):
    return jax.nn.sigmoid(x)

def _layernorm(x, axis=-1, eps=1e-05):
    m = jnp.mean(x, axis=axis, keepdims=True)
    v = jnp.var(x, axis=axis, keepdims=True)
    return (x - m) / jnp.sqrt(v + eps)

def _scatter_add(tgt, idx, src, axis=0):
    return tgt.at[idx].add(src)

def _segment_sum(src, seg, n):
    return jax.ops.segment_sum(src, seg, n)
kernel_name = 'mk_cond_resid_d2_seqx_r4_2562d1'

def setup_inputs(seed: int=0):
    np.random.seed(seed)
    _w = jnp.asarray

    def _rec_inputs():
        import jax
        import jax.numpy as jnp
        _rk = jax.random.key(seed)
        x = -1.394e-06 + 0.9999 * jax.random.normal(jax.random.fold_in(_rk, 1), (64, 64, 512), jnp.float32)
        _lenS = 64 - jax.random.randint(jax.random.fold_in(_rk, 7), (64,), 0, max(1, 64 // 4) + 1, jnp.int32)
        _lenS2 = 64 - jax.random.randint(jax.random.fold_in(_rk, 8), (64,), 0, max(1, 64 // 4) + 1, jnp.int32)
        cond_2048 = -0.00499425 + 1.0058 * jax.random.normal(jax.random.fold_in(_rk, 11), (64, 512), jnp.float32)
        return (x, cond_2048)
    x, cond_2048 = _rec_inputs()

    def _L0_cond_setup():
        import jax, jax.numpy as jnp
        import numpy as np
        B, T, D = (16, 128, 512)
        key = jax.random.key(seed)
        k0, k1, k2, k3 = jax.random.split(key, 4)
        scale = 1.0 / np.sqrt(D)
        return {'initial_state': jax.random.normal(k0, (B, D), jnp.float32), 'inputs': jax.random.normal(k1, (B, T, D), jnp.float32), 'W_ih': jax.random.normal(k2, (D, 3 * D), jnp.float32) * scale, 'W_hh': jax.random.normal(k3, (D, 3 * D), jnp.float32) * scale, 'b_ih': jnp.zeros((3 * D,), jnp.float32), 'b_hh': jnp.zeros((3 * D,), jnp.float32)}
    _L0_cond_all = _L0_cond_setup()
    _L0_cond_in = {k: v for k, v in _L0_cond_all.items() if k in ('W_ih', 'W_hh', 'b_ih', 'b_hh')}
    del _L0_cond_all

    def _L1_cond_setup():
        import jax, jax.numpy as jnp
        import numpy as np
        DIM = 512
        H = 16
        DH = 128
        INNER = H * DH
        MLP = 4 * DIM
        B, T = (2, 512)
        EPS = 1e-06

        def _ln(x):
            mu = jnp.mean(x, axis=-1, keepdims=True)
            var = jnp.var(x, axis=-1, keepdims=True)
            return (x - mu) * jax.lax.rsqrt(var + EPS)
        key = jax.random.key(seed)
        ks = jax.random.split(key, 12)
        s = 0.02
        return {'x': jax.random.normal(ks[0], (B, T, DIM), jnp.float32), 'timestep_embed': jax.random.normal(ks[1], (B, DIM), jnp.float32), 'ada_w': jax.random.normal(ks[2], (DIM, 6 * DIM), jnp.float32) * s, 'ada_b': jnp.zeros((6 * DIM,), jnp.float32), 'qkv_w': jax.random.normal(ks[3], (DIM, 3 * INNER), jnp.float32) * s, 'qkv_b': jnp.zeros((3 * INNER,), jnp.float32), 'out_w': jax.random.normal(ks[4], (INNER, DIM), jnp.float32) * s, 'out_b': jnp.zeros((DIM,), jnp.float32), 'ffn_w1': jax.random.normal(ks[5], (DIM, MLP), jnp.float32) * s, 'ffn_b1': jnp.zeros((MLP,), jnp.float32), 'ffn_w2': jax.random.normal(ks[6], (MLP, DIM), jnp.float32) * s, 'ffn_b2': jnp.zeros((DIM,), jnp.float32)}
    _L1_cond_all = _L1_cond_setup()
    _L1_cond_in = {k: v for k, v in _L1_cond_all.items() if k in ('ada_w', 'ada_b', 'qkv_w', 'qkv_b', 'out_w', 'out_b', 'ffn_w1', 'ffn_b1', 'ffn_w2', 'ffn_b2')}
    del _L1_cond_all
    return {'x': x, 'cond_2048': cond_2048, 'L0_cond_W_ih': _L0_cond_in['W_ih'], 'L0_cond_W_hh': _L0_cond_in['W_hh'], 'L0_cond_b_ih': _L0_cond_in['b_ih'], 'L0_cond_b_hh': _L0_cond_in['b_hh'], 'L1_cond_ada_w': _L1_cond_in['ada_w'], 'L1_cond_ada_b': _L1_cond_in['ada_b'], 'L1_cond_qkv_w': _L1_cond_in['qkv_w'], 'L1_cond_qkv_b': _L1_cond_in['qkv_b'], 'L1_cond_out_w': _L1_cond_in['out_w'], 'L1_cond_out_b': _L1_cond_in['out_b'], 'L1_cond_ffn_w1': _L1_cond_in['ffn_w1'], 'L1_cond_ffn_b1': _L1_cond_in['ffn_b1'], 'L1_cond_ffn_w2': _L1_cond_in['ffn_w2'], 'L1_cond_ffn_b2': _L1_cond_in['ffn_b2']}

def reference(x, cond_2048, L0_cond_W_ih, L0_cond_W_hh, L0_cond_b_ih, L0_cond_b_hh, L1_cond_ada_w, L1_cond_ada_b, L1_cond_qkv_w, L1_cond_qkv_b, L1_cond_out_w, L1_cond_out_b, L1_cond_ffn_w1, L1_cond_ffn_b1, L1_cond_ffn_w2, L1_cond_ffn_b2):
    import jax
    import jax.numpy as jnp

    def _L0_cond_ref(initial_state, inputs, W_ih, W_hh, b_ih, b_hh):
        import jax, jax.numpy as jnp
        import numpy as np
        B, T, D = (16, 128, 512)
        "ScanOverTime(GRU cell): sequential per-timestep module call with\n            dict-state passing; merge_dict_trees stacks the per-step\n            'state_predicted' tensors along axis=1 -> [B, T, D]."

        def cell(h, x):
            gi = x @ W_ih + b_ih
            gh = h @ W_hh + b_hh
            i_r, i_z, i_n = jnp.split(gi, 3, axis=-1)
            h_r, h_z, h_n = jnp.split(gh, 3, axis=-1)
            r = jax.nn.sigmoid(i_r + h_r)
            z = jax.nn.sigmoid(i_z + h_z)
            n = jnp.tanh(i_n + r * h_n)
            h_new = (1.0 - z) * n + z * h
            return (h_new, h_new)
        xs = jnp.swapaxes(inputs, 0, 1)
        _, hs = jax.lax.scan(cell, initial_state, xs)
        return jnp.swapaxes(hs, 0, 1)

    def _L1_cond_ref(x, timestep_embed, ada_w, ada_b, qkv_w, qkv_b, out_w, out_b, ffn_w1, ffn_b1, ffn_w2, ffn_b2):
        import jax, jax.numpy as jnp
        import numpy as np
        DIM = 512
        H = 16
        DH = 128
        INNER = H * DH
        MLP = 4 * DIM
        B, T = (2, 512)
        EPS = 1e-06

        def _ln(x):
            mu = jnp.mean(x, axis=-1, keepdims=True)
            var = jnp.var(x, axis=-1, keepdims=True)
            return (x - mu) * jax.lax.rsqrt(var + EPS)
        Bc, Tc, D = x.shape
        ada = (timestep_embed @ ada_w + ada_b)[:, None, :]
        shift1, scale1, gate1, shift2, scale2, gate2 = jnp.split(ada, 6, axis=-1)
        x1 = _ln(x) * (1.0 + scale1) + shift1
        qkv = (x1 @ qkv_w + qkv_b).reshape(Bc, Tc, 3, H, DH)
        q, k, v = (qkv[:, :, 0], qkv[:, :, 1], qkv[:, :, 2])
        scale = DH ** (-0.5)
        attn = jnp.einsum('bthd,bshd->bhts', q, k) * scale
        attn = jax.nn.softmax(attn, axis=-1)
        attn_out = jnp.einsum('bhts,bshd->bthd', attn, v).reshape(Bc, Tc, INNER)
        attn_out = attn_out @ out_w + out_b
        x = x + gate1 * attn_out
        x2 = _ln(x) * (1.0 + scale2) + shift2
        h = jax.nn.gelu(x2 @ ffn_w1 + ffn_b1, approximate=False)
        x = x + gate2 * (h @ ffn_w2 + ffn_b2)
        return x
    x = x + _L0_cond_ref(cond_2048, x, L0_cond_W_ih, L0_cond_W_hh, L0_cond_b_ih, L0_cond_b_hh)
    x = x + _L1_cond_ref(x, cond_2048, L1_cond_ada_w, L1_cond_ada_b, L1_cond_qkv_w, L1_cond_qkv_b, L1_cond_out_w, L1_cond_out_b, L1_cond_ffn_w1, L1_cond_ffn_b1, L1_cond_ffn_w2, L1_cond_ffn_b2)
    return x

_drawn_inputs = setup_inputs


def setup_inputs(seed=0):
    import zlib

    import numpy as np

    out = dict(_drawn_inputs(seed))
    spreads = {'L0_cond_b_ih': (0.0, 0.1),
     'L0_cond_b_hh': (0.0, 0.1),
     'L1_cond_ada_b': (0.0, 0.379),
     'L1_cond_qkv_b': (0.0, 0.414),
     'L1_cond_out_b': (0.0, 0.389),
     'L1_cond_ffn_b1': (0.0, 0.67),
     'L1_cond_ffn_b2': (0.0, 0.364)}
    factors = {}
    for name, (base, spread) in spreads.items():
        noise = np.random.default_rng([zlib.crc32(name.encode()), seed]).standard_normal(out[name].shape)
        drawn = base * np.exp(spread * noise) if base else spread * noise
        out[name] = jnp.asarray(drawn.astype(out[name].dtype))
    for name, factor in factors.items():
        out[name] = (out[name] * factor).astype(out[name].dtype)
    return out
```

```python
from contextlib import ExitStack

import numpy as np

import concourse.bass as bass
from concourse import mybir

ALU = mybir.AluOpType
ACT = mybir.ActivationFunctionType
AX = mybir.AxisListType
F32 = mybir.dt.float32
F32R = mybir.dt.float32r


def gru_then_transformer(nc, x, cond, w_ih, w_hh, b_ih, b_hh, ada_w, ada_b, qkv_w, qkv_b,
                         out_w, out_b, ffn_w1, ffn_b1, ffn_w2, ffn_b2, out):
    B, T, D = x.shape
    P = 128
    KC = D // P
    G3 = 3 * D
    PAIRS = T // 2

    H, DH = 16, 128
    HQ = 4
    QUADS = H // HQ
    GT = 1024
    GROUPS = B * T // GT
    TILES = GT // P
    SCALE = float(DH) ** -0.5
    EPS = 1e-6

    kept = ExitStack()
    with kept:
        adaT = kept.enter_context(nc.sbuf_tensor("adaT", [P, 4, KC, B], F32))
        ident = kept.enter_context(nc.sbuf_tensor("ident", [P, P], F32))
        res_dram = nc.dram_tensor("res_dram", [B, T, D], F32, kind="Internal").ap()
        gate_dram = nc.dram_tensor("gate_dram", [2, B, D], F32, kind="Internal").ap()
        recurrence(nc, x, cond, w_ih, w_hh, b_ih, b_hh, ada_w, ada_b, res_dram, gate_dram, adaT, ident)
        transformer(nc, qkv_w, qkv_b, out_w, out_b, ffn_w1, ffn_b1, ffn_w2, ffn_b2, res_dram, gate_dram, adaT,
                    ident, out)


def recurrence(nc, x, cond, w_ih, w_hh, b_ih, b_hh, ada_w, ada_b, res_dram, gate_dram, adaT, ident):
    B, T, D = x.shape
    P = 128
    KC = D // P
    G3 = 3 * D
    PAIRS = T // 2
    ADA_SLOT = {0: 0, 1: 1, 3: 2, 4: 3}

    ctx = ExitStack()
    with ctx:
        def sb(name, shape, dt=F32):
            return ctx.enter_context(nc.sbuf_tensor(name, shape, dt))

        def ps(name, cols=512):
            return ctx.enter_context(nc.psum_tensor(name, [P, cols], F32))

        def sem(name):
            return ctx.enter_context(nc.semaphore(name))

        wih_hi = sb("wih_hi", [P, KC, G3], F32R)
        wih_lo = sb("wih_lo", [P, KC, G3], F32R)
        whh_hi = sb("whh_hi", [P, KC, G3], F32R)
        whh_lo = sb("whh_lo", [P, KC, G3], F32R)
        w_raw = [sb(f"w_raw{i}", [P, G3]) for i in range(2)]
        bias_gi = sb("bias_gi", [P, G3])
        bias_hn = sb("bias_hn", [B, D])
        bias_tmp = sb("bias_tmp", [P, 2 * D])
        x_pair = sb("x_pair", [P, D])
        xT_hi = sb("xT_hi", [P, KC, P], F32R)
        xT_lo = sb("xT_lo", [P, KC, P], F32R)
        gi = [sb(f"gi{d}", [B, G3]) for d in range(2)]
        x_res = [sb(f"x_res{d}", [B, D]) for d in range(2)]
        xh = [sb(f"xh{d}", [B, D]) for d in range(2)]
        h = [sb(f"h{d}", [P, D]) for d in range(2)]
        hT_hi = sb("hT_hi", [P, KC, B], F32R)
        hT_lo = sb("hT_lo", [P, KC, B], F32R)
        ar, az, hn, m_t, an = (sb(n, [B, D]) for n in ("ar", "az", "hn", "m_t", "an"))
        r_t, z_t, n_t, dd, e_t = (sb(n, [B, D]) for n in ("r_t", "z_t", "n_t", "dd", "e_t"))

        ada_raw = [sb(f"ada_raw{i}", [P, KC, D]) for i in range(2)]
        adab_col = sb("adab_col", [P, 6, KC])
        adab_gate = [sb(f"adab_gate{i}", [B, D]) for i in range(2)]
        gate_sb = [sb(f"gate_sb{i}", [B, D]) for i in range(2)]
        condT = sb("condT", [P, KC, B])

        ps_gate = [ps(f"ps_gate_{g}") for g in "rnz"]
        ps_gi = [ps(f"ps_gi_{g}") for g in "rnz"]
        ps_hT = ps("ps_hT")
        ps_xT = ps("ps_xT")
        COL = {0: 0, 1: 2 * D, 2: D}

        s_id0, s_ident = sem("s_id0"), sem("s_ident")
        s_wraw = [sem(f"s_wraw{i}") for i in range(2)]
        s_whi, s_wlo = sem("s_whi"), sem("s_wlo")
        s_bias_in, s_bias = sem("s_bias_in"), sem("s_bias")
        s_h0, s_hpad = sem("s_h0"), sem("s_hpad")
        s_xpair, s_xres = sem("s_xpair"), [sem(f"s_xres{d}") for d in range(2)]
        s_xtr, s_xT_hi, s_xT_lo = sem("s_xtr"), sem("s_xT_hi"), sem("s_xT_lo")
        s_gi_mm, s_gi = sem("s_gi_mm"), sem("s_gi")
        s_gate = sem("s_gate")
        s_htr, s_hT_hi, s_hT_lo = sem("s_htr"), sem("s_hT_hi"), sem("s_hT_lo")
        s_ar, s_az, s_hn, s_m, s_an, s_dd, s_e, s_h = (sem(f"s_{n}") for n in ("ar", "az", "hn", "m", "an", "dd", "e", "h"))
        s_r, s_z, s_n = sem("s_r"), sem("s_z"), sem("s_n")
        s_xh = sem("s_xh")
        s_store = [sem(f"s_store{d}") for d in range(2)]

        s_ada_raw = [sem(f"s_ada_raw{i}") for i in range(2)]
        s_ada_mm, s_ada, s_adab, s_condT, s_gate_st = (sem(n) for n in ("s_ada_mm", "s_ada", "s_adab", "s_condT", "s_gate_st"))

        def wait(eng, s, value):
            if not isinstance(value, int) or value > 0:
                eng.wait_ge(s, value)

        def pairs(eng, body):
            body(0)
            with eng.Fori(1, PAIRS - 1) as p:
                body(p)
            body(PAIRS - 1, last=True)

        block = ctx.enter_context(nc.Block())

        @block.sync
        def _(sp):
            for c in range(2 * KC):
                if c >= 2:
                    sp.wait_ge(s_wlo, c - 1)
                    sp.wait_ge(s_whi, c - 1)
                src = (w_ih if c < KC else w_hh)[(c % KC) * P:(c % KC + 1) * P, :]
                sp.dma_start(w_raw[c % 2][:], src).then_inc(s_wraw[c % 2], 16)

            for i in range(6):
                if i >= 2:
                    sp.wait_ge(s_ada_mm, i - 1)
                sp.dma_start(ada_raw[i % 2][:], ada_w[:, i * D:(i + 1) * D].rearrange("(k p) n -> p k n", p=P))\
                    .then_inc(s_ada_raw[i % 2], 16)
            for i in range(2):
                sp.wait_ge(s_ada, 3 * (i + 1))
                sp.dma_start(gate_dram[i], gate_sb[i][:]).then_inc(s_gate_st, 16)

            def body(p, last=False):
                for d in range(2):
                    sp.wait_ge(s_xh, 2 + 2 * p + d + 1)
                    sp.dma_start(res_dram[:, 2 * p + d, :] if isinstance(p, int) else
                                 res_dram[:, bass.ds(2 * p + d, 1), :].rearrange("b o n -> b (o n)"), xh[d][:]).then_inc(s_store[d], 16)
            pairs(sp, body)
            for d in range(2):
                sp.wait_ge(s_store[d], 16 * PAIRS)
            sp.wait_ge(s_gate_st, 32)

        @block.gpsimd
        def _(pool):
            nc.gpsimd.memset(ident[:], 0.0).then_inc(s_id0, 1)
            pool.wait_ge(s_id0, 1)
            nc.gpsimd.affine_select(out=ident[:], in_=ident[:], compare_op=ALU.not_equal, fill=1.0,
                                    base=0, pattern=[[-1, P]], channel_multiplier=1).then_inc(s_ident, 1)
            for d in range(2):
                pool.wait_ge(s_ident, 1)
                nc.gpsimd.memset(xh[d][:], 0.0).then_inc(s_xh, 1)
                pool.wait_ge(s_xh, d + 1)

            def body(p, last=False):
                for d in range(2):
                    s = 2 * p + d
                    pool.wait_ge(s_h, s + 1)
                    pool.wait_ge(s_xres[d], 16 * (p + 1))
                    wait(pool, s_store[d], 16 * p)
                    nc.gpsimd.tensor_tensor(xh[d][:], x_res[d][:], h[d][0:B, :], ALU.add).then_inc(s_xh, 1)
            pairs(pool, body)

        @block.scalar
        def _(act):
            def load_pair(p):
                for d in range(2):
                    src = x[:, 2 * p + d, :] if isinstance(p, int) else \
                        x[:, bass.ds(2 * p + d, 1), :].rearrange("b o n -> b (o n)")
                    act.dma_start(x_pair[d * B:(d + 1) * B, :], src).then_inc(s_xpair, 16)

            def load_res(p, d):
                src = x[:, 2 * p + d, :] if isinstance(p, int) else \
                    x[:, bass.ds(2 * p + d, 1), :].rearrange("b o n -> b (o n)")
                act.dma_start(x_res[d][:], src).then_inc(s_xres[d], 16)

            load_pair(0)
            act.dma_start(h[1][0:B, :], cond[:, :]).then_inc(s_h0, 16)
            for a, t in ((b_ih[:], bias_gi[:]), (b_hh[0:2 * D], bias_tmp[:])):
                act.dma_start(t, a.partition_broadcast(P)).then_inc(s_bias_in, 16)
            act.dma_start(bias_hn[:], b_hh[2 * D:].partition_broadcast(B)).then_inc(s_bias_in, 16)
            for d in range(2):
                load_res(0, d)
            for i in range(6):
                act.dma_start(adab_col[:, i, :], ada_b[i * D:(i + 1) * D].rearrange("(k p) -> p k", p=P), allow_slow_non_contiguous=True).then_inc(s_adab, 16)
            for i in range(2):
                act.dma_start(adab_gate[i][:], ada_b[(2 + 3 * i) * D:(3 + 3 * i) * D].partition_broadcast(B)).then_inc(s_adab, 16)
            act.wait_ge(s_htr, 1)
            nc.scalar.copy(hT_hi[:], ps_hT[:].rearrange("p (k b) -> p k b", k=KC)[:, :, 0:B]).then_inc(s_hT_hi, 1)
            act.wait_ge(s_hT_lo, 1)
            nc.scalar.copy(condT[:], ps_hT[:].rearrange("p (k b) -> p k b", k=KC)[:, :, 0:B]).then_inc(s_condT, 1)
            act.wait_ge(s_xtr, 1)
            nc.scalar.copy(xT_hi[:], ps_xT[:].rearrange("p (k b) -> p k b", k=KC)).then_inc(s_xT_hi, 1)
            load_pair(1)
            for c in range(2 * KC):
                act.wait_ge(s_wraw[c % 2], 16 * (c // 2 + 1))
                w = wih_hi if c < KC else whh_hi
                nc.scalar.copy(w[:, c % KC, :], w_raw[c % 2][:]).then_inc(s_whi, 1)

            def body(p, last=False):
                for d in range(2):
                    s = 2 * p + d
                    act.wait_ge(s_ar, s + 1)
                    nc.scalar.activation(r_t[:], ar[:], ACT.Sigmoid).then_inc(s_r, 1)
                    if d == 0 and not last:
                        act.wait_ge(s_xtr, p + 2)
                        act.wait_ge(s_gi_mm, 3 * (p + 1))
                        nc.scalar.copy(xT_hi[:], ps_xT[:].rearrange("p (k b) -> p k b", k=KC)).then_inc(s_xT_hi, 1)
                        if not isinstance(p, int) or p + 2 < PAIRS:
                            pass
                    act.wait_ge(s_an, s + 1)
                    nc.scalar.activation(n_t[:], an[:], ACT.Tanh).then_inc(s_n, 1)
                    act.wait_ge(s_az, s + 1)
                    nc.scalar.activation(z_t[:], az[:], ACT.Sigmoid).then_inc(s_z, 1)
                    if not (last and d == 1):
                        act.wait_ge(s_htr, s + 2)
                        nc.scalar.copy(hT_hi[:], ps_hT[:].rearrange("p (k b) -> p k b", k=KC)[:, :, 0:B]).then_inc(s_hT_hi, 1)
                    if not last:
                        act.wait_ge(s_xh, 2 + s + 1)
                        load_res(p + 1, d)
                        if d == 0 and (not isinstance(p, int) or p + 2 < PAIRS):
                            load_pair_next(p)

            def load_pair_next(p):
                if isinstance(p, int):
                    load_pair(p + 2)
                else:
                    load_pair(p + 2)
            body(0)
            with act.Fori(1, PAIRS - 2) as p:
                body(p)
            body(PAIRS - 2)
            body(PAIRS - 1, last=True)

        @block.vector
        def _(dve):
            for d in range(2):
                nc.vector.memset(h[d][B:, :], 0.0).then_inc(s_hpad, 1)
            dve.wait_ge(s_htr, 1)
            dve.wait_ge(s_hT_hi, 1)
            nc.vector.tensor_tensor(hT_lo[:], ps_hT[:].rearrange("p (k b) -> p k b", k=KC)[:, :, 0:B],
                                    hT_hi[:].bitcast(F32), ALU.subtract).then_inc(s_hT_lo, 1)
            dve.wait_ge(s_xT_hi, 1)
            nc.vector.tensor_tensor(xT_lo[:], ps_xT[:].rearrange("p (k b) -> p k b", k=KC),
                                    xT_hi[:].bitcast(F32), ALU.subtract).then_inc(s_xT_lo, 1)
            dve.wait_ge(s_bias_in, 48)
            nc.vector.tensor_tensor(bias_gi[:, 0:2 * D], bias_gi[:, 0:2 * D], bias_tmp[:], ALU.add).then_inc(s_bias, 1)
            for c in range(2 * KC):
                dve.wait_ge(s_wraw[c % 2], 16 * (c // 2 + 1))
                dve.wait_ge(s_whi, c + 1)
                hi, lo = (wih_hi, wih_lo) if c < KC else (whh_hi, whh_lo)
                nc.vector.tensor_tensor(lo[:, c % KC, :], w_raw[c % 2][:], hi[:, c % KC, :].bitcast(F32),
                                        ALU.subtract).then_inc(s_wlo, 1)
            dve.wait_ge(s_bias, 1)

            def take_gi(g):
                for d in range(2):
                    last = nc.vector.tensor_tensor(gi[d][:, g * D:(g + 1) * D], ps_gi[g][d * B:(d + 1) * B, :],
                                                   bias_gi[d * B:(d + 1) * B, COL[g]:COL[g] + D], ALU.add)
                last.then_inc(s_gi, 1)

            for g in range(3):
                dve.wait_ge(s_gi_mm, g + 1)
                take_gi(g)
            dve.wait_ge(s_adab, 8 * 16)
            for i in range(6):
                dve.wait_ge(s_ada_mm, i + 1)
                src = ps_gate[i % 2]
                if i in ADA_SLOT:
                    nc.vector.scalar_tensor_tensor(
                        out=adaT[:, ADA_SLOT[i]], in0=src[:, 0:KC * B].rearrange("p (k b) -> p k b", k=KC),
                        scalar=float(i in (1, 4)), in1=adab_col[:, i, :].unsqueeze(2).broadcast_to([P, KC, B]),
                        op0=ALU.add, op1=ALU.add).then_inc(s_ada, 1)
                else:
                    nc.vector.tensor_tensor(gate_sb[i // 3][:], src[0:B, :], adab_gate[i // 3][:], ALU.add)\
                        .then_inc(s_ada, 1)

            def body(p, last=False):
                for d in range(2):
                    s = 2 * p + d
                    old, new = h[1 - d][0:B, :], h[d][0:B, :]
                    dve.wait_ge(s_gate, 3 * s + 1)
                    dve.wait_ge(s_gi, 3 * p + 3)
                    nc.vector.tensor_tensor(ar[:], ps_gate[0][0:B, :], gi[d][:, 0:D], ALU.add).then_inc(s_ar, 1)
                    if d == 0 and not last:
                        dve.wait_ge(s_xT_hi, p + 2)
                        nc.vector.tensor_tensor(xT_lo[:], ps_xT[:].rearrange("p (k b) -> p k b", k=KC),
                                                xT_hi[:].bitcast(F32), ALU.subtract).then_inc(s_xT_lo, 1)
                    if d == 1 and not last:
                        dve.wait_ge(s_gi_mm, 3 * (p + 1) + 1)
                        dve.wait_ge(s_ar, s + 1)
                        take_gi(0)
                    dve.wait_ge(s_gate, 3 * s + 2)
                    nc.vector.tensor_tensor(hn[:], ps_gate[1][0:B, :], bias_hn[:], ALU.add).then_inc(s_hn, 1)
                    dve.wait_ge(s_r, s + 1)
                    dve.wait_ge(s_hn, s + 1)
                    nc.vector.tensor_tensor(m_t[:], hn[:], r_t[:], ALU.mult).then_inc(s_m, 1)
                    dve.wait_ge(s_m, s + 1)
                    nc.vector.tensor_tensor(an[:], m_t[:], gi[d][:, D:2 * D], ALU.add).then_inc(s_an, 1)
                    dve.wait_ge(s_gate, 3 * s + 3)
                    nc.vector.tensor_tensor(az[:], ps_gate[2][0:B, :], gi[d][:, 2 * D:3 * D], ALU.add).then_inc(s_az, 1)
                    dve.wait_ge(s_n, s + 1)
                    if isinstance(s, int) and s == 0:
                        dve.wait_ge(s_h0, 16)
                    nc.vector.tensor_tensor(dd[:], old[:], n_t[:], ALU.subtract).then_inc(s_dd, 1)
                    dve.wait_ge(s_z, s + 1)
                    dve.wait_ge(s_dd, s + 1)
                    nc.vector.tensor_tensor(e_t[:], dd[:], z_t[:], ALU.mult).then_inc(s_e, 1)
                    dve.wait_ge(s_e, s + 1)
                    dve.wait_ge(s_xh, s + 1)
                    nc.vector.tensor_tensor(new[:], e_t[:], n_t[:], ALU.add).then_inc(s_h, 1)
                    if not (last and d == 1):
                        dve.wait_ge(s_hT_hi, s + 2)
                        nc.vector.tensor_tensor(hT_lo[:], ps_hT[:].rearrange("p (k b) -> p k b", k=KC)[:, :, 0:B],
                                                hT_hi[:].bitcast(F32), ALU.subtract).then_inc(s_hT_lo, 1)
                if not last:
                    for g in (1, 2):
                        dve.wait_ge(s_gi_mm, 3 * (p + 1) + 1 + g)
                        take_gi(g)
            pairs(dve, body)

        @block.tensor
        def _(pe):
            def turn_h(d, s):
                for k in range(KC):
                    last = nc.tensor.transpose(ps_hT[:, k * P:(k + 1) * P], h[d][:, k * P:(k + 1) * P], ident[:])
                last.then_inc(s_htr, 1)

            def turn_x():
                for k in range(KC):
                    last = nc.tensor.transpose(ps_xT[:, k * P:(k + 1) * P], x_pair[:, k * P:(k + 1) * P], ident[:])
                last.then_inc(s_xtr, 1)

            def project_x(g, ks):
                for k in ks:
                    for n, (a, w) in enumerate(((xT_hi, wih_hi), (xT_hi, wih_lo), (xT_lo, wih_hi))):
                        last = nc.tensor.matmul(ps_gi[g][:], a[:, k, :], w[:, k, COL[g]:COL[g] + D],
                                                start=(k == 0 and n == 0), stop=(k == KC - 1 and n == 2))
                if ks[-1] == KC - 1:
                    last.then_inc(s_gi_mm, 1)

            def project_h(g):
                for k in range(KC):
                    for n, (a, w) in enumerate(((hT_hi, whh_hi), (hT_hi, whh_lo), (hT_lo, whh_hi))):
                        last = nc.tensor.matmul(ps_gate[g][0:B, :], a[:, k, :], w[:, k, COL[g]:COL[g] + D],
                                                start=(k == 0 and n == 0), stop=(k == KC - 1 and n == 2))
                last.then_inc(s_gate, 1)

            pe.wait_ge(s_ident, 1)
            pe.wait_ge(s_hpad, 2)
            pe.wait_ge(s_h0, 16)
            turn_h(1, -1)
            pe.wait_ge(s_xpair, 32)
            turn_x()
            pe.wait_ge(s_xT_hi, 1)
            pe.wait_ge(s_xT_lo, 1)
            pe.wait_ge(s_whi, KC)
            pe.wait_ge(s_wlo, KC)
            for g in range(3):
                project_x(g, range(KC))
            pe.wait_ge(s_condT, 1)
            for i in range(6):
                pe.wait_ge(s_ada_raw[i % 2], 16 * (i // 2 + 1))
                if i >= 2:
                    pe.wait_ge(s_ada, i - 1)
                if i in ADA_SLOT:
                    for c in range(KC):
                        for k in range(KC):
                            last = nc.tensor.matmul(ps_gate[i % 2][:, c * B:(c + 1) * B], ada_raw[i % 2][:, k, c * P:(c + 1) * P],
                                                    condT[:, k, :], start=(k == 0), stop=(k == KC - 1))
                else:
                    for k in range(KC):
                        last = nc.tensor.matmul(ps_gate[i % 2][0:B, :], condT[:, k, :], ada_raw[i % 2][:, k, :],
                                                start=(k == 0), stop=(k == KC - 1))
                last.then_inc(s_ada_mm, 1)
            pe.wait_ge(s_ada, 6)
            pe.wait_ge(s_whi, 2 * KC)
            pe.wait_ge(s_wlo, 2 * KC)

            def body(p, last=False):
                if not last:
                    pe.wait_ge(s_xpair, 32 * (p + 2))
                    pe.wait_ge(s_xT_lo, p + 1)
                    turn_x()
                for d in range(2):
                    s = 2 * p + d
                    pe.wait_ge(s_hT_hi, s + 1)
                    pe.wait_ge(s_hT_lo, s + 1)
                    for g in range(3):
                        project_h(g)
                    if not last:
                        if d == 0:
                            pe.wait_ge(s_xT_hi, p + 2)
                            pe.wait_ge(s_xT_lo, p + 2)
                            pe.wait_ge(s_gi, 3 * p + 3)
                            project_x(0, range(KC))
                            project_x(1, range(KC // 2))
                        else:
                            project_x(1, range(KC // 2, KC))
                            project_x(2, range(KC))
                    if not (last and d == 1):
                        pe.wait_ge(s_h, s + 1)
                        turn_h(d, s)
            pairs(pe, body)


def transformer(nc, qkv_w, qkv_b, out_w, out_b, ffn_w1, ffn_b1, ffn_w2, ffn_b2, res_dram, gate_dram, adaT,
                ident, out):
    B, T, D = res_dram.shape
    P = 128
    KC = D // P
    H, DH = 16, 128
    HQ = 4
    QUADS = H // HQ
    GT = 1024
    HALF = GT // 2
    GROUPS = B * T // GT
    TILES = GT // P
    HT = TILES // 2
    INNER = H * DH
    SCALE = float(DH) ** -0.5
    EPS = 1e-6
    LAG = 3
    RAW = 4

    PROJ_A, PROJ_F = 4 * HQ, 2 * HQ
    PROJ_G = QUADS * (PROJ_A + PROJ_F)
    CH_A, CH_A_LAST, CH_F, CH_F_LAST = 8, 6, 4, 6
    CH_G = 3 * CH_A + CH_A_LAST + 3 * CH_F + CH_F_LAST

    nc.disable_value_cache = True
    rows = res_dram.rearrange("b t d -> (b t) d")
    out_rows = out.rearrange("b t d -> (b t) d")

    ctx = ExitStack()
    with ctx:
        def sb(name, shape, dt=F32):
            return ctx.enter_context(nc.sbuf_tensor(name, shape, dt))

        def ps(name):
            return ctx.enter_context(nc.psum_tensor(name, [P, 512], F32))

        def sem(name):
            return ctx.enter_context(nc.semaphore(name))

        xT_hi = sb("xnT_hi", [P, KC, GT], F32R)
        xT_lo = sb("xnT_lo", [P, KC, GT], F32R)
        y = sb("y", [P, TILES, D])
        wq, wk, wv, wo = ([sb(f"{n}_{h}", [P, KC, HQ * P], F32R) for h in ("hi", "lo")] for n in ("wq", "wk", "wv", "wo"))
        raw = [sb(f"raw{i}", [P, 2, 512]) for i in range(RAW)]
        qT = sb("qT", [P, HQ, HALF])
        kT = sb("kT", [P, HQ, HALF])
        at_hi = sb("at_hi", [P, 4, HQ * P], F32R)
        at_lo = sb("at_lo", [P, 4, HQ * P], F32R)
        v_sb = [sb(f"v{i}", [P, 512]) for i in range(2)]
        sc = sb("sc", [P, HQ, T])
        ex = sb("ex", [P, HQ, T])
        mx = sb("mx", [P, HQ])
        sm = sb("sm", [P, HQ])
        rc = sb("rc", [P, HQ])
        pr = sb("pr", [P, HQ, P])
        pT = sb("pT", [P, HQ * P])
        xr = [sb(f"xr{i}", [P, D]) for i in range(2)]
        gt = [sb(f"gt{i}", [P, D]) for i in range(2)]
        xn = [sb(f"xn{i}", [P, D]) for i in range(2)]
        x2 = [sb(f"x2{i}", [P, D]) for i in range(2)]
        st = [sb(f"st{i}", [P, D]) for i in range(2)]
        tmp = sb("tmp", [P, D])
        stat = sb("stat", [P, 6])
        mv = sb("mv", [P, 2])
        eps, mhalf, veps = (sb(n, [P, 1]) for n in ("eps", "mhalf", "veps"))
        rstd = sb("rstd", [P, 1])
        qkvb = sb("qkvb", [P, 3 * H])
        f1b = sb("f1b", [P, H])
        bv = sb("bv", [P, HQ * P])
        ob = sb("ob", [P, D])
        b2 = sb("b2", [P, D])

        ps_p = [ps("ps_p0"), ps("ps_p1")]
        ps_v, ps_s, ps_pt, ps_pv, ps_o, ps_ln = (ps(f"ps_{n}") for n in ("v", "s", "pt", "pv", "o", "ln"))

        s_raw = [sem(f"s_raw{i}") for i in range(RAW)]
        s_whi, s_wlo = sem("s_w2hi"), sem("s_w2lo")
        s_proj, s_projd = sem("s_proj"), sem("s_projd")
        s_v, s_vd, s_bv = sem("s_v"), sem("s_vd"), sem("s_bv")
        s_s, s_mx, s_sub, s_exp, s_sum, s_rec, s_p = (sem(f"s_{n}") for n in ("s", "mx", "sub", "exp", "sum", "rec", "p"))
        s_t, s_pt, s_pv, s_ahi, s_alo, s_o, s_od = (sem(f"s_{n}") for n in ("t", "pt", "pv", "ahi", "alo", "o", "od"))
        s_hs = sem("s_hs")
        s_hhi = sem("s_hhi")
        s_xr, s_gt = [sem(f"s_xr{i}") for i in range(2)], [sem(f"s_gt{i}") for i in range(2)]
        s_sr = [sem(f"s_sr{i}") for i in range(2)]
        s_yg, s_x2, s_ssum, s_bn, s_mv, s_veps, s_rstd, s_xn = (sem(f"s_{n}") for n in ("yg", "x2", "ssum", "bn", "mv", "veps", "rstd", "xn"))
        s_lnT, s_aff1, s_aff, s_xhi, s_xlo = (sem(f"s_{n}") for n in ("lnT", "aff1", "aff", "xhi", "xlo"))
        s_fg, s_fin = sem("s_fg"), sem("s_fin")
        s_st = [sem(f"s_st{i}") for i in range(2)]
        s_const, s_pz, s_credit = sem("s_const"), sem("s_pz"), sem("s_credit")

        def wait(eng, s, value):
            if not isinstance(value, int) or value > 0:
                eng.wait_ge(s, value)

        def proj_a(g, q): return PROJ_G * g + PROJ_A * q
        def proj_f(g, q): return PROJ_G * g + PROJ_A * QUADS + PROJ_F * q
        def outs_a(g, q): return 2 * QUADS * TILES * g + TILES * q
        def outs_f(g, q): return 2 * QUADS * TILES * g + TILES * (QUADS + q)
        def chunks_a(g, q): return 4 + CH_G * g + CH_A * q
        def chunks_f(g, q): return 4 + CH_G * g + 3 * CH_A + CH_A_LAST + CH_F * q
        def tiles_a(g, q): return TILES * (QUADS * g + q)
        def ln1(g, j): return 2 * TILES * g + j
        def ln2(g, j): return 2 * TILES * g + TILES + j
        def hid(g, q): return PROJ_F * (QUADS * g + q)

        def steps_a(first, last):
            ln = {-1: [("norm1", 4), ("norm1", 5)], 0: [("turn1", 4), ("norm1", 6)], 2: [("turn1", 5), ("norm1", 7)],
                  4: [("turn1", 6)], 6: [("turn1", 7)]} if first else {}
            yield from ln.get(-1, [])
            for n in range(PROJ_A):
                if n == PROJ_A // 2:
                    for j in range(HT):
                        yield from slot(j, last)
                yield "proj", n
                yield from ln.get(n, [])
                if n < 8 and n % 2:
                    yield "split", n // 2
            for j in range(HT, TILES):
                yield from slot(j, last)
                if not last:
                    yield "split", j
                elif j < HT + 2:
                    yield "split", j
            yield "turn", TILES - 1
            yield "out", TILES - 3
            yield "pv", TILES - 1
            yield "out", TILES - 2
            if last:
                yield "norm2", TILES - 3
            yield "out", TILES - 1

        def slot(j, last):
            yield "score", j
            if j >= 1:
                yield "turn", j - 1
            yield "soften", j
            yield "value", j
            if last and j > LAG:
                yield "turn2", j - LAG - 1
            if j >= LAG:
                yield "out", j - LAG
            if j >= 1:
                yield "pv", j - 1
            if last and j >= LAG:
                yield "norm2", j - LAG

        def steps_f(first, last, more):
            if first:
                yield from [("fproj", 0), ("split", 0), ("turn2", 4), ("norm2", 6), ("fproj", 1), ("split", 1),
                            ("fproj", 2), ("turn2", 5), ("norm2", 7), ("fproj", 3), ("fout", 0), ("turn2", 6),
                            ("fout", 1), ("fout", 2), ("turn2", 7), ("fout", 3)]
                for n in range(HQ, PROJ_F):
                    yield "fproj", n
                for j in range(HT, TILES):
                    yield "fout", j
                    if j in (4, 5):
                        yield "split", j - 2
                return
            if last:
                ln = {-1: [("norm1", 0), ("norm1", 1)], 0: [("turn1", 0), ("norm1", 2)], 2: [("turn1", 1), ("norm1", 3)],
                      4: [("turn1", 2)], 6: [("turn1", 3)]} if more else {}
            for n in range(PROJ_F):
                yield "fproj", n
                if n in (0, 2):
                    yield "split", n // 2
                if last and n == 6:
                    yield from ln.get(-1, [])
            for j in range(TILES):
                yield "fout", j
                if not last:
                    if j in (0, 2):
                        yield "split", 2 + j // 2
                    continue
                yield from ln.get(j, [])
                yield "fin", j
                if more and j in (0, 1, 4, 5):
                    yield "split", {0: 2, 1: 3, 4: 4, 5: 5}[j]

        def group(eng, g, body, more):
            body("a", g, 0, steps_a(True, False), dict(first=True))
            with eng.Fori(1, QUADS - 1) as q:
                body("a", g, q, steps_a(False, False), {})
            body("a", g, QUADS - 1, steps_a(False, True), dict(last=True))
            body("f", g, 0, steps_f(True, False, more), dict(first=True))
            with eng.Fori(1, QUADS - 1) as q:
                body("f", g, q, steps_f(False, False, more), {})
            body("f", g, QUADS - 1, steps_f(False, True, more), dict(last=True))

        def groups(eng, body):
            for i, j in ((0, "norm1"), (0, "turn1"), (1, "norm1"), (1, "turn1"), (2, "norm1"), (2, "turn1"),
                         (3, "norm1"), (3, "turn1")):
                body("a", -1, QUADS - 1, [(j, i)], {})
            with eng.Fori(0, GROUPS - 1) as g:
                group(eng, g, body, True)
            group(eng, GROUPS - 1, body, False)

        def w_cols(w, at):
            return w[:, bass.ds(at, HQ * P)].rearrange("(k p) n -> p k n", p=P)

        def w_rows(w, at):
            return w[bass.ds(at, HQ * P), :].rearrange("(k p) n -> p k n", p=P)

        def chunk(kind, g, q, c, last=False):
            W = HQ * P
            if kind == "a":
                if c < 2:
                    return w_cols(qkv_w, 2 * INNER + q * W), wv, c
                if c < 4:
                    return w_rows(out_w, q * W), wo, c - 2
                if last:
                    return w_cols(ffn_w1, 0), wq, c - 4
                if c < 6:
                    return w_cols(qkv_w, (q + 1) * W), wq, c - 4
                return w_cols(qkv_w, INNER + (q + 1) * W), wk, c - 6
            if c < 2:
                return w_rows(ffn_w2, q * W), wo, c
            if not last:
                return w_cols(ffn_w1, (q + 1) * W), wq, c - 2
            if c < 4:
                return w_cols(qkv_w, 0), wq, c - 2
            return w_cols(qkv_w, INNER), wk, c - 4

        def n_chunks(kind, last, more):
            if kind == "a":
                return CH_A_LAST if last else CH_A
            return (CH_F_LAST if more else 2) if last else CH_F

        def slot_of(kind, q, c):
            if kind == "a":
                return c % RAW
            return (2 + c) % RAW

        def raw_count(kind, g, q, c):
            if kind == "a":
                return 16 * (1 + CH_G // RAW * g + CH_A // RAW * q + c // RAW + 1)
            return 16 * (1 + CH_G // RAW * g + (3 * CH_A + CH_A_LAST - 2) // RAW + CH_F // RAW * q + (c + 2) // RAW + 1)

        def region_free(kind, g, q, c, last):
            if kind == "a":
                return proj_a(g, q) + (1 if c < 4 else PROJ_A)
            return proj_f(g, q) + (1 if c < 2 else PROJ_F)

        def ln_of(kind, g, q, what, j):
            if what in ("turn2", "norm2"):
                return ln2(g, j)
            if kind == "f":
                return ln1(g + 1, j)
            if isinstance(g, int) and g < 0:
                return ln1(0, j)
            return ln1(g, j)

        def xr_count(g, which, j):
            return 16 * (TILES * g + which * TILES // 2 + j // 2 + 1)

        def ps_out(j):
            return ps_v if j == TILES - 2 else ps_o

        first_chunks = [(w_cols(qkv_w, 0), wq, 0), (w_cols(qkv_w, 0), wq, 1),
                        (w_cols(qkv_w, INNER), wk, 0), (w_cols(qkv_w, INNER), wk, 1)]

        block = ctx.enter_context(nc.Block())

        @block.sync
        def _(sp):
            for i in range(2):
                sp.sem_inc(s_st[i], 16)
            for c, (src, _, part) in enumerate(first_chunks):
                sp.dma_start(raw[c][:], src[:, 2 * part:2 * part + 2, :]).then_inc(s_raw[c], 16)

            def body(kind, g, q, steps, at):
                if isinstance(g, int) and g < 0:
                    return
                last = at.get("last", False)
                more = not (isinstance(g, int) and g == GROUPS - 1)
                for c in range(n_chunks(kind, last, more)):
                    if kind == "a" and c == 4:
                        sp.wait_ge(s_vd, tiles_a(g, q) + 1)
                        sp.dma_start(bv[:], qkv_b[bass.ds(2 * INNER + q * HQ * P, HQ * P)].partition_broadcast(P))\
                            .then_inc(s_bv, 16)
                    n = (chunks_a if kind == "a" else chunks_f)(g, q) + c
                    src, _, part = chunk(kind, g, q, c, last)
                    sp.wait_ge(s_wlo, n - RAW + 1)
                    sp.dma_start(raw[slot_of(kind, q, c)][:], src[:, 2 * part:2 * part + 2, :])\
                        .then_inc(s_raw[slot_of(kind, q, c)], 16)
            groups(sp, body)
            for i in range(2):
                sp.wait_ge(s_st[i], 16 + 16 * TILES * GROUPS)

        @block.gpsimd
        def _(pool):
            nc.gpsimd.memset(pr[:], 0.0).then_inc(s_pz, 1)
            pool.wait_ge(s_pz, 1)
            nc.gpsimd.memset(eps[:], EPS).then_inc(s_pz, 1)
            pool.wait_ge(s_pz, 2)
            nc.gpsimd.memset(mhalf[:], -0.5).then_inc(s_pz, 1)
            pool.wait_ge(s_pz, 3)
            pool.sem_inc(s_ssum, 2)
            pool.sem_inc(s_fin, 2)

            def body(kind, g, q, steps, at):
                for what, j in steps:
                    b = j % 2
                    if what == "norm2":
                        pool.wait_ge(s_od, outs_a(g, QUADS - 1) + j + 2)
                        pool.wait_ge(s_gt[b], 32 * (TILES * g + j // 2 + 1))
                        nc.gpsimd.tensor_tensor(y[:, j, :], y[:, j, :], gt[b][:], ALU.mult).then_inc(s_yg, 1)
                        pool.wait_ge(s_yg, TILES * g + j + 1)
                        pool.wait_ge(s_xr[b], xr_count(g, 1, j))
                        if j >= 2:
                            pool.wait_ge(s_xn, ln2(g, j) - 1)
                        nc.gpsimd.tensor_tensor(x2[b][:], y[:, j, :], xr[b][:], ALU.add).then_inc(s_x2, 1)
                    if what in ("norm1", "norm2"):
                        n = ln_of(kind, g, q, what, j)
                        pool.wait_ge(s_mv, n + 1)
                        nc.gpsimd.tensor_tensor(veps[:], mv[:, 1:2], eps[:], ALU.add).then_inc(s_veps, 1)
                        pool.wait_ge(s_veps, n + 1)
                        nc.gpsimd.tensor_tensor(rstd[:], veps[:], mhalf[:], ALU.pow).then_inc(s_rstd, 1)
                    if what == "norm2":
                        pool.wait_ge(s_x2, TILES * g + j + 1)
                        pool.wait_ge(s_st[b], 16 * (TILES * g + j // 2 + 1))
                        nc.gpsimd.tensor_tensor(st[b][:], x2[b][:], xr[b][:], ALU.add).then_inc(s_ssum, 1)
                    if what == "fin":
                        pool.wait_ge(s_od, outs_f(g, q) + j + 2)
                        pool.wait_ge(s_gt[b], 32 * (TILES * g + TILES // 2 + j // 2 + 1))
                        pool.wait_ge(s_st[b], 16 * (TILES * g + TILES // 2 + j // 2 + 1))
                        nc.gpsimd.tensor_tensor(st[b][:], y[:, j, :], gt[b][:], ALU.mult).then_inc(s_fg, 1)
                        pool.wait_ge(s_fg, TILES * g + j + 1)
                        pool.wait_ge(s_sr[b], 16 * ((TILES // 2) * g + j // 2 + 1))
                        nc.gpsimd.tensor_tensor(st[b][:], st[b][:], x2[b][:], ALU.add).then_inc(s_fin, 1)
            groups(pool, body)

        @block.scalar
        def _(act):
            act.dma_start(qkvb[:], qkv_b.rearrange("(c p) -> p c", p=P), allow_slow_non_contiguous=True).then_inc(s_const, 16)
            act.dma_start(f1b[:], ffn_b1.rearrange("(c p) -> p c", p=P), allow_slow_non_contiguous=True).then_inc(s_const, 16)
            act.dma_start(ob[:], out_b.partition_broadcast(P)).then_inc(s_const, 16)
            act.dma_start(b2[:], ffn_b2.partition_broadcast(P)).then_inc(s_const, 16)
            act.sem_inc(s_projd, 2)

            def load_rows(dst, src, g, j, s):
                act.dma_start(dst[:], src[bass.ds((g * TILES + j) * P, P), :]).then_inc(s, 16)

            def load_gate(b, which, g, j):
                for i in range(2):
                    act.dma_start(gt[b][i * T:(i + 1) * T, :],
                                  gate_dram[which, bass.ds(2 * (g * TILES + j) + i, 1), :].rearrange("o d -> (o d)").partition_broadcast(T)
                                  ).then_inc(s_gt[b], 16)

            def load_ln1(g, j):
                b = j % 2
                if isinstance(g, int) and g == 0:
                    wait(act, s_xn, j - 1)
                else:
                    if j < 2:
                        act.wait_ge(s_ssum, TILES * g + 2)
                        act.wait_ge(s_xn, ln1(g, 0))
                    else:
                        act.wait_ge(s_xn, ln1(g, j) - 1)
                load_rows(xr[b], rows, g, j, s_xr[b])

            def load_ln2(g, j):
                b = j % 2
                if j < 2:
                    act.wait_ge(s_xn, ln2(g, 0))
                    act.wait_ge(s_fin, TILES * g + 2)
                else:
                    act.wait_ge(s_x2, TILES * g + j - 1)
                act.wait_ge(s_ssum, TILES * g + j + 1 if j >= 2 else TILES * g + 2)
                load_rows(xr[b], rows, g, j, s_xr[b])
                load_gate(b, 0, g, j)

            def load_fin(g, j):
                b = j % 2
                if j < 2:
                    act.wait_ge(s_ssum, TILES * g + TILES + 2)
                    act.wait_ge(s_xn, ln2(g, TILES))
                else:
                    act.wait_ge(s_fin, TILES * g + j - 1 + 2)
                act.wait_ge(s_st[b], 16 + 16 * (TILES * g + j // 2 + 1))
                load_rows(x2[b], rows, g, j, s_sr[b])
                load_gate(b, 1, g, j)

            load_ln1(0, 0)
            load_ln1(0, 1)
            act.wait_ge(s_const, 64)

            def body(kind, g, q, steps, at):
                last = at.get("last", False)
                for what, j in steps:
                    b = j % 2
                    if what == "split":
                        n = (chunks_a if kind == "a" else chunks_f)(g, q) + j
                        _, dst, part = chunk(kind, g, q, j, last)
                        s = slot_of(kind, q, j)
                        act.wait_ge(s_raw[s], raw_count(kind, g, q, j))
                        act.wait_ge(s_proj, region_free(kind, g, q, j, last))
                        if kind == "f" and last and j >= 4:
                            act.wait_ge(s_o, outs_f(g, q) + HT)
                        nc.scalar.copy(dst[0][:, 2 * part:2 * part + 2, :], raw[s][:]).then_inc(s_whi, 1)
                    if what == "proj":
                        n = proj_a(g, q) + j
                        hf, w, hd = j // 8, j // HQ % 2, j % HQ
                        act.wait_ge(s_proj, n + 1)
                        nc.scalar.activation((qT, kT)[w][:, hd, :], ps_p[b][:], ACT.Identity,
                                             bias=qkvb[:, bass.ds(w * H + q * HQ + hd, 1)]).then_inc(s_projd, 1)
                    if what == "fproj":
                        n = proj_f(g, q) + j
                        act.wait_ge(s_proj, n + 1)
                        act.wait_ge(s_hs, hid(g, q) + j + 1)
                        nc.scalar.activation(v_sb[b][:], ps_p[b][:], ACT.Gelu,
                                             bias=f1b[:, bass.ds(q * HQ + j % HQ, 1)]).then_inc(s_projd, 1)
                    if what == "soften":
                        act.wait_ge(s_sub, tiles_a(g, q) + j + 2)
                        nc.scalar.activation(ex[:], sc[:], ACT.Exp, scale=SCALE).then_inc(s_exp, 1)
                    if what == "turn":
                        act.wait_ge(s_t, tiles_a(g, q) + j + 2)
                        nc.scalar.copy(pT[:], ps_pt[:]).then_inc(s_pt, 1)
                    if what == "pv":
                        act.wait_ge(s_pv, tiles_a(g, q) + j + 1)
                        nc.scalar.copy(at_hi[:, j % 4, :], ps_pv[:]).then_inc(s_ahi, 1)
                    if what == "norm1":
                        if kind == "f":
                            gg = g + 1
                        elif isinstance(g, int) and g < 0:
                            gg = 0
                        else:
                            gg = g
                        if j + 2 < TILES and not (kind == "f" and j + 2 >= 6):
                            load_ln1(gg, j + 2)
                    if what in ("turn1", "turn2"):
                        lidx = ln_of(kind, g, q, what, j)
                        act.wait_ge(s_aff, lidx + 1)
                        nc.scalar.copy(xT_hi[:, :, j * P:(j + 1) * P], tmp[:].rearrange("p (k t) -> p k t", k=KC)).then_inc(s_xhi, 1)
                    if what == "norm2":
                        if j + 2 < TILES:
                            load_ln2(g, j + 2)
                        act.wait_ge(s_ssum, TILES * g + j + 1 + 2)
                        act.dma_start(rows[bass.ds((g * TILES + j) * P, P), :], st[b][:]).then_inc(s_st[b], 16)
                    if kind == "a" and last and what == "value" and j in (0, 1):
                        load_ln2(g, j)
                    if kind == "f" and last:
                        if what == "fproj" and j in (5, 6):
                            load_fin(g, j - 5)
                        if what == "fproj" and j == 3 and not (isinstance(g, int) and g == GROUPS - 1):
                            load_ln1(g + 1, 0)
                            load_ln1(g + 1, 1)
                        if what == "fin":
                            if j >= 1:
                                finish(g, j - 1)
                            if j == TILES - 1:
                                finish(g, j)

            def finish(g, j):
                b = j % 2
                act.wait_ge(s_fin, TILES * g + j + 1 + 2)
                act.dma_start(out_rows[bass.ds((g * TILES + j) * P, P), :], st[b][:]).then_inc(s_st[b], 16)
                if j + 2 < TILES:
                    load_fin(g, j + 2)

            for c in range(4):
                act.wait_ge(s_raw[c], 16)
                nc.scalar.copy(first_chunks[c][1][0][:, 2 * (c % 2):2 * (c % 2) + 2, :], raw[c][:]).then_inc(s_whi, 1)
            groups(act, body)

        @block.vector
        def _(dve):
            for c in range(4):
                dve.wait_ge(s_whi, c + 1)
                _, dst, part = first_chunks[c]
                nc.vector.tensor_tensor(dst[1][:, 2 * part:2 * part + 2, :], raw[c][:],
                                        dst[0][:, 2 * part:2 * part + 2, :].bitcast(F32), ALU.subtract).then_inc(s_wlo, 1)
            for s, n in ((s_vd, 1), (s_sub, 1), (s_alo, 1), (s_od, 1), (s_hs, 2)):
                dve.sem_inc(s, n)

            def norm(src, lidx, b):
                nc.vector.bn_stats(stat[:], src[:]).then_inc(s_bn, 1)
                dve.wait_ge(s_bn, lidx + 1)
                dve.nop(nofuse=True)
                nc.vector.bn_aggr(mv[:], stat[:]).then_inc(s_mv, 1)
                dve.wait_ge(s_rstd, lidx + 1)
                nc.vector.tensor_scalar(xn[b][:], src[:], mv[:, 0:1], rstd[:], ALU.subtract, ALU.mult).then_inc(s_xn, 1)

            def body(kind, g, q, steps, at):
                last, first = at.get("last", False), at.get("first", False)
                for what, j in steps:
                    b = j % 2
                    if what == "split":
                        n = (chunks_a if kind == "a" else chunks_f)(g, q) + j
                        _, dst, part = chunk(kind, g, q, j, last)
                        s = slot_of(kind, q, j)
                        dve.wait_ge(s_whi, n + 1)
                        nc.vector.tensor_tensor(dst[1][:, 2 * part:2 * part + 2, :], raw[s][:],
                                                dst[0][:, 2 * part:2 * part + 2, :].bitcast(F32), ALU.subtract).then_inc(s_wlo, 1)
                    if what == "value":
                        dve.wait_ge(s_v, tiles_a(g, q) + j + 1)
                        if j == 0:
                            dve.wait_ge(s_bv, 16 * (QUADS * g + q + 1))
                        nc.vector.tensor_tensor(v_sb[b][:], ps_v[:], bv[:], ALU.add).then_inc(s_vd, 1)
                    if what == "score":
                        n = tiles_a(g, q) + j
                        if first and j == 0:
                            dve.wait_ge(s_pz, 1)
                        dve.wait_ge(s_s, n + 1)
                        S = ps_s[:, 0:HQ * T].rearrange("p (h t) -> p h t", h=HQ)
                        nc.vector.tensor_reduce(mx[:], S, AX.X, ALU.max).then_inc(s_mx, 1)
                        dve.wait_ge(s_mx, n + 1)
                        nc.vector.tensor_tensor(sc[:], S, mx[:].unsqueeze(2).broadcast_to([P, HQ, T]), ALU.subtract).then_inc(s_sub, 1)
                    if what == "soften":
                        n = tiles_a(g, q) + j
                        dve.wait_ge(s_exp, n + 1)
                        nc.vector.tensor_reduce(sm[:], ex[:], AX.X, ALU.add).then_inc(s_sum, 1)
                        dve.wait_ge(s_sum, n + 1)
                        nc.vector.reciprocal(rc[:], sm[:]).then_inc(s_rec, 1)
                        dve.wait_ge(s_rec, n + 1)
                        dve.wait_ge(s_t, n + 1)
                        for i in range(2):
                            r = slice(i * T, (i + 1) * T)
                            lastop = nc.vector.tensor_tensor(pr[r, :, i * T:(i + 1) * T], ex[r, :, :],
                                                             rc[r, :].unsqueeze(2).broadcast_to([T, HQ, T]), ALU.mult)
                        lastop.then_inc(s_p, 1)
                    if what == "pv":
                        n = tiles_a(g, q) + j
                        dve.wait_ge(s_ahi, n + 1)
                        nc.vector.tensor_tensor(at_lo[:, j % 4, :], ps_pv[:], at_hi[:, j % 4, :].bitcast(F32),
                                                ALU.subtract).then_inc(s_alo, 1)
                    if what == "out":
                        dve.wait_ge(s_o, outs_a(g, q) + j + 1)
                        if first and j == 0:
                            dve.wait_ge(s_fin, TILES * g + 2)
                        nc.vector.tensor_tensor(y[:, j, :], ps_out(j)[:], ob[:] if first else y[:, j, :], ALU.add).then_inc(s_od, 1)
                    if what == "fproj":
                        n = hid(g, q) + j
                        dve.wait_ge(s_projd, 2 + proj_f(g, q) + j + 1)
                        hi, lo = (wk, (at_hi, at_lo))[j // HQ]
                        nc.vector.tensor_copy(hi[:, j % HQ, :], v_sb[b][:]).then_inc(s_hhi, 1)
                        dve.wait_ge(s_hhi, n + 1)
                        nc.vector.tensor_tensor(lo[:, j % HQ, :], v_sb[b][:], hi[:, j % HQ, :].bitcast(F32), ALU.subtract).then_inc(s_hs, 1)
                    if what == "fout":
                        dve.wait_ge(s_o, outs_f(g, q) + j + 1)
                        nc.vector.tensor_tensor(y[:, j, :], (ps_o, ps_v)[b][:], b2[:] if first else y[:, j, :], ALU.add).then_inc(s_od, 1)
                    if what == "norm1":
                        n = ln_of(kind, g, q, what, j)
                        gg = g + 1 if kind == "f" else (0 if isinstance(g, int) and g < 0 else g)
                        dve.wait_ge(s_xr[b], xr_count(gg, 0, j))
                        norm(xr[b], n, b)
                    if what == "norm2":
                        n = ln_of(kind, g, q, what, j)
                        dve.wait_ge(s_x2, TILES * g + j + 1)
                        norm(x2[b], n, b)
                    if what in ("turn1", "turn2"):
                        n = ln_of(kind, g, q, what, j)
                        two = 2 * (what == "turn2")
                        gg = g + 1 if (kind == "f" and what == "turn1") else (0 if isinstance(g, int) and g < 0 else g)
                        at_b = bass.ds(2 * (gg * TILES + j), 2)
                        dve.wait_ge(s_lnT, n + 1)
                        wait(dve, s_xlo, n)
                        v4 = lambda a: a.rearrange("p (k b t) -> p k b t", k=KC, b=2)
                        nc.vector.tensor_tensor(v4(tmp[:]), v4(ps_ln[:]),
                                                adaT[:, two + 1, :, at_b].unsqueeze(3).broadcast_to([P, KC, 2, T]), ALU.mult).then_inc(s_aff1, 1)
                        dve.wait_ge(s_aff1, n + 1)
                        nc.vector.tensor_tensor(v4(tmp[:]), v4(tmp[:]),
                                                adaT[:, two, :, at_b].unsqueeze(3).broadcast_to([P, KC, 2, T]), ALU.add).then_inc(s_aff, 1)
                        dve.wait_ge(s_xhi, n + 1)
                        nc.vector.tensor_tensor(xT_lo[:, :, j * P:(j + 1) * P], tmp[:].rearrange("p (k t) -> p k t", k=KC),
                                                xT_hi[:, :, j * P:(j + 1) * P].bitcast(F32), ALU.subtract).then_inc(s_xlo, 1)
            dve.wait_ge(s_const, 64)
            groups(dve, body)

        @block.tensor
        def _(pe):
            pe.sem_inc(s_t, 1)

            def product(dst, a, w, ready=None):
                for k in range(KC):
                    if ready:
                        ready(k)
                    for i, (ha, hw) in enumerate(((0, 0), (0, 1), (1, 0))):
                        last = nc.tensor.matmul(dst, a(ha, k), w(hw, k), start=(k == 0 and i == 0), stop=(k == KC - 1 and i == 2))
                return last

            xT = (xT_hi, xT_lo)
            at = (at_hi, at_lo)

            def body(kind, g, q, steps, flags):
                last, first = flags.get("last", False), flags.get("first", False)
                for what, j in steps:
                    b = j % 2
                    if what == "proj":
                        hf, w, hd = j // 8, j // HQ % 2, j % HQ
                        if j == 0:
                            pe.wait_ge(s_wlo, chunks_a(g, q))
                            pe.wait_ge(s_xlo, ln1(g, HT))
                        if j == 8:
                            pe.wait_ge(s_xlo, ln1(g, TILES))
                        pe.wait_ge(s_projd, proj_a(g, q) + j + 1)
                        W = (wq, wk)[w]
                        product(ps_p[b][:], lambda h, k: W[h][:, k, hd * P:(hd + 1) * P],
                                lambda h, k: xT[h][:, k, hf * HALF:(hf + 1) * HALF]).then_inc(s_proj, 1)
                    if what == "fproj":
                        hf, m = j // HQ, j % HQ
                        if j == 0:
                            pe.wait_ge(s_wlo, chunks_f(g, q))
                            pe.wait_ge(s_xlo, ln2(g, HT))
                        if j == HQ:
                            pe.wait_ge(s_xlo, ln2(g, TILES))
                        pe.wait_ge(s_projd, proj_f(g, q) + j + 1)
                        product(ps_p[b][:], lambda h, k: wq[h][:, k, m * P:(m + 1) * P],
                                lambda h, k: xT[h][:, k, hf * HALF:(hf + 1) * HALF]).then_inc(s_proj, 1)
                    if what == "value":
                        n = tiles_a(g, q) + j
                        if j == 0:
                            pe.wait_ge(s_wlo, chunks_a(g, q) + 2)
                            pe.wait_ge(s_od, outs_a(g, q) + 1)
                        pe.wait_ge(s_vd, n + 1)
                        product(ps_v[:], lambda h, k: xT[h][:, k, j * P:(j + 1) * P],
                                lambda h, k: wv[h][:, k, :]).then_inc(s_v, 1)
                    if what == "score":
                        n = tiles_a(g, q) + j
                        pe.wait_ge(s_projd, 2 + proj_a(g, q) + 8 * (j // HT + 1))
                        pe.wait_ge(s_sub, n + 1)
                        for hd in range(HQ):
                            for i in range(2):
                                c = (j % HT) * P + i * T
                                lastmm = nc.tensor.matmul(ps_s[i * T:(i + 1) * T, hd * T:(hd + 1) * T], qT[:, hd, c:c + T],
                                                          kT[:, hd, c:c + T], start=True, stop=True)
                        lastmm.then_inc(s_s, 1)
                    if what == "turn":
                        n = tiles_a(g, q) + j
                        pe.wait_ge(s_p, n + 1)
                        for hd in range(HQ):
                            lastmm = nc.tensor.transpose(ps_pt[:, hd * P:(hd + 1) * P], pr[:, hd, :], ident[:])
                        lastmm.then_inc(s_t, 1)
                    if what == "pv":
                        n = tiles_a(g, q) + j
                        pe.wait_ge(s_pt, n + 1)
                        pe.wait_ge(s_vd, n + 2)
                        pe.wait_ge(s_alo, n + 1)
                        for hd in range(HQ):
                            lastmm = nc.tensor.matmul(ps_pv[:, hd * P:(hd + 1) * P], v_sb[b][:, hd * P:(hd + 1) * P],
                                                      pT[:, hd * P:(hd + 1) * P], start=True, stop=True)
                        lastmm.then_inc(s_pv, 1)
                    if what == "out":
                        n = tiles_a(g, q) + j
                        if j == 0:
                            pe.wait_ge(s_wlo, chunks_a(g, q) + 4)
                        pe.wait_ge(s_alo, n + 2)
                        pe.wait_ge(s_od, outs_a(g, q) + j + (j < TILES - 2))
                        product(ps_out(j)[:], lambda h, k: at[h][:, j % 4, k * P:(k + 1) * P],
                                lambda h, k: wo[h][:, k, :]).then_inc(s_o, 1)
                    if what == "fout":
                        hf = j // HT
                        if j == 0:
                            pe.wait_ge(s_wlo, chunks_f(g, q) + 2)
                        pe.wait_ge(s_od, outs_f(g, q) + (j if j else 1))
                        Hh = (wk, at)[hf]
                        c = (j % HT) * P
                        ready = (lambda k: pe.wait_ge(s_hs, 2 + hid(g, q) + HQ * hf + k + 1)) if j % HT == 0 else None
                        product((ps_o, ps_v)[b][:], lambda h, k: Hh[h][:, k, c:c + P],
                                lambda h, k: wo[h][:, k, :], ready).then_inc(s_o, 1)
                    if what in ("turn1", "turn2"):
                        n = ln_of(kind, g, q, what, j)
                        pe.wait_ge(s_xn, n + 1)
                        wait(pe, s_aff, n)
                        for k in range(KC):
                            lastmm = nc.tensor.transpose(ps_ln[:, k * P:(k + 1) * P], xn[b][:, k * P:(k + 1) * P], ident[:])
                        lastmm.then_inc(s_lnT, 1)
            groups(pe, body)


_INS = ['x', 'cond_2048', 'L0_cond_W_ih', 'L0_cond_W_hh', 'L0_cond_b_ih', 'L0_cond_b_hh', 'L1_cond_ada_w',
        'L1_cond_ada_b', 'L1_cond_qkv_w', 'L1_cond_qkv_b', 'L1_cond_out_w', 'L1_cond_out_b', 'L1_cond_ffn_w1',
        'L1_cond_ffn_b1', 'L1_cond_ffn_w2', 'L1_cond_ffn_b2']
_OUTS = [((64, 64, 512), 'float32')]


def kernel(**inputs):
    import numpy as _np
    import concourse.bacc as _bacc
    from concourse import mybir as _mybir
    from concourse.bass_utils import run_bass_kernel_spmd as _run

    nc = _bacc.Bacc("TRN2", target_bir_lowering=False, num_devices=1)
    arrays, args = {}, []
    for name in _INS:
        a = _np.ascontiguousarray(inputs[name])
        arrays[f"in_{name}_dram"] = a
        args.append(nc.dram_tensor(f"in_{name}_dram", a.shape, _mybir.dt.from_np(a.dtype), kind="ExternalInput").ap())
    for i, (shape, dtype) in enumerate(_OUTS):
        dt = _mybir.dt.from_np(_np.dtype(dtype))
        args.append(nc.dram_tensor(f"out_{i}_dram", shape, dt, kind="ExternalOutput").ap())
    gru_then_transformer(nc, *args)
    r = _run(nc, [arrays], core_ids=[0])
    return r.results[0]["out_0_dram"]
```

```python
from contextlib import ExitStack

import numpy as np

import concourse.bass as bass
from concourse import mybir

ALU = mybir.AluOpType
ACT = mybir.ActivationFunctionType
AX = mybir.AxisListType
F32 = mybir.dt.float32
F32R = mybir.dt.float32r


def gru_then_transformer(nc, x, cond, w_ih, w_hh, b_ih, b_hh, ada_w, ada_b, qkv_w, qkv_b,
                         out_w, out_b, ffn_w1, ffn_b1, ffn_w2, ffn_b2, out):
    B, T, D = x.shape
    P = 128
    KC = D // P
    G3 = 3 * D
    PAIRS = T // 2

    H, DH = 16, 128
    HQ = 4
    QUADS = H // HQ
    GT = 1024
    GROUPS = B * T // GT
    TILES = GT // P
    SCALE = float(DH) ** -0.5
    EPS = 1e-6

    kept = ExitStack()
    with kept:
        adaT = kept.enter_context(nc.sbuf_tensor("adaT", [P, 4, KC, B], F32))
        ident = kept.enter_context(nc.sbuf_tensor("ident", [P, P], F32))
        res_dram = nc.dram_tensor("res_dram", [B, T, D], F32, kind="Internal").ap()
        gate_dram = nc.dram_tensor("gate_dram", [2, B, D], F32, kind="Internal").ap()
        recurrence(nc, x, cond, w_ih, w_hh, b_ih, b_hh, ada_w, ada_b, res_dram, gate_dram, adaT, ident)
        transformer(nc, qkv_w, qkv_b, out_w, out_b, ffn_w1, ffn_b1, ffn_w2, ffn_b2, res_dram, gate_dram, adaT,
                    ident, out)


def recurrence(nc, x, cond, w_ih, w_hh, b_ih, b_hh, ada_w, ada_b, res_dram, gate_dram, adaT, ident):
    B, T, D = x.shape
    P = 128
    KC = D // P
    G3 = 3 * D
    HD = D // 2
    PAIRS = T // 2
    R, N, Z = range(3)
    COL = {R: 0, N: 2 * D, Z: D}
    ADA_SLOT = {0: 0, 1: 1, 3: 2, 4: 3}

    ctx = ExitStack()
    with ctx:
        def sb(name, shape, dt=F32):
            return ctx.enter_context(nc.sbuf_tensor(name, shape, dt))

        def ps(name):
            return ctx.enter_context(nc.psum_tensor(name, [P, 512], F32))

        def sem(name):
            return ctx.enter_context(nc.semaphore(name))

        wih_hi = sb("wih_hi", [P, KC, G3], F32R)
        wih_lo = sb("wih_lo", [P, KC, G3], F32R)
        whh_hi = sb("whh_hi", [P, KC, G3], F32R)
        whh_lo = sb("whh_lo", [P, KC, G3], F32R)
        raw = sb("raw", [P, 6 * KC * D])
        gru_raw = raw[:].rearrange("p (c n) -> p c n", n=G3)
        ada_raw = raw[:].rearrange("p (i k n) -> p i k n", i=6, k=KC)
        bias_r, bias_r_hh = sb("bias_r", [P, D]), sb("bias_r_hh", [P, D])
        bias_z, bias_z_hh = sb("bias_z", [P, HD]), sb("bias_z_hh", [P, HD])
        bias_n = sb("bias_n", [P, HD])
        bias_hn = sb("bias_hn", [P, D])
        x_pair = sb("x_pair", [P, D])
        xT_hi = sb("xT_hi", [P, KC, P], F32R)
        xT_lo = sb("xT_lo", [P, KC, P], F32R)
        gi_r = [sb(f"gi_r{d}", [P, D]) for d in range(2)]
        gi_n = [sb(f"gi_n{d}", [P, HD]) for d in range(2)]
        gi_z = [sb(f"gi_z{d}", [P, HD]) for d in range(2)]
        t_r, t_n, t_z = sb("t_r", [B, D]), sb("t_n", [B, D]), sb("t_z", [B, HD])
        x_res = [sb(f"x_res{d}", [P, HD]) for d in range(2)]
        xh = [sb(f"xh{d}", [P, HD]) for d in range(2)]
        h = [sb(f"h{d}", [P, HD]) for d in range(2)]
        hT = sb("hT", [P, KC, 2 * B], F32R)
        ar, az, hn, m_t, an = (sb(n, [P, HD]) for n in ("ar", "az", "hn", "m_t", "an"))
        r_t, z_t, n_t, dd, e_t = (sb(n, [P, HD]) for n in ("r_t", "z_t", "n_t", "dd", "e_t"))

        adab_col = sb("adab_col", [P, 6, KC])
        adab_gate = sb("adab_gate", [P, D])
        gate_sb = sb("gate_sb", [P, D])
        condT = sb("condT", [P, KC, B])

        ps_gate = [ps(f"ps_gate_{g}") for g in "rnz"]
        ps_gi = [ps(f"ps_gi_{g}") for g in "rnz"]
        ps_hT = ps("ps_hT")
        ps_xT = ps("ps_xT")
        ps_ada = [ps_gi[R], ps_gi[N], ps_xT]

        s_id0, s_ident = sem("s_id0"), sem("s_ident")
        s_wraw = [sem(f"s_wraw{c}") for c in range(2 * KC)]
        s_whi, s_wlo = sem("s_whi"), sem("s_wlo")
        s_bias_in, s_bias, s_h0 = sem("s_bias_in"), sem("s_bias"), sem("s_h0")
        s_xpair, s_xres = sem("s_xpair"), [sem(f"s_xres{d}") for d in range(2)]
        s_xtr, s_xT_hi, s_xT_lo = sem("s_xtr"), sem("s_xT_hi"), sem("s_xT_lo")
        s_gi_mm, s_gi_raw, s_gi = sem("s_gi_mm"), sem("s_gi_raw"), sem("s_gi")
        s_gate = sem("s_gate")
        s_htr, s_hT_hi, s_hT_lo = sem("s_htr"), sem("s_hT_hi"), sem("s_hT_lo")
        s_tr, s_tn, s_tz = sem("s_tr"), sem("s_tn"), sem("s_tz")
        s_ar, s_az, s_hn, s_m, s_an, s_dd, s_e, s_h = (
            sem(f"s_{n}") for n in ("ar", "az", "hn", "m", "an", "dd", "e", "h"))
        s_r, s_z, s_n = sem("s_r"), sem("s_z"), sem("s_n")
        s_xh = sem("s_xh")
        s_store = [sem(f"s_store{d}") for d in range(2)]
        s_ada_raw, s_ada_mm, s_ada = sem("s_ada_raw"), sem("s_ada_mm"), sem("s_ada")
        s_adab, s_condT, s_gate_st = sem("s_adab"), sem("s_condT"), sem("s_gate_st")

        def wait(eng, s, value):
            if not isinstance(value, int) or value > 0:
                eng.wait_ge(s, value)

        def step_rows(t3, t):
            return t3[:, t, :] if isinstance(t, int) else t3[:, bass.ds(t, 1), :].rearrange("b o n -> b (o n)")

        def fold(c):
            return slice(c * B, (c + 1) * B), slice(c * HD, (c + 1) * HD)

        ps_hT_v = ps_hT[:, 0:HD].rearrange("p (i c b) -> p i c b", i=2, c=2)
        hT_v = hT[:].rearrange("p (c i) m -> p i c m", c=2)
        condT_v = condT[:].rearrange("p (c i) b -> p i c b", c=2)

        ps_z = [ps_gate[Z][:, 0:HD], ps_hT[:, HD:D]]

        block = ctx.enter_context(nc.Block())

        @block.sync
        def _(sp):
            def load_res(p, d):
                for c in range(2):
                    parts, cols = fold(c)
                    sp.dma_start(x_res[d][parts, :], step_rows(x, 2 * p + d)[:, cols]).then_inc(s_xres[d], 16)

            for c in range(2):
                parts, cols = fold(c)
                sp.dma_start(h[1][parts, :], cond[:, cols]).then_inc(s_h0, 16)
            for e in range(2):
                sp.dma_start(x_pair[e * B:(e + 1) * B, :], x[:, e, :]).then_inc(s_xpair, 16)
            for c in range(2 * KC):
                src = (w_ih if c < KC else w_hh)[(c % KC) * P:(c % KC + 1) * P, :]
                sp.dma_start(gru_raw[:, c], src).then_inc(s_wraw[c], 16)
            for d in range(2):
                load_res(0, d)
            sp.wait_ge(s_whi, 2 * KC)
            sp.wait_ge(s_wlo, 2 * KC)
            for i in range(6):
                sp.dma_start(ada_raw[:, i], ada_w[:, i * D:(i + 1) * D].rearrange("(k p) n -> p k n", p=P))\
                    .then_inc(s_ada_raw, 16)

            def body(p, more=True, last=False):
                for d in range(2):
                    sp.wait_ge(s_xh, 2 * p + d + 1)
                    for c in range(2):
                        parts, cols = fold(c)
                        sp.dma_start(step_rows(res_dram, 2 * p + d)[:, cols], xh[d][parts, :])\
                            .then_inc(s_store[d], 16)
                    if not last:
                        load_res(p + 1, d)
                        if d == 0 and more:
                            sp.wait_ge(s_xtr, p + 2)
                            for e in range(2):
                                sp.dma_start(x_pair[e * B:(e + 1) * B, :], step_rows(x, 2 * (p + 2) + e))\
                                    .then_inc(s_xpair, 16)
            body(0)
            with sp.Fori(1, PAIRS - 2) as p:
                body(p)
            body(PAIRS - 2, more=False)
            body(PAIRS - 1, last=True)
            sp.wait_ge(s_ada, 6)
            for i in range(2):
                sp.dma_start(gate_dram[i], gate_sb[i * B:(i + 1) * B, :]).then_inc(s_gate_st, 16)
            for d in range(2):
                sp.wait_ge(s_store[d], 32 * PAIRS)
            sp.wait_ge(s_gate_st, 32)

        @block.gpsimd
        def _(pool):
            nc.gpsimd.memset(ident[:], 0.0).then_inc(s_id0, 1)
            pool.wait_ge(s_id0, 1)
            nc.gpsimd.affine_select(out=ident[:], in_=ident[:], compare_op=ALU.not_equal, fill=1.0,
                                    base=0, pattern=[[-1, P]], channel_multiplier=1).then_inc(s_ident, 1)

            def add_bias(g, count):
                pool.wait_ge(s_gi_raw, count)
                for d in range(2):
                    if g == R:
                        gi, bias = gi_r[d][B:2 * B, :], bias_r[B:2 * B, :]
                    else:
                        gi, bias = (gi_n[d][:], bias_n[:]) if g == N else (gi_z[d][:], bias_z[:])
                    last = nc.gpsimd.tensor_tensor(gi, gi, bias, ALU.add)
                last.then_inc(s_gi, 1)

            pool.wait_ge(s_bias, 2)
            pool.wait_ge(s_bias_in, 9 * 16)
            for g in (R, N, Z):
                wait(pool, s_gi, g)
                add_bias(g, g + 1)

            def body(p, last=False):
                for d in range(2):
                    s = 2 * p + d
                    if d == 1 and not last:
                        pool.wait_ge(s_xh, s)
                        add_bias(R, 3 * (p + 1) + 1)
                    pool.wait_ge(s_gi, 3 * (p + 1) + (d if not last else 0))
                    pool.wait_ge(s_h, s + 1)
                    pool.wait_ge(s_xres[d], 32 * (p + 1))
                    wait(pool, s_store[d], 32 * p)
                    nc.gpsimd.tensor_tensor(xh[d][:], x_res[d][:], h[d][:], ALU.add).then_inc(s_xh, 1)
                if not last:
                    pool.wait_ge(s_xh, s + 1)
                    for g in (N, Z):
                        pool.wait_ge(s_gi, 3 * (p + 1) + g)
                        add_bias(g, 3 * (p + 1) + g + 1)
            body(0)
            with pool.Fori(1, PAIRS - 1) as p:
                body(p)
            body(PAIRS - 1, last=True)

        @block.scalar
        def _(act):
            act.dma_start(bias_r[:], b_ih[0:D].partition_broadcast(P)).then_inc(s_bias_in, 16)
            act.dma_start(bias_r_hh[:], b_hh[0:D].partition_broadcast(P)).then_inc(s_bias_in, 16)
            act.dma_start(bias_hn[:], b_hh[2 * D:].partition_broadcast(P)).then_inc(s_bias_in, 16)
            for c in range(2):
                for tile, b, place, g in ((bias_n, b_ih, c, N), (bias_z, b_ih, 1 - c, Z), (bias_z_hh, b_hh, 1 - c, Z)):
                    first = COL[g] + c * HD
                    act.dma_start(tile[fold(place)[0], :], b[first:first + HD].partition_broadcast(B))\
                        .then_inc(s_bias_in, 16)

            def take_hT():
                nc.scalar.copy(hT_v[:, :, :, 0:B], ps_hT_v).then_inc(s_hT_hi, 1)

            def take_xT():
                nc.scalar.copy(xT_hi[:], ps_xT[:].rearrange("p (k b) -> p k b", k=KC)).then_inc(s_xT_hi, 1)

            def take_gi(g):
                for d in range(2):
                    half = slice(d * B, (d + 1) * B)
                    if g == R:
                        last = nc.scalar.copy(gi_r[d][B:2 * B, :], ps_gi[R][half, :])
                        continue
                    for c in range(2):
                        to = gi_n[d][fold(c)[0], :] if g == N else gi_z[d][fold(1 - c)[0], :]
                        last = nc.scalar.copy(to, ps_gi[g][half, fold(c)[1]])
                last.then_inc(s_gi_raw, 1)

            act.wait_ge(s_htr, 1)
            take_hT()
            act.wait_ge(s_hT_lo, 1)
            nc.scalar.copy(condT_v, ps_hT_v).then_inc(s_condT, 1)
            act.wait_ge(s_xtr, 1)
            take_xT()
            for e in range(2):
                act.dma_start(x_pair[e * B:(e + 1) * B, :], x[:, 2 + e, :]).then_inc(s_xpair, 16)
            for c in range(2 * KC):
                act.wait_ge(s_wraw[c], 16)
                w = wih_hi if c < KC else whh_hi
                nc.scalar.copy(w[:, c % KC, :], gru_raw[:, c]).then_inc(s_whi, 1)
            for g in (R, N, Z):
                act.wait_ge(s_gi_mm, g + 1)
                take_gi(g)
            for i in range(6):
                act.dma_start(adab_col[:, i, :], ada_b[i * D:(i + 1) * D].rearrange("(k p) -> p k", p=P),
                              allow_slow_non_contiguous=True).then_inc(s_adab, 16)
            for i in range(2):
                act.dma_start(adab_gate[i * B:(i + 1) * B, :],
                              ada_b[(2 + 3 * i) * D:(3 + 3 * i) * D].partition_broadcast(B)).then_inc(s_adab, 16)

            def body(p, first=False, last=False):
                for d in range(2):
                    s = 2 * p + d
                    if d == 0 and not last:
                        act.wait_ge(s_xtr, p + 2)
                        act.wait_ge(s_gi_mm, 3 * (p + 1))
                        take_xT()
                    if d == 0 and not first:
                        for g in (N, Z):
                            act.wait_ge(s_gi_mm, 3 * p + g + 1)
                            take_gi(g)
                    act.wait_ge(s_ar, s + 1)
                    nc.scalar.activation(r_t[:], ar[:], ACT.Sigmoid).then_inc(s_r, 1)
                    if d == 1 and not last:
                        act.wait_ge(s_gi_mm, 3 * (p + 1) + 1)
                        act.wait_ge(s_tr, s + 1)
                        take_gi(R)
                    act.wait_ge(s_an, s + 1)
                    nc.scalar.activation(n_t[:], an[:], ACT.Tanh).then_inc(s_n, 1)
                    act.wait_ge(s_az, 2 * s + 2)
                    nc.scalar.activation(z_t[:], az[:], ACT.Sigmoid).then_inc(s_z, 1)
                    if not (last and d == 1):
                        act.wait_ge(s_htr, s + 2)
                        take_hT()
            body(0, first=True)
            with act.Fori(1, PAIRS - 1) as p:
                body(p)
            body(PAIRS - 1, last=True)

        @block.vector
        def _(dve):
            def take_hT_lo():
                nc.vector.tensor_tensor(hT_v[:, :, :, B:2 * B], ps_hT_v, hT_v[:, :, :, 0:B].bitcast(F32),
                                        ALU.subtract).then_inc(s_hT_lo, 1)

            def take_xT_lo():
                nc.vector.tensor_tensor(xT_lo[:], ps_xT[:].rearrange("p (k b) -> p k b", k=KC),
                                        xT_hi[:].bitcast(F32), ALU.subtract).then_inc(s_xT_lo, 1)

            def take_ada(i):
                src = ps_ada[i % 3]
                if i in ADA_SLOT:
                    nc.vector.scalar_tensor_tensor(
                        out=adaT[:, ADA_SLOT[i]], in0=src[:, 0:KC * B].rearrange("p (k b) -> p k b", k=KC),
                        scalar=float(i in (1, 4)), in1=adab_col[:, i, :].unsqueeze(2).broadcast_to([P, KC, B]),
                        op0=ALU.add, op1=ALU.add).then_inc(s_ada, 1)
                else:
                    rows = slice((i // 3) * B, (i // 3 + 1) * B)
                    nc.vector.tensor_tensor(gate_sb[rows, :], src[rows, :], adab_gate[rows, :], ALU.add)\
                        .then_inc(s_ada, 1)

            dve.wait_ge(s_htr, 1)
            dve.wait_ge(s_hT_hi, 1)
            take_hT_lo()
            dve.wait_ge(s_xT_hi, 1)
            take_xT_lo()
            for c in range(2 * KC):
                dve.wait_ge(s_wraw[c], 16)
                dve.wait_ge(s_whi, c + 1)
                hi, lo = (wih_hi, wih_lo) if c < KC else (whh_hi, whh_lo)
                nc.vector.tensor_tensor(lo[:, c % KC, :], gru_raw[:, c], hi[:, c % KC, :].bitcast(F32),
                                        ALU.subtract).then_inc(s_wlo, 1)
            dve.wait_ge(s_bias_in, 9 * 16)
            for bias, more in ((bias_r, bias_r_hh), (bias_z, bias_z_hh)):
                nc.vector.tensor_tensor(bias[:], bias[:], more[:], ALU.add).then_inc(s_bias, 1)
            def body(p, last=False):
                for d in range(2):
                    s = 2 * p + d
                    old, new = h[1 - d], h[d]
                    if d == 0 and not last:
                        dve.wait_ge(s_xT_hi, p + 2)
                        take_xT_lo()
                    dve.wait_ge(s_gate, 4 * s + 1)
                    if d == 0:
                        dve.wait_ge(s_gi, 3 * p + 1)
                    nc.vector.tensor_tensor(t_r[:], ps_gate[R][B:2 * B, :], gi_r[d][B:2 * B, :], ALU.add)\
                        .then_inc(s_tr, 1)
                    dve.wait_ge(s_tr, s + 1)
                    for c in range(2):
                        parts, cols = fold(c)
                        done = nc.vector.tensor_tensor(ar[parts, :], ps_gate[R][0:B, cols], t_r[:, cols], ALU.add)
                    done.then_inc(s_ar, 1)
                    dve.wait_ge(s_gate, 4 * s + 2)
                    nc.vector.tensor_tensor(t_n[:], ps_gate[N][B:2 * B, :], bias_hn[B:2 * B, :], ALU.add)\
                        .then_inc(s_tn, 1)
                    dve.wait_ge(s_tn, s + 1)
                    for c in range(2):
                        parts, cols = fold(c)
                        done = nc.vector.tensor_tensor(hn[parts, :], ps_gate[N][0:B, cols], t_n[:, cols], ALU.add)
                    done.then_inc(s_hn, 1)
                    dve.wait_ge(s_gate, 4 * s + 3)
                    if d == 0:
                        dve.wait_ge(s_gi, 3 * p + 3)
                    nc.vector.tensor_tensor(t_z[:], ps_z[0][B:2 * B, :], gi_z[d][B:2 * B, :], ALU.add)\
                        .then_inc(s_tz, 1)
                    dve.wait_ge(s_r, s + 1)
                    dve.wait_ge(s_hn, s + 1)
                    nc.vector.tensor_tensor(m_t[:], hn[:], r_t[:], ALU.mult).then_inc(s_m, 1)
                    dve.wait_ge(s_tz, s + 1)
                    nc.vector.tensor_tensor(az[0:B, :], ps_z[0][0:B, :], t_z[:], ALU.add).then_inc(s_az, 1)
                    dve.wait_ge(s_m, s + 1)
                    nc.vector.tensor_tensor(an[:], m_t[:], gi_n[d][:], ALU.add).then_inc(s_an, 1)
                    dve.wait_ge(s_gate, 4 * s + 4)
                    nc.vector.tensor_tensor(az[B:2 * B, :], ps_z[1][0:B, :], gi_z[d][0:B, :], ALU.add)\
                        .then_inc(s_az, 1)
                    dve.wait_ge(s_n, s + 1)
                    nc.vector.tensor_tensor(dd[:], old[:], n_t[:], ALU.subtract).then_inc(s_dd, 1)
                    dve.wait_ge(s_z, s + 1)
                    dve.wait_ge(s_dd, s + 1)
                    nc.vector.tensor_tensor(e_t[:], dd[:], z_t[:], ALU.mult).then_inc(s_e, 1)
                    dve.wait_ge(s_e, s + 1)
                    wait(dve, s_xh, s - 1)
                    nc.vector.tensor_tensor(new[:], e_t[:], n_t[:], ALU.add).then_inc(s_h, 1)
                    if not (last and d == 1):
                        dve.wait_ge(s_hT_hi, s + 2)
                        take_hT_lo()
                    if last:
                        if d == 0:
                            dve.wait_ge(s_adab, 8 * 16)
                        for i in range(3 * d, 3 * d + 3):
                            dve.wait_ge(s_ada_mm, i + 1)
                            take_ada(i)
            body(0)
            with dve.Fori(1, PAIRS - 1) as p:
                body(p)
            body(PAIRS - 1, last=True)

        @block.tensor
        def _(pe):
            def turn_h(d):
                for i in range(2):
                    last = nc.tensor.transpose(ps_hT[:, i * P:(i + 1) * P], h[d][:, i * P:(i + 1) * P], ident[:])
                last.then_inc(s_htr, 1)

            def turn_x():
                for k in range(KC):
                    last = nc.tensor.transpose(ps_xT[:, k * P:(k + 1) * P], x_pair[:, k * P:(k + 1) * P], ident[:])
                last.then_inc(s_xtr, 1)

            def project_x(g, ks):
                for k in ks:
                    for n, (a, w) in enumerate(((xT_hi, wih_hi), (xT_hi, wih_lo), (xT_lo, wih_hi))):
                        last = nc.tensor.matmul(ps_gi[g][:], a[:, k, :], w[:, k, COL[g]:COL[g] + D],
                                                start=(k == 0 and n == 0), stop=(k == KC - 1 and n == 2))
                if ks[-1] == KC - 1:
                    last.then_inc(s_gi_mm, 1)

            def project_h(to, col, cols):
                for k in range(KC):
                    for n, w in enumerate((whh_hi, whh_lo)):
                        last = nc.tensor.matmul(to, hT[:, k, :], w[:, k, col:col + cols],
                                                start=(k == 0 and n == 0), stop=(k == KC - 1 and n == 1))
                last.then_inc(s_gate, 1)

            def project_cond(i):
                if i in ADA_SLOT:
                    for c in range(KC):
                        for k in range(KC):
                            last = nc.tensor.matmul(ps_ada[i % 3][:, c * B:(c + 1) * B],
                                                    ada_raw[:, i, k, c * P:(c + 1) * P],
                                                    condT[:, k, :], start=(k == 0), stop=(k == KC - 1))
                else:
                    rows = slice((i // 3) * B, (i // 3 + 1) * B)
                    for k in range(KC):
                        last = nc.tensor.matmul(ps_ada[i % 3][rows, :], condT[:, k, :], ada_raw[:, i, k, :],
                                                start=(k == 0), stop=(k == KC - 1))
                last.then_inc(s_ada_mm, 1)

            pe.wait_ge(s_ident, 1)
            pe.wait_ge(s_h0, 32)
            turn_h(1)
            pe.wait_ge(s_xpair, 32)
            turn_x()
            pe.wait_ge(s_xT_hi, 1)
            pe.wait_ge(s_xT_lo, 1)
            for k in range(KC):
                pe.wait_ge(s_whi, k + 1)
                pe.wait_ge(s_wlo, k + 1)
                for g in range(3):
                    project_x(g, [k])
            pe.wait_ge(s_condT, 1)
            pe.wait_ge(s_whi, 2 * KC)
            pe.wait_ge(s_wlo, 2 * KC)

            def body(p, last=False):
                if not last:
                    pe.wait_ge(s_xpair, 32 * (p + 2))
                    pe.wait_ge(s_xT_lo, p + 1)
                    turn_x()
                for d in range(2):
                    s = 2 * p + d
                    pe.wait_ge(s_hT_hi, s + 1)
                    pe.wait_ge(s_hT_lo, s + 1)
                    for g in (R, N):
                        project_h(ps_gate[g][:], COL[g], D)
                    project_h(ps_z[0], COL[Z], HD)
                    for k in range(KC):
                        for n, (rows, w) in enumerate(((0, whh_hi), (0, whh_lo), (B, whh_hi))):
                            last_z = nc.tensor.matmul(ps_z[1][0:B, :], hT[:, k, rows:rows + B],
                                                      w[:, k, COL[Z] + HD:COL[Z] + D],
                                                      start=(k == 0 and n == 0), stop=(k == KC - 1 and n == 2))
                    last_z.then_inc(s_gate, 1)
                    if last:
                        if d == 0:
                            pe.wait_ge(s_ada_raw, 6 * 16)
                            pe.wait_ge(s_gi_raw, 3 * p + 3)
                            pe.wait_ge(s_xT_lo, p + 1)
                        for i in range(3 * d, 3 * d + 3):
                            if d == 1:
                                pe.wait_ge(s_ada, i - 2)
                            project_cond(i)
                    elif d == 0:
                        pe.wait_ge(s_xT_hi, p + 2)
                        pe.wait_ge(s_xT_lo, p + 2)
                        pe.wait_ge(s_gi_raw, 3 * p + 3)
                        project_x(R, range(KC))
                        project_x(N, range(KC // 2 - 1))
                    else:
                        project_x(N, range(KC // 2, KC))
                        project_x(Z, range(KC - 1))
                    if not (last and d == 1):
                        pe.wait_ge(s_h, s + 1)
                        turn_h(d)
                    if not last:
                        project_x(*((N, [KC // 2 - 1]) if d == 0 else (Z, [KC - 1])))
            body(0)
            with pe.Fori(1, PAIRS - 1) as p:
                body(p)
            body(PAIRS - 1, last=True)


def transformer(nc, qkv_w, qkv_b, out_w, out_b, ffn_w1, ffn_b1, ffn_w2, ffn_b2, res_dram, gate_dram, adaT,
                ident, out):
    B, T, D = res_dram.shape
    P = 128
    KC = D // P
    H, DH = 16, 128
    HQ = 4
    QUADS = H // HQ
    GT = 1024
    HALF = GT // 2
    GROUPS = B * T // GT
    TILES = GT // P
    HT = TILES // 2
    INNER = H * DH
    SCALE = float(DH) ** -0.5
    EPS = 1e-6
    LAG = 3
    RAW = 4

    PROJ_A, PROJ_F = 4 * HQ, 2 * HQ
    PROJ_G = QUADS * (PROJ_A + PROJ_F)
    CH_A, CH_A_LAST, CH_F, CH_F_LAST = 8, 6, 4, 6
    CH_G = 3 * CH_A + CH_A_LAST + 3 * CH_F + CH_F_LAST

    nc.disable_value_cache = True
    rows = res_dram.rearrange("b t d -> (b t) d")
    out_rows = out.rearrange("b t d -> (b t) d")

    ctx = ExitStack()
    with ctx:
        def sb(name, shape, dt=F32):
            return ctx.enter_context(nc.sbuf_tensor(name, shape, dt))

        def ps(name):
            return ctx.enter_context(nc.psum_tensor(name, [P, 512], F32))

        def sem(name):
            return ctx.enter_context(nc.semaphore(name))

        xT_hi = sb("xnT_hi", [P, KC, GT], F32R)
        xT_lo = sb("xnT_lo", [P, KC, GT], F32R)
        y = sb("y", [P, TILES, D])
        wq, wk, wv, wo = ([sb(f"{n}_{h}", [P, KC, HQ * P], F32R) for h in ("hi", "lo")] for n in ("wq", "wk", "wv", "wo"))
        raw = [sb(f"raw{i}", [P, 2, 512]) for i in range(RAW)]
        qT = sb("qT", [P, HQ, HALF])
        kT = sb("kT", [P, HQ, HALF])
        at_hi = sb("at_hi", [P, 4, HQ * P], F32R)
        at_lo = sb("at_lo", [P, 4, HQ * P], F32R)
        v_sb = [sb(f"v{i}", [P, 512]) for i in range(2)]
        sc = sb("sc", [P, HQ, T])
        ex = sb("ex", [P, HQ, T])
        mx = sb("mx", [P, HQ])
        sm = sb("sm", [P, HQ])
        rc = sb("rc", [P, HQ])
        pr = sb("pr", [P, HQ, P])
        pT = sb("pT", [P, HQ * P])
        xr = [sb(f"xr{i}", [P, D]) for i in range(2)]
        gt = [sb(f"gt{i}", [P, D]) for i in range(2)]
        xn = [sb(f"xn{i}", [P, D]) for i in range(2)]
        x2 = [sb(f"x2{i}", [P, D]) for i in range(2)]
        st = [sb(f"st{i}", [P, D]) for i in range(2)]
        tmp = sb("tmp", [P, D])
        stat = sb("stat", [P, 6])
        mv = sb("mv", [P, 2])
        eps, mhalf, veps = (sb(n, [P, 1]) for n in ("eps", "mhalf", "veps"))
        rstd = sb("rstd", [P, 1])
        qkvb = sb("qkvb", [P, 3 * H])
        f1b = sb("f1b", [P, H])
        bv = sb("bv", [P, HQ * P])
        ob = sb("ob", [P, D])
        b2 = sb("b2", [P, D])

        ps_p = [ps("ps_p0"), ps("ps_p1")]
        ps_v, ps_s, ps_pt, ps_pv, ps_o, ps_ln = (ps(f"ps_{n}") for n in ("v", "s", "pt", "pv", "o", "ln"))

        s_raw = [sem(f"s_raw{i}") for i in range(RAW)]
        s_whi, s_wlo = sem("s_w2hi"), sem("s_w2lo")
        s_proj, s_projd = sem("s_proj"), sem("s_projd")
        s_v, s_vd, s_bv = sem("s_v"), sem("s_vd"), sem("s_bv")
        s_s, s_mx, s_sub, s_exp, s_sum, s_rec, s_p = (sem(f"s_{n}") for n in ("s", "mx", "sub", "exp", "sum", "rec", "p"))
        s_t, s_pt, s_pv, s_ahi, s_alo, s_o, s_od = (sem(f"s_{n}") for n in ("t", "pt", "pv", "ahi", "alo", "o", "od"))
        s_hs = sem("s_hs")
        s_hhi = sem("s_hhi")
        s_xr, s_gt = [sem(f"s_xr{i}") for i in range(2)], [sem(f"s_gt{i}") for i in range(2)]
        s_sr = [sem(f"s_sr{i}") for i in range(2)]
        s_yg, s_x2, s_ssum, s_bn, s_mv, s_veps, s_rstd, s_xn = (sem(f"s_{n}") for n in ("yg", "x2", "ssum", "bn", "mv", "veps", "rstd", "xn"))
        s_lnT, s_aff, s_xhi, s_xlo = (sem(f"s_{n}") for n in ("lnT", "aff", "xhi", "xlo"))
        s_fg, s_fin = sem("s_fg"), sem("s_fin")
        s_st = [sem(f"s_st{i}") for i in range(2)]
        s_const, s_pz, s_credit = sem("s_const"), sem("s_pz"), sem("s_credit")

        def wait(eng, s, value):
            if not isinstance(value, int) or value > 0:
                eng.wait_ge(s, value)

        def proj_a(g, q): return PROJ_G * g + PROJ_A * q
        def proj_f(g, q): return PROJ_G * g + PROJ_A * QUADS + PROJ_F * q
        def outs_a(g, q): return 2 * QUADS * TILES * g + TILES * q
        def outs_f(g, q): return 2 * QUADS * TILES * g + TILES * (QUADS + q)
        def chunks_a(g, q): return 4 + CH_G * g + CH_A * q
        def chunks_f(g, q): return 4 + CH_G * g + 3 * CH_A + CH_A_LAST + CH_F * q
        def tiles_a(g, q): return TILES * (QUADS * g + q)
        def ln1(g, j): return 2 * TILES * g + j
        def ln2(g, j): return 2 * TILES * g + TILES + j
        def hid(g, q): return PROJ_F * (QUADS * g + q)

        def steps_a(first, last):
            ln = {-1: [("norm1", 4)], 0: [("norm1", 5)], 1: [("turn1", 4)], 2: [("turn1", 5)], 3: [("norm1", 6)],
                  4: [("norm1", 7)], 5: [("turn1", 6)], 6: [("turn1", 7)]} if first else {}
            splits = (3, 4, 5, 7) if first else (1, 3, 5, 7)
            yield from ln.get(-1, [])
            for n in range(PROJ_A):
                if n == PROJ_A // 2:
                    for j in range(HT):
                        yield from slot(j, last)
                yield "proj", n
                yield from ln.get(n, [])
                if n in splits:
                    yield "split", splits.index(n)
            for j in range(HT, TILES):
                yield from slot(j, last)
                if not last:
                    yield "split", j
                elif j < HT + 2:
                    yield "split", j
            yield "turn", TILES - 1
            yield "out", TILES - 3
            yield "pv", TILES - 1
            yield "out", TILES - 2
            if last:
                yield "norm2", TILES - 3
            yield "out", TILES - 1

        def slot(j, last):
            yield "score", j
            if j >= 1:
                yield "turn", j - 1
            yield "soften", j
            yield "value", j
            if last and j > LAG:
                yield "turn2", j - LAG - 1
            if j >= LAG:
                yield "out", j - LAG
            if j >= 1:
                yield "pv", j - 1
            if last and j >= LAG:
                yield "norm2", j - LAG

        def steps_f(first, last, more):
            if first:
                yield from [("fproj", 0), ("split", 0), ("turn2", 4), ("norm2", 6), ("fproj", 1), ("split", 1),
                            ("fproj", 2), ("turn2", 5), ("norm2", 7), ("fproj", 3), ("fout", 0), ("turn2", 6),
                            ("fout", 1), ("fout", 2), ("turn2", 7), ("fout", 3)]
                for n in range(HQ, PROJ_F):
                    yield "fproj", n
                for j in range(HT, TILES):
                    yield "fout", j
                    if j in (4, 5):
                        yield "split", j - 2
                return
            ln = {1: [("norm1", 0)], 3: [("norm1", 1)], 4: [("turn1", 0)], 5: [("turn1", 1), ("norm1", 2)],
                  6: [("norm1", 3)], 7: [("turn1", 2)]} if last and more else {}
            for n in range(PROJ_F):
                yield "fproj", n
                if n in (0, 2):
                    yield "split", n // 2
                yield from ln.get(n, [])
            for j in range(TILES):
                yield "fout", j
                if not last:
                    if j in (0, 2):
                        yield "split", 2 + j // 2
                    continue
                if more and j == 0:
                    yield "turn1", 3
                if more and j in (1, 2, 4, 5):
                    yield "split", {1: 2, 2: 3, 4: 4, 5: 5}[j]
                yield "fin", j

        def group(eng, g, body, more):
            body("a", g, 0, steps_a(True, False), dict(first=True))
            with eng.Fori(1, QUADS - 1) as q:
                body("a", g, q, steps_a(False, False), {})
            body("a", g, QUADS - 1, steps_a(False, True), dict(last=True))
            body("f", g, 0, steps_f(True, False, more), dict(first=True))
            with eng.Fori(1, QUADS - 1) as q:
                body("f", g, q, steps_f(False, False, more), {})
            body("f", g, QUADS - 1, steps_f(False, True, more), dict(last=True))

        def groups(eng, body):
            body("a", -1, QUADS - 1, [("norm1", 0), ("norm1", 1), ("turn1", 0), ("start", 0), ("norm1", 2), ("turn1", 1),
                                      ("start", 1), ("norm1", 3), ("turn1", 2), ("start", 2), ("turn1", 3), ("start", 3)], {})
            with eng.Fori(0, GROUPS - 1) as g:
                group(eng, g, body, True)
            group(eng, GROUPS - 1, body, False)

        def w_cols(w, at):
            return w[:, bass.ds(at, HQ * P)].rearrange("(k p) n -> p k n", p=P)

        def w_rows(w, at):
            return w[bass.ds(at, HQ * P), :].rearrange("(k p) n -> p k n", p=P)

        def chunk(kind, g, q, c, last=False):
            W = HQ * P
            if kind == "a":
                if c < 2:
                    return w_cols(qkv_w, 2 * INNER + q * W), wv, c
                if c < 4:
                    return w_rows(out_w, q * W), wo, c - 2
                if last:
                    return w_cols(ffn_w1, 0), wq, c - 4
                if c < 6:
                    return w_cols(qkv_w, (q + 1) * W), wq, c - 4
                return w_cols(qkv_w, INNER + (q + 1) * W), wk, c - 6
            if c < 2:
                return w_rows(ffn_w2, q * W), wo, c
            if not last:
                return w_cols(ffn_w1, (q + 1) * W), wq, c - 2
            if c < 4:
                return w_cols(qkv_w, 0), wq, c - 2
            return w_cols(qkv_w, INNER), wk, c - 4

        def n_chunks(kind, last, more):
            if kind == "a":
                return CH_A_LAST if last else CH_A
            return (CH_F_LAST if more else 2) if last else CH_F

        def slot_of(kind, q, c):
            if kind == "a":
                return c % RAW
            return (2 + c) % RAW

        def raw_count(kind, g, q, c):
            if kind == "a":
                return 16 * (1 + CH_G // RAW * g + CH_A // RAW * q + c // RAW + 1)
            return 16 * (1 + CH_G // RAW * g + (3 * CH_A + CH_A_LAST - 2) // RAW + CH_F // RAW * q + (c + 2) // RAW + 1)

        def region_free(kind, g, q, c, last):
            if kind == "a":
                return proj_a(g, q) + (1 if c < 4 else PROJ_A)
            return proj_f(g, q) + (1 if c < 2 else PROJ_F)

        def ln_of(kind, g, q, what, j):
            if what in ("turn2", "norm2"):
                return ln2(g, j)
            if kind == "f":
                return ln1(g + 1, j)
            if isinstance(g, int) and g < 0:
                return ln1(0, j)
            return ln1(g, j)

        def group_of(kind, g, what):
            if kind == "f" and what in ("norm1", "turn1"):
                return g + 1
            return 0 if isinstance(g, int) and g < 0 else g

        def xr_count(g, which, j):
            return 16 * (TILES * g + which * TILES // 2 + j // 2 + 1)

        def ps_out(j):
            return ps_v if j == TILES - 2 else ps_o

        first_chunks = [(w_cols(qkv_w, 0), wq, 0), (w_cols(qkv_w, 0), wq, 1),
                        (w_cols(qkv_w, INNER), wk, 0), (w_cols(qkv_w, INNER), wk, 1)]

        block = ctx.enter_context(nc.Block())

        @block.sync
        def _(sp):
            for i in range(2):
                sp.sem_inc(s_st[i], 16)
            for c, (src, _, part) in enumerate(first_chunks):
                sp.dma_start(raw[c][:], src[:, 2 * part:2 * part + 2, :]).then_inc(s_raw[c], 16)

            def load_rows(dst, src, g, j, s):
                sp.dma_start(dst[:], src[bass.ds((g * TILES + j) * P, P), :]).then_inc(s, 16)

            def load_gate(b, which, g, j):
                for i in range(2):
                    sp.dma_start(gt[b][i * T:(i + 1) * T, :],
                                  gate_dram[which, bass.ds(2 * (g * TILES + j) + i, 1), :].rearrange("o d -> (o d)").partition_broadcast(T)
                                  ).then_inc(s_gt[b], 16)

            def load_ln2(g, j):
                b = j % 2
                if j < 2:
                    sp.wait_ge(s_xn, ln2(g, 0))
                    sp.wait_ge(s_fin, TILES * g + 2)
                else:
                    sp.wait_ge(s_x2, TILES * g + j - 1)
                sp.wait_ge(s_ssum, TILES * g + j + 1 if j >= 2 else TILES * g + 2)
                load_rows(xr[b], rows, g, j, s_xr[b])
                load_gate(b, 0, g, j)

            def load_fin(g, j):
                b = j % 2
                if j < 2:
                    sp.wait_ge(s_ssum, TILES * g + TILES + 2)
                    sp.wait_ge(s_xn, ln2(g, TILES))
                else:
                    sp.wait_ge(s_fin, TILES * g + j - 1 + 2)
                sp.wait_ge(s_st[b], 16 + 16 * (TILES * g + j // 2 + 1))
                load_rows(x2[b], rows, g, j, s_sr[b])
                load_gate(b, 1, g, j)


            def body(kind, g, q, steps, at):
                if isinstance(g, int) and g < 0:
                    return
                last = at.get("last", False)
                if kind == "a" and last:
                    load_ln2(g, 0)
                    load_ln2(g, 1)
                more = not (isinstance(g, int) and g == GROUPS - 1)
                for c in range(n_chunks(kind, last, more)):
                    if kind == "a" and c == 4:
                        sp.wait_ge(s_vd, tiles_a(g, q) + 1)
                        sp.dma_start(bv[:], qkv_b[bass.ds(2 * INNER + q * HQ * P, HQ * P)].partition_broadcast(P))\
                            .then_inc(s_bv, 16)
                    n = (chunks_a if kind == "a" else chunks_f)(g, q) + c
                    src, _, part = chunk(kind, g, q, c, last)
                    sp.wait_ge(s_wlo, n - RAW + 1)
                    sp.dma_start(raw[slot_of(kind, q, c)][:], src[:, 2 * part:2 * part + 2, :])\
                        .then_inc(s_raw[slot_of(kind, q, c)], 16)
                if kind == "f" and last:
                    load_fin(g, 0)
                    load_fin(g, 1)
                for what, j in steps:
                    if what == "norm2":
                        if j + 2 < TILES:
                            load_ln2(g, j + 2)
                        sp.wait_ge(s_ssum, TILES * g + j + 1 + 2)
                        sp.dma_start(rows[bass.ds((g * TILES + j) * P, P), :], st[j % 2][:]).then_inc(s_st[j % 2], 16)
                    if what == "fin":
                        sp.wait_ge(s_fin, TILES * g + j + 1 + 2)
                        sp.dma_start(out_rows[bass.ds((g * TILES + j) * P, P), :], st[j % 2][:]).then_inc(s_st[j % 2], 16)
                        if j + 2 < TILES:
                            load_fin(g, j + 2)
            groups(sp, body)
            for i in range(2):
                sp.wait_ge(s_st[i], 16 + 16 * TILES * GROUPS)

        @block.gpsimd
        def _(pool):
            nc.gpsimd.memset(pr[:], 0.0).then_inc(s_pz, 1)
            pool.wait_ge(s_pz, 1)
            nc.gpsimd.memset(eps[:], EPS).then_inc(s_pz, 1)
            pool.wait_ge(s_pz, 2)
            nc.gpsimd.memset(mhalf[:], -0.5).then_inc(s_pz, 1)
            pool.wait_ge(s_pz, 3)
            pool.sem_inc(s_ssum, 2)
            pool.sem_inc(s_fin, 2)

            def body(kind, g, q, steps, at):
                for what, j in steps:
                    b = j % 2
                    if what == "norm2":
                        pool.wait_ge(s_od, outs_a(g, QUADS - 1) + j + 2)
                        pool.wait_ge(s_gt[b], 32 * (TILES * g + j // 2 + 1))
                        nc.gpsimd.tensor_tensor(y[:, j, :], y[:, j, :], gt[b][:], ALU.mult).then_inc(s_yg, 1)
                        pool.wait_ge(s_yg, TILES * g + j + 1)
                        pool.wait_ge(s_xr[b], xr_count(g, 1, j))
                        if j >= 2:
                            pool.wait_ge(s_xn, ln2(g, j) - 1)
                        nc.gpsimd.tensor_tensor(x2[b][:], y[:, j, :], xr[b][:], ALU.add).then_inc(s_x2, 1)
                    if what in ("norm1", "norm2"):
                        n = ln_of(kind, g, q, what, j)
                        pool.wait_ge(s_mv, n + 1)
                        nc.gpsimd.tensor_tensor(veps[:], mv[:, 1:2], eps[:], ALU.add).then_inc(s_veps, 1)
                        pool.wait_ge(s_veps, n + 1)
                        nc.gpsimd.tensor_tensor(rstd[:], veps[:], mhalf[:], ALU.pow).then_inc(s_rstd, 1)
                    if what == "norm2":
                        pool.wait_ge(s_x2, TILES * g + j + 1)
                        pool.wait_ge(s_st[b], 16 * (TILES * g + j // 2 + 1))
                        nc.gpsimd.tensor_tensor(st[b][:], x2[b][:], xr[b][:], ALU.add).then_inc(s_ssum, 1)
                    if what == "fin":
                        pool.wait_ge(s_od, outs_f(g, q) + j + 2)
                        pool.wait_ge(s_gt[b], 32 * (TILES * g + TILES // 2 + j // 2 + 1))
                        pool.wait_ge(s_st[b], 16 * (TILES * g + TILES // 2 + j // 2 + 1))
                        nc.gpsimd.tensor_tensor(st[b][:], y[:, j, :], gt[b][:], ALU.mult).then_inc(s_fg, 1)
                        pool.wait_ge(s_fg, TILES * g + j + 1)
                        pool.wait_ge(s_sr[b], 16 * ((TILES // 2) * g + j // 2 + 1))
                        nc.gpsimd.tensor_tensor(st[b][:], st[b][:], x2[b][:], ALU.add).then_inc(s_fin, 1)
            groups(pool, body)

        @block.scalar
        def _(act):
            act.sem_inc(s_projd, 2)

            def load_rows(dst, src, g, j, s):
                act.dma_start(dst[:], src[bass.ds((g * TILES + j) * P, P), :]).then_inc(s, 16)

            def load_ln1(g, j):
                b = j % 2
                if isinstance(g, int) and g == 0:
                    wait(act, s_xn, j - 1)
                else:
                    if j < 2:
                        act.wait_ge(s_ssum, TILES * g + 2)
                        act.wait_ge(s_xn, ln1(g, 0))
                    else:
                        act.wait_ge(s_xn, ln1(g, j) - 1)
                load_rows(xr[b], rows, g, j, s_xr[b])

            load_ln1(0, 0)
            load_ln1(0, 1)
            act.dma_start(qkvb[:], qkv_b.rearrange("(c p) -> p c", p=P), allow_slow_non_contiguous=True).then_inc(s_const, 16)
            act.dma_start(f1b[:], ffn_b1.rearrange("(c p) -> p c", p=P), allow_slow_non_contiguous=True).then_inc(s_const, 16)
            act.dma_start(ob[:], out_b.partition_broadcast(P)).then_inc(s_const, 16)
            act.dma_start(b2[:], ffn_b2.partition_broadcast(P)).then_inc(s_const, 16)

            def body(kind, g, q, steps, at):
                last = at.get("last", False)
                for what, j in steps:
                    b = j % 2
                    if what == "split":
                        n = (chunks_a if kind == "a" else chunks_f)(g, q) + j
                        _, dst, part = chunk(kind, g, q, j, last)
                        s = slot_of(kind, q, j)
                        act.wait_ge(s_raw[s], raw_count(kind, g, q, j))
                        act.wait_ge(s_proj, region_free(kind, g, q, j, last))
                        if kind == "f" and last and j >= 4:
                            act.wait_ge(s_o, outs_f(g, q) + HT)
                        nc.scalar.copy(dst[0][:, 2 * part:2 * part + 2, :], raw[s][:]).then_inc(s_whi, 1)
                    if what == "proj":
                        n = proj_a(g, q) + j
                        hf, w, hd = j // 8, j // HQ % 2, j % HQ
                        act.wait_ge(s_proj, n + 1)
                        nc.scalar.activation((qT, kT)[w][:, hd, :], ps_p[b][:], ACT.Identity,
                                             bias=qkvb[:, bass.ds(w * H + q * HQ + hd, 1)]).then_inc(s_projd, 1)
                    if what == "fproj":
                        n = proj_f(g, q) + j
                        act.wait_ge(s_proj, n + 1)
                        act.wait_ge(s_hs, hid(g, q) + j + 1)
                        nc.scalar.activation(v_sb[b][:], ps_p[b][:], ACT.Gelu,
                                             bias=f1b[:, bass.ds(q * HQ + j % HQ, 1)]).then_inc(s_projd, 1)
                    if what == "soften":
                        act.wait_ge(s_sub, tiles_a(g, q) + j + 2)
                        nc.scalar.activation(ex[:], sc[:], ACT.Exp, scale=SCALE).then_inc(s_exp, 1)
                    if what == "turn":
                        act.wait_ge(s_t, tiles_a(g, q) + j + 2)
                        nc.scalar.copy(pT[:], ps_pt[:]).then_inc(s_pt, 1)
                    if what == "pv":
                        act.wait_ge(s_pv, tiles_a(g, q) + j + 1)
                        nc.scalar.copy(at_hi[:, j % 4, :], ps_pv[:]).then_inc(s_ahi, 1)
                    if what == "start":
                        act.wait_ge(s_raw[j], 16)
                        nc.scalar.copy(first_chunks[j][1][0][:, 2 * (j % 2):2 * (j % 2) + 2, :], raw[j][:]).then_inc(s_whi, 1)
                        if j == 3:
                            act.wait_ge(s_const, 64)
                    if what in ("turn1", "turn2"):
                        n = ln_of(kind, g, q, what, j)
                        two = 2 * (what == "turn2")
                        gg = group_of(kind, g, what)
                        act.wait_ge(s_lnT, n + 1)
                        wait(act, s_xlo, n)
                        for k in range(KC):
                            for i in range(2):
                                c = slice(k * P + i * T, k * P + (i + 1) * T)
                                seq = bass.ds(2 * (gg * TILES + j) + i, 1)
                                done = nc.scalar.activation(tmp[:, c], ps_ln[:, c], ACT.Identity,
                                                            scale=adaT[:, two + 1, k, seq], bias=adaT[:, two, k, seq])
                        done.then_inc(s_aff, 1)
                        act.wait_ge(s_aff, n + 1)
                        nc.scalar.copy(xT_hi[:, :, j * P:(j + 1) * P], tmp[:].rearrange("p (k t) -> p k t", k=KC)).then_inc(s_xhi, 1)
                    starting = isinstance(g, int) and g < 0
                    if what == ("norm1" if starting else "turn1") and j + 2 < TILES and not (kind == "f" and j + 2 >= 6):
                        load_ln1(group_of(kind, g, what), j + 2)
                    if kind == "f" and last and what == "fproj" and j == 0 and not (isinstance(g, int) and g == GROUPS - 1):
                        load_ln1(g + 1, 0)
                        load_ln1(g + 1, 1)
            groups(act, body)

        @block.vector
        def _(dve):
            for s, n in ((s_vd, 1), (s_sub, 1), (s_alo, 1), (s_od, 1), (s_hs, 2)):
                dve.sem_inc(s, n)

            def norm(src, lidx, b):
                nc.vector.bn_stats(stat[:], src[:]).then_inc(s_bn, 1)
                dve.wait_ge(s_bn, lidx + 1)
                dve.nop(nofuse=True)
                nc.vector.bn_aggr(mv[:], stat[:]).then_inc(s_mv, 1)
                dve.wait_ge(s_rstd, lidx + 1)
                nc.vector.tensor_scalar(xn[b][:], src[:], mv[:, 0:1], rstd[:], ALU.subtract, ALU.mult).then_inc(s_xn, 1)

            def body(kind, g, q, steps, at):
                last, first = at.get("last", False), at.get("first", False)
                for what, j in steps:
                    b = j % 2
                    if what == "split":
                        n = (chunks_a if kind == "a" else chunks_f)(g, q) + j
                        _, dst, part = chunk(kind, g, q, j, last)
                        s = slot_of(kind, q, j)
                        dve.wait_ge(s_whi, n + 1)
                        nc.vector.tensor_tensor(dst[1][:, 2 * part:2 * part + 2, :], raw[s][:],
                                                dst[0][:, 2 * part:2 * part + 2, :].bitcast(F32), ALU.subtract).then_inc(s_wlo, 1)
                    if what == "start":
                        dve.wait_ge(s_whi, j + 1)
                        _, dst, part = first_chunks[j]
                        nc.vector.tensor_tensor(dst[1][:, 2 * part:2 * part + 2, :], raw[j][:],
                                                dst[0][:, 2 * part:2 * part + 2, :].bitcast(F32), ALU.subtract).then_inc(s_wlo, 1)
                        if j == 3:
                            dve.wait_ge(s_const, 64)
                    if what == "value":
                        dve.wait_ge(s_v, tiles_a(g, q) + j + 1)
                        if j == 0:
                            dve.wait_ge(s_bv, 16 * (QUADS * g + q + 1))
                        nc.vector.tensor_tensor(v_sb[b][:], ps_v[:], bv[:], ALU.add).then_inc(s_vd, 1)
                    if what == "score":
                        n = tiles_a(g, q) + j
                        if first and j == 0:
                            dve.wait_ge(s_pz, 1)
                        dve.wait_ge(s_s, n + 1)
                        S = ps_s[:, 0:HQ * T].rearrange("p (h t) -> p h t", h=HQ)
                        nc.vector.tensor_reduce(mx[:], S, AX.X, ALU.max).then_inc(s_mx, 1)
                        dve.wait_ge(s_mx, n + 1)
                        nc.vector.tensor_tensor(sc[:], S, mx[:].unsqueeze(2).broadcast_to([P, HQ, T]), ALU.subtract).then_inc(s_sub, 1)
                    if what == "soften":
                        n = tiles_a(g, q) + j
                        dve.wait_ge(s_exp, n + 1)
                        nc.vector.tensor_reduce(sm[:], ex[:], AX.X, ALU.add).then_inc(s_sum, 1)
                        dve.wait_ge(s_sum, n + 1)
                        nc.vector.reciprocal(rc[:], sm[:]).then_inc(s_rec, 1)
                        dve.wait_ge(s_rec, n + 1)
                        dve.wait_ge(s_t, n + 1)
                        for i in range(2):
                            r = slice(i * T, (i + 1) * T)
                            lastop = nc.vector.tensor_tensor(pr[r, :, i * T:(i + 1) * T], ex[r, :, :],
                                                             rc[r, :].unsqueeze(2).broadcast_to([T, HQ, T]), ALU.mult)
                        lastop.then_inc(s_p, 1)
                    if what == "pv":
                        n = tiles_a(g, q) + j
                        dve.wait_ge(s_ahi, n + 1)
                        nc.vector.tensor_tensor(at_lo[:, j % 4, :], ps_pv[:], at_hi[:, j % 4, :].bitcast(F32),
                                                ALU.subtract).then_inc(s_alo, 1)
                    if what == "out":
                        dve.wait_ge(s_o, outs_a(g, q) + j + 1)
                        if first and j == 0:
                            dve.wait_ge(s_fin, TILES * g + 2)
                        nc.vector.tensor_tensor(y[:, j, :], ps_out(j)[:], ob[:] if first else y[:, j, :], ALU.add).then_inc(s_od, 1)
                    if what == "fproj":
                        n = hid(g, q) + j
                        dve.wait_ge(s_projd, 2 + proj_f(g, q) + j + 1)
                        hi, lo = (wk, (at_hi, at_lo))[j // HQ]
                        nc.vector.tensor_copy(hi[:, j % HQ, :], v_sb[b][:]).then_inc(s_hhi, 1)
                        dve.wait_ge(s_hhi, n + 1)
                        nc.vector.tensor_tensor(lo[:, j % HQ, :], v_sb[b][:], hi[:, j % HQ, :].bitcast(F32), ALU.subtract).then_inc(s_hs, 1)
                    if what == "fout":
                        dve.wait_ge(s_o, outs_f(g, q) + j + 1)
                        nc.vector.tensor_tensor(y[:, j, :], (ps_o, ps_v)[b][:], b2[:] if first else y[:, j, :], ALU.add).then_inc(s_od, 1)
                    if what == "norm1":
                        n = ln_of(kind, g, q, what, j)
                        gg = g + 1 if kind == "f" else (0 if isinstance(g, int) and g < 0 else g)
                        dve.wait_ge(s_xr[b], xr_count(gg, 0, j))
                        norm(xr[b], n, b)
                    if what == "norm2":
                        n = ln_of(kind, g, q, what, j)
                        dve.wait_ge(s_x2, TILES * g + j + 1)
                        norm(x2[b], n, b)
                    if what in ("turn1", "turn2"):
                        n = ln_of(kind, g, q, what, j)
                        dve.wait_ge(s_xhi, n + 1)
                        nc.vector.tensor_tensor(xT_lo[:, :, j * P:(j + 1) * P], tmp[:].rearrange("p (k t) -> p k t", k=KC),
                                                xT_hi[:, :, j * P:(j + 1) * P].bitcast(F32), ALU.subtract).then_inc(s_xlo, 1)
            groups(dve, body)

        @block.tensor
        def _(pe):
            pe.sem_inc(s_t, 1)

            def product(dst, a, w, ready=None):
                for k in range(KC):
                    if ready:
                        ready(k)
                    for i, (ha, hw) in enumerate(((0, 0), (0, 1), (1, 0))):
                        last = nc.tensor.matmul(dst, a(ha, k), w(hw, k), start=(k == 0 and i == 0), stop=(k == KC - 1 and i == 2))
                return last

            xT = (xT_hi, xT_lo)
            at = (at_hi, at_lo)

            def body(kind, g, q, steps, flags):
                last, first = flags.get("last", False), flags.get("first", False)
                for what, j in steps:
                    b = j % 2
                    if what == "proj":
                        hf, w, hd = j // 8, j // HQ % 2, j % HQ
                        if j == 0:
                            pe.wait_ge(s_wlo, chunks_a(g, q))
                            pe.wait_ge(s_xlo, ln1(g, HT))
                        if j == 8:
                            pe.wait_ge(s_xlo, ln1(g, TILES))
                        pe.wait_ge(s_projd, proj_a(g, q) + j + 1)
                        W = (wq, wk)[w]
                        product(ps_p[b][:], lambda h, k: W[h][:, k, hd * P:(hd + 1) * P],
                                lambda h, k: xT[h][:, k, hf * HALF:(hf + 1) * HALF]).then_inc(s_proj, 1)
                    if what == "fproj":
                        hf, m = j // HQ, j % HQ
                        if j == 0:
                            pe.wait_ge(s_wlo, chunks_f(g, q))
                            pe.wait_ge(s_xlo, ln2(g, HT))
                        if j == HQ:
                            pe.wait_ge(s_xlo, ln2(g, TILES))
                        pe.wait_ge(s_projd, proj_f(g, q) + j + 1)
                        product(ps_p[b][:], lambda h, k: wq[h][:, k, m * P:(m + 1) * P],
                                lambda h, k: xT[h][:, k, hf * HALF:(hf + 1) * HALF]).then_inc(s_proj, 1)
                    if what == "value":
                        n = tiles_a(g, q) + j
                        if j == 0:
                            pe.wait_ge(s_wlo, chunks_a(g, q) + 2)
                            pe.wait_ge(s_od, outs_a(g, q) + 1)
                        pe.wait_ge(s_vd, n + 1)
                        product(ps_v[:], lambda h, k: xT[h][:, k, j * P:(j + 1) * P],
                                lambda h, k: wv[h][:, k, :]).then_inc(s_v, 1)
                    if what == "score":
                        n = tiles_a(g, q) + j
                        pe.wait_ge(s_projd, 2 + proj_a(g, q) + 8 * (j // HT + 1))
                        pe.wait_ge(s_sub, n + 1)
                        for hd in range(HQ):
                            for i in range(2):
                                c = (j % HT) * P + i * T
                                lastmm = nc.tensor.matmul(ps_s[i * T:(i + 1) * T, hd * T:(hd + 1) * T], qT[:, hd, c:c + T],
                                                          kT[:, hd, c:c + T], start=True, stop=True)
                        lastmm.then_inc(s_s, 1)
                    if what == "turn":
                        n = tiles_a(g, q) + j
                        pe.wait_ge(s_p, n + 1)
                        for hd in range(HQ):
                            lastmm = nc.tensor.transpose(ps_pt[:, hd * P:(hd + 1) * P], pr[:, hd, :], ident[:])
                        lastmm.then_inc(s_t, 1)
                    if what == "pv":
                        n = tiles_a(g, q) + j
                        pe.wait_ge(s_pt, n + 1)
                        pe.wait_ge(s_vd, n + 2)
                        pe.wait_ge(s_alo, n + 1)
                        for hd in range(HQ):
                            lastmm = nc.tensor.matmul(ps_pv[:, hd * P:(hd + 1) * P], v_sb[b][:, hd * P:(hd + 1) * P],
                                                      pT[:, hd * P:(hd + 1) * P], start=True, stop=True)
                        lastmm.then_inc(s_pv, 1)
                    if what == "out":
                        n = tiles_a(g, q) + j
                        if j == 0:
                            pe.wait_ge(s_wlo, chunks_a(g, q) + 4)
                        pe.wait_ge(s_alo, n + 2)
                        pe.wait_ge(s_od, outs_a(g, q) + j + (j < TILES - 2))
                        product(ps_out(j)[:], lambda h, k: at[h][:, j % 4, k * P:(k + 1) * P],
                                lambda h, k: wo[h][:, k, :]).then_inc(s_o, 1)
                    if what == "fout":
                        hf = j // HT
                        if j == 0:
                            pe.wait_ge(s_wlo, chunks_f(g, q) + 2)
                        pe.wait_ge(s_od, outs_f(g, q) + (j if j else 1))
                        Hh = (wk, at)[hf]
                        c = (j % HT) * P
                        ready = (lambda k: pe.wait_ge(s_hs, 2 + hid(g, q) + HQ * hf + k + 1)) if j % HT == 0 else None
                        product((ps_o, ps_v)[b][:], lambda h, k: Hh[h][:, k, c:c + P],
                                lambda h, k: wo[h][:, k, :], ready).then_inc(s_o, 1)
                    if what in ("turn1", "turn2"):
                        n = ln_of(kind, g, q, what, j)
                        pe.wait_ge(s_xn, n + 1)
                        wait(pe, s_aff, n)
                        for k in range(KC):
                            lastmm = nc.tensor.transpose(ps_ln[:, k * P:(k + 1) * P], xn[b][:, k * P:(k + 1) * P], ident[:])
                        lastmm.then_inc(s_lnT, 1)
            groups(pe, body)


_INS = ['x', 'cond_2048', 'L0_cond_W_ih', 'L0_cond_W_hh', 'L0_cond_b_ih', 'L0_cond_b_hh', 'L1_cond_ada_w',
        'L1_cond_ada_b', 'L1_cond_qkv_w', 'L1_cond_qkv_b', 'L1_cond_out_w', 'L1_cond_out_b', 'L1_cond_ffn_w1',
        'L1_cond_ffn_b1', 'L1_cond_ffn_w2', 'L1_cond_ffn_b2']
_OUTS = [((64, 64, 512), 'float32')]


def kernel(**inputs):
    import numpy as _np
    import concourse.bacc as _bacc
    from concourse import mybir as _mybir
    from concourse.bass_utils import run_bass_kernel_spmd as _run

    nc = _bacc.Bacc("TRN2", target_bir_lowering=False, num_devices=1)
    arrays, args = {}, []
    for name in _INS:
        a = _np.ascontiguousarray(inputs[name])
        arrays[f"in_{name}_dram"] = a
        args.append(nc.dram_tensor(f"in_{name}_dram", a.shape, _mybir.dt.from_np(a.dtype), kind="ExternalInput").ap())
    for i, (shape, dtype) in enumerate(_OUTS):
        dt = _mybir.dt.from_np(_np.dtype(dtype))
        args.append(nc.dram_tensor(f"out_{i}_dram", shape, dt, kind="ExternalOutput").ap())
    gru_then_transformer(nc, *args)
    r = _run(nc, [arrays], core_ids=[0])
    return r.results[0]["out_0_dram"]
```

```python
from contextlib import ExitStack

import concourse.bass as bass
from concourse import mybir

ALU = mybir.AluOpType
ACT = mybir.ActivationFunctionType
AX = mybir.AxisListType
F32 = mybir.dt.float32
F32R = mybir.dt.float32r


def gru_then_transformer(nc, x, cond, w_ih, w_hh, b_ih, b_hh, ada_w, ada_b, qkv_w, qkv_b,
                         out_w, out_b, ffn_w1, ffn_b1, ffn_w2, ffn_b2, out):
    B, T, D = x.shape
    P = 128
    KC = D // P

    kept = ExitStack()
    with kept:
        adaT = kept.enter_context(nc.sbuf_tensor("adaT", [P, 4, KC, B], F32))
        ident = kept.enter_context(nc.sbuf_tensor("ident", [P, P], F32))
        res_dram = nc.dram_tensor("res_dram", [B, T, D], F32, kind="Internal").ap()
        gate_dram = nc.dram_tensor("gate_dram", [2, B, D], F32, kind="Internal").ap()
        recurrence(nc, x, cond, w_ih, w_hh, b_ih, b_hh, ada_w, ada_b, res_dram, gate_dram, adaT, ident)
        transformer(nc, qkv_w, qkv_b, out_w, out_b, ffn_w1, ffn_b1, ffn_w2, ffn_b2, res_dram, gate_dram, adaT,
                    ident, out)


def recurrence(nc, x, cond, w_ih, w_hh, b_ih, b_hh, ada_w, ada_b, res_dram, gate_dram, adaT, ident):
    B, T, D = x.shape
    P = 128
    KC = D // P
    G3 = 3 * D
    HD = D // 2
    PAIRS = T // 2
    R, N, Z = range(3)
    COL = {R: 0, N: 2 * D, Z: D}
    ADA_SLOT = {0: 0, 1: 1, 3: 2, 4: 3}

    ctx = ExitStack()
    with ctx:
        def sb(name, shape, dt=F32):
            return ctx.enter_context(nc.sbuf_tensor(name, shape, dt))

        def ps(name):
            return ctx.enter_context(nc.psum_tensor(name, [P, 512], F32))

        def sem(name):
            return ctx.enter_context(nc.semaphore(name))

        wih_hi = sb("wih_hi", [P, KC, G3], F32R)
        wih_lo = sb("wih_lo", [P, KC, G3], F32R)
        whh_hi = sb("whh_hi", [P, KC, G3], F32R)
        whh_lo = sb("whh_lo", [P, KC, G3], F32R)
        raw = sb("raw", [P, 6 * KC * D])
        gru_raw = raw[:].rearrange("p (c n) -> p c n", n=G3)
        ada_raw = raw[:].rearrange("p (i k n) -> p i k n", i=6, k=KC)
        bias_r, bias_r_hh = sb("bias_r", [P, D]), sb("bias_r_hh", [P, D])
        bias_z, bias_z_hh = sb("bias_z", [P, HD]), sb("bias_z_hh", [P, HD])
        bias_n = sb("bias_n", [P, HD])
        bias_hn = sb("bias_hn", [P, D])
        x_pair = sb("x_pair", [P, D])
        xT_hi = sb("xT_hi", [P, KC, P], F32R)
        xT_lo = sb("xT_lo", [P, KC, P], F32R)
        gi_r = [sb(f"gi_r{d}", [P, D]) for d in range(2)]
        gi_n = [sb(f"gi_n{d}", [P, HD]) for d in range(2)]
        gi_z = [sb(f"gi_z{d}", [P, HD]) for d in range(2)]
        t_r, t_n, t_z = sb("t_r", [B, D]), sb("t_n", [B, D]), sb("t_z", [B, HD])
        x_res = [sb(f"x_res{d}", [P, HD]) for d in range(2)]
        xh = [sb(f"xh{d}", [P, HD]) for d in range(2)]
        h = [sb(f"h{d}", [P, HD]) for d in range(2)]
        hT = sb("hT", [P, KC, 2 * B], F32R)
        ar, az, hn, m_t, an = (sb(n, [P, HD]) for n in ("ar", "az", "hn", "m_t", "an"))
        r_t, z_t, n_t, dd, e_t = (sb(n, [P, HD]) for n in ("r_t", "z_t", "n_t", "dd", "e_t"))

        adab_col = sb("adab_col", [P, 6, KC])
        adab_gate = sb("adab_gate", [P, D])
        gate_sb = sb("gate_sb", [P, D])
        condT = sb("condT", [P, KC, B])

        ps_gate = [ps(f"ps_gate_{g}") for g in "rnz"]
        ps_gi = [ps(f"ps_gi_{g}") for g in "rnz"]
        ps_hT = ps("ps_hT")
        ps_xT = ps("ps_xT")
        ps_ada = [ps_gi[R], ps_gi[N], ps_xT]

        s_id0, s_ident = sem("s_id0"), sem("s_ident")
        s_wraw = [sem(f"s_wraw{c}") for c in range(2 * KC)]
        s_whi, s_wlo = sem("s_whi"), sem("s_wlo")
        s_bias_in, s_bias, s_h0 = sem("s_bias_in"), sem("s_bias"), sem("s_h0")
        s_xpair, s_xres = sem("s_xpair"), [sem(f"s_xres{d}") for d in range(2)]
        s_xtr, s_xT_hi, s_xT_lo = sem("s_xtr"), sem("s_xT_hi"), sem("s_xT_lo")
        s_gi_mm, s_gi_raw, s_gi = sem("s_gi_mm"), sem("s_gi_raw"), sem("s_gi")
        s_gate = sem("s_gate")
        s_htr, s_hT_hi, s_hT_lo = sem("s_htr"), sem("s_hT_hi"), sem("s_hT_lo")
        s_tr, s_tn, s_tz = sem("s_tr"), sem("s_tn"), sem("s_tz")
        s_ar, s_az, s_hn, s_m, s_an, s_dd, s_e, s_h = (
            sem(f"s_{n}") for n in ("ar", "az", "hn", "m", "an", "dd", "e", "h"))
        s_r, s_z, s_n = sem("s_r"), sem("s_z"), sem("s_n")
        s_xh = sem("s_xh")
        s_store = [sem(f"s_store{d}") for d in range(2)]
        s_ada_raw, s_ada_mm, s_ada = sem("s_ada_raw"), sem("s_ada_mm"), sem("s_ada")
        s_adab, s_condT, s_gate_st = sem("s_adab"), sem("s_condT"), sem("s_gate_st")

        def wait(eng, s, value):
            if not isinstance(value, int) or value > 0:
                eng.wait_ge(s, value)

        def step_rows(t3, t):
            return t3[:, t, :] if isinstance(t, int) else t3[:, bass.ds(t, 1), :].rearrange("b o n -> b (o n)")

        def fold(c):
            return slice(c * B, (c + 1) * B), slice(c * HD, (c + 1) * HD)

        ps_hT_v = ps_hT[:, 0:HD].rearrange("p (i c b) -> p i c b", i=2, c=2)
        hT_v = hT[:].rearrange("p (c i) m -> p i c m", c=2)
        condT_v = condT[:].rearrange("p (c i) b -> p i c b", c=2)

        ps_z = [ps_gate[Z][:, 0:HD], ps_hT[:, HD:D]]

        block = ctx.enter_context(nc.Block())

        @block.sync
        def _(sp):
            def load_res(p, d):
                for c in range(2):
                    parts, cols = fold(c)
                    sp.dma_start(x_res[d][parts, :], step_rows(x, 2 * p + d)[:, cols]).then_inc(s_xres[d], 16)

            for c in range(2):
                parts, cols = fold(c)
                sp.dma_start(h[1][parts, :], cond[:, cols]).then_inc(s_h0, 16)
            for e in range(2):
                sp.dma_start(x_pair[e * B:(e + 1) * B, :], x[:, e, :]).then_inc(s_xpair, 16)
            for c in range(2 * KC):
                src = (w_ih if c < KC else w_hh)[(c % KC) * P:(c % KC + 1) * P, :]
                sp.dma_start(gru_raw[:, c], src).then_inc(s_wraw[c], 16)
            for d in range(2):
                load_res(0, d)
            sp.wait_ge(s_whi, 2 * KC)
            sp.wait_ge(s_wlo, 2 * KC)
            for i in range(6):
                sp.dma_start(ada_raw[:, i], ada_w[:, i * D:(i + 1) * D].rearrange("(k p) n -> p k n", p=P))\
                    .then_inc(s_ada_raw, 16)

            def body(p, more=True, last=False):
                for d in range(2):
                    sp.wait_ge(s_xh, 2 * p + d + 1)
                    for c in range(2):
                        parts, cols = fold(c)
                        sp.dma_start(step_rows(res_dram, 2 * p + d)[:, cols], xh[d][parts, :])\
                            .then_inc(s_store[d], 16)
                    if not last:
                        load_res(p + 1, d)
                        if d == 0 and more:
                            sp.wait_ge(s_xtr, p + 2)
                            for e in range(2):
                                sp.dma_start(x_pair[e * B:(e + 1) * B, :], step_rows(x, 2 * (p + 2) + e))\
                                    .then_inc(s_xpair, 16)
            body(0)
            with sp.Fori(1, PAIRS - 2) as p:
                body(p)
            body(PAIRS - 2, more=False)
            body(PAIRS - 1, last=True)
            sp.wait_ge(s_ada, 6)
            for i in range(2):
                sp.dma_start(gate_dram[i], gate_sb[i * B:(i + 1) * B, :]).then_inc(s_gate_st, 16)
            for d in range(2):
                sp.wait_ge(s_store[d], 32 * PAIRS)
            sp.wait_ge(s_gate_st, 32)

        @block.gpsimd
        def _(pool):
            nc.gpsimd.memset(ident[:], 0.0).then_inc(s_id0, 1)
            pool.wait_ge(s_id0, 1)
            nc.gpsimd.affine_select(out=ident[:], in_=ident[:], compare_op=ALU.not_equal, fill=1.0,
                                    base=0, pattern=[[-1, P]], channel_multiplier=1).then_inc(s_ident, 1)

            def add_bias(g, count):
                pool.wait_ge(s_gi_raw, count)
                for d in range(2):
                    if g == R:
                        gi, bias = gi_r[d][B:2 * B, :], bias_r[B:2 * B, :]
                    else:
                        gi, bias = (gi_n[d][:], bias_n[:]) if g == N else (gi_z[d][:], bias_z[:])
                    last = nc.gpsimd.tensor_tensor(gi, gi, bias, ALU.add)
                last.then_inc(s_gi, 1)

            pool.wait_ge(s_bias, 2)
            pool.wait_ge(s_bias_in, 9 * 16)
            for g in (R, N, Z):
                wait(pool, s_gi, g)
                add_bias(g, g + 1)

            def body(p, last=False):
                for d in range(2):
                    s = 2 * p + d
                    if d == 1 and not last:
                        pool.wait_ge(s_xh, s)
                        add_bias(R, 3 * (p + 1) + 1)
                    pool.wait_ge(s_gi, 3 * (p + 1) + (d if not last else 0))
                    pool.wait_ge(s_h, s + 1)
                    pool.wait_ge(s_xres[d], 32 * (p + 1))
                    wait(pool, s_store[d], 32 * p)
                    nc.gpsimd.tensor_tensor(xh[d][:], x_res[d][:], h[d][:], ALU.add).then_inc(s_xh, 1)
                if not last:
                    pool.wait_ge(s_xh, s + 1)
                    for g in (N, Z):
                        pool.wait_ge(s_gi, 3 * (p + 1) + g)
                        add_bias(g, 3 * (p + 1) + g + 1)
            body(0)
            with pool.Fori(1, PAIRS - 1) as p:
                body(p)
            body(PAIRS - 1, last=True)

        @block.scalar
        def _(act):
            act.dma_start(bias_r[:], b_ih[0:D].partition_broadcast(P)).then_inc(s_bias_in, 16)
            act.dma_start(bias_r_hh[:], b_hh[0:D].partition_broadcast(P)).then_inc(s_bias_in, 16)
            act.dma_start(bias_hn[:], b_hh[2 * D:].partition_broadcast(P)).then_inc(s_bias_in, 16)
            for c in range(2):
                for tile, b, place, g in ((bias_n, b_ih, c, N), (bias_z, b_ih, 1 - c, Z), (bias_z_hh, b_hh, 1 - c, Z)):
                    first = COL[g] + c * HD
                    act.dma_start(tile[fold(place)[0], :], b[first:first + HD].partition_broadcast(B))\
                        .then_inc(s_bias_in, 16)

            def take_hT():
                nc.scalar.copy(hT_v[:, :, :, 0:B], ps_hT_v).then_inc(s_hT_hi, 1)

            def take_xT():
                nc.scalar.copy(xT_hi[:], ps_xT[:].rearrange("p (k b) -> p k b", k=KC)).then_inc(s_xT_hi, 1)

            def take_gi(g):
                for d in range(2):
                    half = slice(d * B, (d + 1) * B)
                    if g == R:
                        last = nc.scalar.copy(gi_r[d][B:2 * B, :], ps_gi[R][half, :])
                        continue
                    for c in range(2):
                        to = gi_n[d][fold(c)[0], :] if g == N else gi_z[d][fold(1 - c)[0], :]
                        last = nc.scalar.copy(to, ps_gi[g][half, fold(c)[1]])
                last.then_inc(s_gi_raw, 1)

            act.wait_ge(s_htr, 1)
            take_hT()
            act.wait_ge(s_hT_lo, 1)
            nc.scalar.copy(condT_v, ps_hT_v).then_inc(s_condT, 1)
            act.wait_ge(s_xtr, 1)
            take_xT()
            for e in range(2):
                act.dma_start(x_pair[e * B:(e + 1) * B, :], x[:, 2 + e, :]).then_inc(s_xpair, 16)
            for c in range(2 * KC):
                act.wait_ge(s_wraw[c], 16)
                w = wih_hi if c < KC else whh_hi
                nc.scalar.copy(w[:, c % KC, :], gru_raw[:, c]).then_inc(s_whi, 1)
            for g in (R, N, Z):
                act.wait_ge(s_gi_mm, g + 1)
                take_gi(g)
            for i in range(6):
                act.dma_start(adab_col[:, i, :], ada_b[i * D:(i + 1) * D].rearrange("(k p) -> p k", p=P),
                              allow_slow_non_contiguous=True).then_inc(s_adab, 16)
            for i in range(2):
                act.dma_start(adab_gate[i * B:(i + 1) * B, :],
                              ada_b[(2 + 3 * i) * D:(3 + 3 * i) * D].partition_broadcast(B)).then_inc(s_adab, 16)

            def body(p, first=False, last=False):
                for d in range(2):
                    s = 2 * p + d
                    if d == 0 and not last:
                        act.wait_ge(s_xtr, p + 2)
                        act.wait_ge(s_gi_mm, 3 * (p + 1))
                        take_xT()
                    if d == 0 and not first:
                        for g in (N, Z):
                            act.wait_ge(s_gi_mm, 3 * p + g + 1)
                            take_gi(g)
                    act.wait_ge(s_ar, s + 1)
                    nc.scalar.activation(r_t[:], ar[:], ACT.Sigmoid).then_inc(s_r, 1)
                    if d == 1 and not last:
                        act.wait_ge(s_gi_mm, 3 * (p + 1) + 1)
                        act.wait_ge(s_tr, s + 1)
                        take_gi(R)
                    act.wait_ge(s_an, s + 1)
                    nc.scalar.activation(n_t[:], an[:], ACT.Tanh).then_inc(s_n, 1)
                    act.wait_ge(s_az, 2 * s + 2)
                    nc.scalar.activation(z_t[:], az[:], ACT.Sigmoid).then_inc(s_z, 1)
                    if not (last and d == 1):
                        act.wait_ge(s_htr, s + 2)
                        take_hT()
            body(0, first=True)
            with act.Fori(1, PAIRS - 1) as p:
                body(p)
            body(PAIRS - 1, last=True)

        @block.vector
        def _(dve):
            def take_hT_lo():
                nc.vector.tensor_tensor(hT_v[:, :, :, B:2 * B], ps_hT_v, hT_v[:, :, :, 0:B].bitcast(F32),
                                        ALU.subtract).then_inc(s_hT_lo, 1)

            def take_xT_lo():
                nc.vector.tensor_tensor(xT_lo[:], ps_xT[:].rearrange("p (k b) -> p k b", k=KC),
                                        xT_hi[:].bitcast(F32), ALU.subtract).then_inc(s_xT_lo, 1)

            def take_ada(i):
                src = ps_ada[i % 3]
                if i in ADA_SLOT:
                    nc.vector.scalar_tensor_tensor(
                        out=adaT[:, ADA_SLOT[i]], in0=src[:, 0:KC * B].rearrange("p (k b) -> p k b", k=KC),
                        scalar=float(i in (1, 4)), in1=adab_col[:, i, :].unsqueeze(2).broadcast_to([P, KC, B]),
                        op0=ALU.add, op1=ALU.add).then_inc(s_ada, 1)
                else:
                    rows = slice((i // 3) * B, (i // 3 + 1) * B)
                    nc.vector.tensor_tensor(gate_sb[rows, :], src[rows, :], adab_gate[rows, :], ALU.add)\
                        .then_inc(s_ada, 1)

            dve.wait_ge(s_htr, 1)
            dve.wait_ge(s_hT_hi, 1)
            take_hT_lo()
            dve.wait_ge(s_xT_hi, 1)
            take_xT_lo()
            for c in range(2 * KC):
                dve.wait_ge(s_wraw[c], 16)
                dve.wait_ge(s_whi, c + 1)
                hi, lo = (wih_hi, wih_lo) if c < KC else (whh_hi, whh_lo)
                nc.vector.tensor_tensor(lo[:, c % KC, :], gru_raw[:, c], hi[:, c % KC, :].bitcast(F32),
                                        ALU.subtract).then_inc(s_wlo, 1)
            dve.wait_ge(s_bias_in, 9 * 16)
            for bias, more in ((bias_r, bias_r_hh), (bias_z, bias_z_hh)):
                nc.vector.tensor_tensor(bias[:], bias[:], more[:], ALU.add).then_inc(s_bias, 1)
            def body(p, last=False):
                for d in range(2):
                    s = 2 * p + d
                    old, new = h[1 - d], h[d]
                    if d == 0 and not last:
                        dve.wait_ge(s_xT_hi, p + 2)
                        take_xT_lo()
                    dve.wait_ge(s_gate, 4 * s + 1)
                    if d == 0:
                        dve.wait_ge(s_gi, 3 * p + 1)
                    nc.vector.tensor_tensor(t_r[:], ps_gate[R][B:2 * B, :], gi_r[d][B:2 * B, :], ALU.add)\
                        .then_inc(s_tr, 1)
                    dve.wait_ge(s_tr, s + 1)
                    for c in range(2):
                        parts, cols = fold(c)
                        done = nc.vector.tensor_tensor(ar[parts, :], ps_gate[R][0:B, cols], t_r[:, cols], ALU.add)
                    done.then_inc(s_ar, 1)
                    dve.wait_ge(s_gate, 4 * s + 2)
                    nc.vector.tensor_tensor(t_n[:], ps_gate[N][B:2 * B, :], bias_hn[B:2 * B, :], ALU.add)\
                        .then_inc(s_tn, 1)
                    dve.wait_ge(s_tn, s + 1)
                    for c in range(2):
                        parts, cols = fold(c)
                        done = nc.vector.tensor_tensor(hn[parts, :], ps_gate[N][0:B, cols], t_n[:, cols], ALU.add)
                    done.then_inc(s_hn, 1)
                    dve.wait_ge(s_gate, 4 * s + 3)
                    if d == 0:
                        dve.wait_ge(s_gi, 3 * p + 3)
                    nc.vector.tensor_tensor(t_z[:], ps_z[0][B:2 * B, :], gi_z[d][B:2 * B, :], ALU.add)\
                        .then_inc(s_tz, 1)
                    dve.wait_ge(s_r, s + 1)
                    dve.wait_ge(s_hn, s + 1)
                    nc.vector.tensor_tensor(m_t[:], hn[:], r_t[:], ALU.mult).then_inc(s_m, 1)
                    dve.wait_ge(s_tz, s + 1)
                    nc.vector.tensor_tensor(az[0:B, :], ps_z[0][0:B, :], t_z[:], ALU.add).then_inc(s_az, 1)
                    dve.wait_ge(s_m, s + 1)
                    nc.vector.tensor_tensor(an[:], m_t[:], gi_n[d][:], ALU.add).then_inc(s_an, 1)
                    dve.wait_ge(s_gate, 4 * s + 4)
                    nc.vector.tensor_tensor(az[B:2 * B, :], ps_z[1][0:B, :], gi_z[d][0:B, :], ALU.add)\
                        .then_inc(s_az, 1)
                    dve.wait_ge(s_n, s + 1)
                    nc.vector.tensor_tensor(dd[:], old[:], n_t[:], ALU.subtract).then_inc(s_dd, 1)
                    dve.wait_ge(s_z, s + 1)
                    dve.wait_ge(s_dd, s + 1)
                    nc.vector.tensor_tensor(e_t[:], dd[:], z_t[:], ALU.mult).then_inc(s_e, 1)
                    dve.wait_ge(s_e, s + 1)
                    wait(dve, s_xh, s - 1)
                    nc.vector.tensor_tensor(new[:], e_t[:], n_t[:], ALU.add).then_inc(s_h, 1)
                    if not (last and d == 1):
                        dve.wait_ge(s_hT_hi, s + 2)
                        take_hT_lo()
                    if last:
                        if d == 0:
                            dve.wait_ge(s_adab, 8 * 16)
                        for i in range(3 * d, 3 * d + 3):
                            dve.wait_ge(s_ada_mm, i + 1)
                            take_ada(i)
            body(0)
            with dve.Fori(1, PAIRS - 1) as p:
                body(p)
            body(PAIRS - 1, last=True)

        @block.tensor
        def _(pe):
            def turn_h(d):
                for i in range(2):
                    last = nc.tensor.transpose(ps_hT[:, i * P:(i + 1) * P], h[d][:, i * P:(i + 1) * P], ident[:])
                last.then_inc(s_htr, 1)

            def turn_x():
                for k in range(KC):
                    last = nc.tensor.transpose(ps_xT[:, k * P:(k + 1) * P], x_pair[:, k * P:(k + 1) * P], ident[:])
                last.then_inc(s_xtr, 1)

            def project_x(g, ks):
                for k in ks:
                    for n, (a, w) in enumerate(((xT_hi, wih_hi), (xT_hi, wih_lo), (xT_lo, wih_hi))):
                        last = nc.tensor.matmul(ps_gi[g][:], a[:, k, :], w[:, k, COL[g]:COL[g] + D],
                                                start=(k == 0 and n == 0), stop=(k == KC - 1 and n == 2))
                if ks[-1] == KC - 1:
                    last.then_inc(s_gi_mm, 1)

            def project_h(to, col, cols):
                for k in range(KC):
                    for n, w in enumerate((whh_hi, whh_lo)):
                        last = nc.tensor.matmul(to, hT[:, k, :], w[:, k, col:col + cols],
                                                start=(k == 0 and n == 0), stop=(k == KC - 1 and n == 1))
                last.then_inc(s_gate, 1)

            def project_cond(i):
                if i in ADA_SLOT:
                    for c in range(KC):
                        for k in range(KC):
                            last = nc.tensor.matmul(ps_ada[i % 3][:, c * B:(c + 1) * B],
                                                    ada_raw[:, i, k, c * P:(c + 1) * P],
                                                    condT[:, k, :], start=(k == 0), stop=(k == KC - 1))
                else:
                    rows = slice((i // 3) * B, (i // 3 + 1) * B)
                    for k in range(KC):
                        last = nc.tensor.matmul(ps_ada[i % 3][rows, :], condT[:, k, :], ada_raw[:, i, k, :],
                                                start=(k == 0), stop=(k == KC - 1))
                last.then_inc(s_ada_mm, 1)

            pe.wait_ge(s_ident, 1)
            pe.wait_ge(s_h0, 32)
            turn_h(1)
            pe.wait_ge(s_xpair, 32)
            turn_x()
            pe.wait_ge(s_xT_hi, 1)
            pe.wait_ge(s_xT_lo, 1)
            for k in range(KC):
                pe.wait_ge(s_whi, k + 1)
                pe.wait_ge(s_wlo, k + 1)
                for g in range(3):
                    project_x(g, [k])
            pe.wait_ge(s_condT, 1)
            pe.wait_ge(s_whi, 2 * KC)
            pe.wait_ge(s_wlo, 2 * KC)

            def body(p, last=False):
                if not last:
                    pe.wait_ge(s_xpair, 32 * (p + 2))
                    pe.wait_ge(s_xT_lo, p + 1)
                    turn_x()
                for d in range(2):
                    s = 2 * p + d
                    pe.wait_ge(s_hT_hi, s + 1)
                    pe.wait_ge(s_hT_lo, s + 1)
                    for g in (R, N):
                        project_h(ps_gate[g][:], COL[g], D)
                    project_h(ps_z[0], COL[Z], HD)
                    for k in range(KC):
                        for n, (rows, w) in enumerate(((0, whh_hi), (0, whh_lo), (B, whh_hi))):
                            last_z = nc.tensor.matmul(ps_z[1][0:B, :], hT[:, k, rows:rows + B],
                                                      w[:, k, COL[Z] + HD:COL[Z] + D],
                                                      start=(k == 0 and n == 0), stop=(k == KC - 1 and n == 2))
                    last_z.then_inc(s_gate, 1)
                    if last:
                        if d == 0:
                            pe.wait_ge(s_ada_raw, 6 * 16)
                            pe.wait_ge(s_gi_raw, 3 * p + 3)
                            pe.wait_ge(s_xT_lo, p + 1)
                        for i in range(3 * d, 3 * d + 3):
                            if d == 1:
                                pe.wait_ge(s_ada, i - 2)
                            project_cond(i)
                    elif d == 0:
                        pe.wait_ge(s_xT_hi, p + 2)
                        pe.wait_ge(s_xT_lo, p + 2)
                        pe.wait_ge(s_gi_raw, 3 * p + 3)
                        project_x(R, range(KC))
                        project_x(N, range(KC // 2 - 1))
                    else:
                        project_x(N, range(KC // 2, KC))
                        project_x(Z, range(KC - 1))
                    if not (last and d == 1):
                        pe.wait_ge(s_h, s + 1)
                        turn_h(d)
                    if not last:
                        project_x(*((N, [KC // 2 - 1]) if d == 0 else (Z, [KC - 1])))
            body(0)
            with pe.Fori(1, PAIRS - 1) as p:
                body(p)
            body(PAIRS - 1, last=True)


def transformer(nc, qkv_w, qkv_b, out_w, out_b, ffn_w1, ffn_b1, ffn_w2, ffn_b2, res_dram, gate_dram, adaT,
                ident, out):
    B, T, D = res_dram.shape
    P = 128
    KC = D // P
    H, DH = 16, 128
    HQ = 4
    QUADS = H // HQ
    GT = 1024
    HALF = GT // 2
    GROUPS = B * T // GT
    TILES = GT // P
    HT = TILES // 2
    INNER = H * DH
    SCALE = float(DH) ** -0.5
    EPS = 1e-6
    RAW = 4
    FIN = HQ
    FIN0 = FIN + 1

    PROJ_A, PROJ_F = 2 * HQ * 2, HQ * 2
    PROJ_G = QUADS * (PROJ_A + PROJ_F)
    CH_A, CH_A_LAST, CH_F, CH_F_LAST = 8, 6, 4, 6
    CH_G = 3 * CH_A + CH_A_LAST + 3 * CH_F + CH_F_LAST

    nc.disable_value_cache = True
    rows = res_dram.rearrange("b t d -> (b t) d")
    out_rows = out.rearrange("b t d -> (b t) d")

    ctx = ExitStack()
    with ctx:
        def sb(name, shape, dt=F32):
            return ctx.enter_context(nc.sbuf_tensor(name, shape, dt))

        def ps(name):
            return ctx.enter_context(nc.psum_tensor(name, [P, 512], F32))

        def sem(name):
            return ctx.enter_context(nc.semaphore(name))

        xT_hi = sb("xnT_hi", [P, KC, GT], F32R)
        xT_lo = sb("xnT_lo", [P, KC, GT], F32R)
        y = sb("y", [P, TILES, D])
        wq, wk, wv, wo = ([sb(f"{n}_{h}", [P, KC, HQ * P], F32R) for h in ("hi", "lo")] for n in ("wq", "wk", "wv", "wo"))
        raw = [sb(f"raw{i}", [P, 2, HQ * P]) for i in range(RAW)]
        qT = sb("qT", [P, HQ, HALF])
        kT = sb("kT", [P, HQ, HALF])
        at_hi = sb("at_hi", [P, 4, HQ * P], F32R)
        at_lo = sb("at_lo", [P, 4, HQ * P], F32R)
        v_sb = [sb(f"v{i}", [P, HQ * P]) for i in range(2)]
        sc, ex = (sb(n, [P, HQ, T]) for n in ("sc", "ex"))
        row_max, row_sum, row_rec = (sb(n, [P, HQ]) for n in ("row_max", "row_sum", "row_rec"))
        pr = sb("pr", [P, HQ, P])
        pT = sb("pT", [P, HQ * P])
        xr = [sb(f"xr{i}", [P, D]) for i in range(2)]
        gt = [sb(f"gt{i}", [P, D]) for i in range(2)]
        xn = [sb(f"xn{i}", [P, D]) for i in range(2)]
        x2 = [sb(f"x2{i}", [P, D]) for i in range(2)]
        st = [sb(f"st{i}", [P, D]) for i in range(2)]
        tmp = sb("tmp", [P, D])
        stat = sb("stat", [P, 6])
        mv = sb("mv", [P, 2])
        eps, mhalf, veps, rstd = (sb(n, [P, 1]) for n in ("eps", "mhalf", "veps", "rstd"))
        qkvb = sb("qkvb", [P, 3 * H])
        f1b = sb("f1b", [P, H])
        bv = sb("bv", [P, HQ * P])
        ob = sb("ob", [P, D])
        b2 = sb("b2", [P, D])

        ps_p = [ps("ps_p0"), ps("ps_p1")]
        ps_v, ps_s, ps_pt, ps_pv, ps_o, ps_ln = (ps(f"ps_{n}") for n in ("v", "s", "pt", "pv", "o", "ln"))

        s_raw = [sem(f"s_raw{i}") for i in range(RAW)]
        s_w_hi, s_w_lo = sem("s_w_hi"), sem("s_w_lo")
        s_proj, s_proj_taken = sem("s_proj"), sem("s_proj_taken")
        s_value, s_value_taken = sem("s_value"), sem("s_value_taken")
        s_score, s_score_taken = sem("s_score"), sem("s_score_taken")
        s_turned, s_turned_taken = sem("s_turned"), sem("s_turned_taken")
        s_head, s_head_hi, s_head_lo = sem("s_head"), sem("s_head_hi"), sem("s_head_lo")
        s_out, s_out_taken = sem("s_out"), sem("s_out_taken")
        s_max, s_exp, s_sum, s_rec, s_prob = (sem(f"s_{n}") for n in ("max", "exp", "sum", "rec", "prob"))
        s_hid_hi, s_hid_lo = sem("s_hid_hi"), sem("s_hid_lo")
        s_xr, s_gt = [sem(f"s_xr{i}") for i in range(2)], [sem(f"s_gt{i}") for i in range(2)]
        s_sum_here, s_gate_here = [sem(f"s_sum_here{i}") for i in range(FIN)], [sem(f"s_gate_here{i}") for i in range(FIN)]
        s_gated, s_x2, s_twice = sem("s_gated"), sem("s_x2"), sem("s_twice")
        s_moments, s_mv, s_veps, s_rstd, s_xn = (sem(f"s_{n}") for n in ("moments", "mv", "veps", "rstd", "xn"))
        s_lnT, s_scaled, s_aff, s_xhi, s_xlo = (sem(f"s_{n}") for n in ("lnT", "scaled", "aff", "xhi", "xlo"))
        s_end_gated, s_end = sem("s_end_gated"), sem("s_end")
        s_stored = [sem(f"s_stored{i}") for i in range(2)]
        s_const, s_bv, s_fill = sem("s_const"), sem("s_bv"), sem("s_fill")

        def wait(eng, s, value):
            if not isinstance(value, int) or value > 0:
                eng.wait_ge(s, value)

        def proj_a(g, q): return PROJ_G * g + PROJ_A * q
        def proj_f(g, q): return PROJ_G * g + PROJ_A * QUADS + PROJ_F * q
        def outs_a(g, q): return 2 * QUADS * TILES * g + TILES * q
        def outs_f(g, q): return 2 * QUADS * TILES * g + TILES * (QUADS + q)
        def chunks_a(g, q): return 4 + CH_G * g + CH_A * q
        def chunks_f(g, q): return 4 + CH_G * g + 3 * CH_A + CH_A_LAST + CH_F * q
        def tiles_a(g, q): return TILES * (QUADS * g + q)
        def ln1(g, j): return 2 * TILES * g + j
        def ln2(g, j): return 2 * TILES * g + TILES + j
        def hid(g, q): return PROJ_F * (QUADS * g + q)

        def half(c, between, fill):
            yield from [("value", c), ("keep", c), ("score", c), ("soften", c)]
            yield from between[0]
            yield from [("value", c + 1), ("keep", c + 1), ("score", c + 1), ("turn", c), ("soften", c + 1)]
            yield from between[1]
            for j in (c + 2, c + 3):
                yield from [("value", j), ("pv", j - 2), ("keep", j), ("lower", j - 2), ("score", j),
                            ("turn", j - 1), ("soften", j)]
                yield from between[j - c]
            yield from fill[0]
            yield from [("pv", c + 2), ("lower", c + 2), ("turn", c + 3)]
            yield from fill[1]
            yield from [("pv", c + 3), ("lower", c + 3)]

        def norm(which, j):
            return [("norm" + which, j), ("scale" + which, j)]

        def shift(which, j):
            return [("shift" + which, j), ("halve" + which, j)]

        def steps_a(first, last):
            none = {}
            ln = {1: norm("1", 4), 2: norm("1", 5), 3: [("turn1", 4)], 4: shift("1", 4),
                  5: [("turn1", 5)] + norm("1", 6), 6: shift("1", 5),
                  7: [("turn1", 6)] + norm("1", 7)} if first else none
            splits = (3, 4, 5, 6) if first else (0, 2, 4, 6)
            for n in range(PROJ_A // 2):
                yield "proj", n
                yield from ln.get(n, [])
                if n in splits:
                    yield "split", splits.index(n)
            between = [shift("1", 6), [("turn1", 7)], shift("1", 7), []] if first else [[]] * 4
            yield from half(0, between, ([("proj", 8)], [("proj", 9)]))
            ln = {12: norm("2", 0), 13: [("turn2", 0)] + norm("2", 1), 14: shift("2", 0),
                  15: [("turn2", 1)] + norm("2", 2)} if last else none
            for n in range(10, PROJ_A):
                yield "proj", n
                if n < 14:
                    yield "out", n - 10
                yield from ln.get(n, [])
            if last:
                between = [shift("2", 1), [("turn2", 2)] + norm("2", 3), shift("2", 2), [("turn2", 3), ("split", 4)]]
            else:
                between = [[("split", 4)], [("split", 5)], [("split", 6)], []]
            yield from half(HT, between, ([("out", 4)] + (shift("2", 3) if last else []), [("out", 5)]))
            if last:
                yield from [("split", 5)] + norm("2", 4)
            yield "out", 6
            yield "out", 7
            if last:
                yield from [("turn2", 4)] + norm("2", 5)
            else:
                yield "split", 7

        def steps_f(first, last, more):
            if first:
                yield from ([("fproj", 0)] + shift("2", 4) + norm("2", 6) + [("fproj", 1), ("split", 0), ("fproj", 2),
                             ("turn2", 5)] + shift("2", 5) + [("split", 1)] + norm("2", 7) + [("fproj", 3),
                             ("turn2", 6), ("fout", 0)] + shift("2", 6) + [("fout", 1), ("turn2", 7), ("fout", 2)] +
                            shift("2", 7) + [("fout", 3)])
                for n in range(HQ, PROJ_F):
                    yield "fproj", n
                for j in range(HT, TILES):
                    yield "fout", j
                    if j in (4, 5):
                        yield "split", j - 2
                return
            ln = {1: [("norm1", 0), ("scale1", 0)], 3: [("norm1", 1), ("scale1", 1)], 4: [("turn1", 0)],
                  5: [("shift1", 0), ("halve1", 0)], 6: [("norm1", 2), ("scale1", 2), ("turn1", 1)],
                  7: [("shift1", 1), ("halve1", 1)]} if last and more else {}
            late = {0: [("norm1", 3), ("scale1", 3), ("turn1", 2)], 1: [("shift1", 2), ("halve1", 2)],
                    2: [("turn1", 3)], 3: [("shift1", 3), ("halve1", 3)]}
            for n in range(PROJ_F):
                yield "fproj", n
                if n in (0, 2):
                    yield "split", n // 2
                yield from ln.get(n, [])
            for j in range(TILES):
                yield "fout", j
                if not last:
                    if j in (0, 2):
                        yield "split", 2 + j // 2
                    continue
                if more and j in late:
                    yield from late[j]
                if more and j in (1, 2, 4, 5):
                    yield "split", {1: 2, 2: 3, 4: 4, 5: 5}[j]
                yield "fin", j

        def group(eng, g, body, more):
            body("a", g, 0, steps_a(True, False), dict(first=True))
            with eng.Fori(1, QUADS - 1) as q:
                body("a", g, q, steps_a(False, False), {})
            body("a", g, QUADS - 1, steps_a(False, True), dict(last=True))
            body("f", g, 0, steps_f(True, False, more), dict(first=True))
            with eng.Fori(1, QUADS - 1) as q:
                body("f", g, q, steps_f(False, False, more), {})
            body("f", g, QUADS - 1, steps_f(False, True, more), dict(last=True))

        def groups(eng, body):
            body("a", -1, QUADS - 1, norm("1", 0) + [("norm1", 1), ("turn1", 0), ("scale1", 1), ("shift1", 0), ("start", 0),
                                      ("turn1", 1), ("norm1", 2), ("halve1", 0), ("shift1", 1), ("scale1", 2),
                                      ("start", 1), ("halve1", 1), ("turn1", 2), ("norm1", 3), ("shift1", 2),
                                      ("scale1", 3), ("turn1", 3), ("halve1", 2)] + shift("1", 3) +
                                      [("start", 2), ("start", 3)], {})
            with eng.Fori(0, GROUPS - 1) as g:
                group(eng, g, body, True)
            group(eng, GROUPS - 1, body, False)

        def w_cols(w, at):
            return w[:, bass.ds(at, HQ * P)].rearrange("(k p) n -> p k n", p=P)

        def w_rows(w, at):
            return w[bass.ds(at, HQ * P), :].rearrange("(k p) n -> p k n", p=P)

        def chunk(kind, g, q, c, last=False):
            W = HQ * P
            if kind == "a":
                if c < 2:
                    return w_cols(qkv_w, 2 * INNER + q * W), wv, c
                if c < 4:
                    return w_rows(out_w, q * W), wo, c - 2
                if last:
                    return w_cols(ffn_w1, 0), wq, c - 4
                if c < 6:
                    return w_cols(qkv_w, (q + 1) * W), wq, c - 4
                return w_cols(qkv_w, INNER + (q + 1) * W), wk, c - 6
            if c < 2:
                return w_rows(ffn_w2, q * W), wo, c
            if not last:
                return w_cols(ffn_w1, (q + 1) * W), wq, c - 2
            if c < 4:
                return w_cols(qkv_w, 0), wq, c - 2
            return w_cols(qkv_w, INNER), wk, c - 4

        def n_chunks(kind, last, more):
            if kind == "a":
                return CH_A_LAST if last else CH_A
            return (CH_F_LAST if more else 2) if last else CH_F

        def slot_of(kind, q, c):
            if kind == "a":
                return c % RAW
            return (2 + c) % RAW

        def raw_count(kind, g, q, c):
            if kind == "a":
                return 16 * (1 + CH_G // RAW * g + CH_A // RAW * q + c // RAW + 1)
            return 16 * (1 + CH_G // RAW * g + (3 * CH_A + CH_A_LAST - 2) // RAW + CH_F // RAW * q + (c + 2) // RAW + 1)

        def region_free(kind, g, q, c, last):
            if kind == "a":
                return proj_a(g, q) + (1 if c < 4 else PROJ_A)
            return proj_f(g, q) + (1 if c < 2 else PROJ_F)

        def ln_of(kind, g, q, what, j):
            if what in ("norm2", "scale2", "turn2", "shift2", "halve2"):
                return ln2(g, j)
            if kind == "f":
                return ln1(g + 1, j)
            if isinstance(g, int) and g < 0:
                return ln1(0, j)
            return ln1(g, j)

        def group_of(kind, g, what):
            if kind == "f" and what in ("norm1", "scale1", "turn1", "shift1", "halve1"):
                return g + 1
            return 0 if isinstance(g, int) and g < 0 else g

        def xr_count(g, which, j):
            return 16 * (TILES * g + which * TILES // 2 + j // 2 + 1)

        def ps_out(j):
            return ps_v if j in (TILES - 3, TILES - 1) else ps_o

        first_chunks = [(w_cols(qkv_w, 0), wq, 0), (w_cols(qkv_w, 0), wq, 1),
                        (w_cols(qkv_w, INNER), wk, 0), (w_cols(qkv_w, INNER), wk, 1)]

        block = ctx.enter_context(nc.Block())

        @block.sync
        def _(sp):
            for i in range(2):
                sp.sem_inc(s_stored[i], 16)
            for c, (src, _, part) in enumerate(first_chunks):
                if c == 2:
                    sp.wait_ge(s_xr[1], 32)
                sp.dma_start(raw[c][:], src[:, 2 * part:2 * part + 2, :]).then_inc(s_raw[c], 16)
            sp.dma_start(ob[:], out_b.partition_broadcast(P)).then_inc(s_const, 16)
            sp.dma_start(b2[:], ffn_b2.partition_broadcast(P)).then_inc(s_const, 16)

            def load_rows(dst, src, g, j, s):
                sp.dma_start(dst, src[bass.ds((g * TILES + j) * P, P), :]).then_inc(s, 16)

            def load_gate(dst, which, g, j, s):
                for i in range(2):
                    row = gate_dram[which, bass.ds(2 * (g * TILES + j) + i, 1), :].rearrange("o d -> (o d)")
                    sp.dma_start(dst[i * T:(i + 1) * T, :], row.partition_broadcast(T)).then_inc(s, 16)

            def load_ln2(g, j):
                b = j % 2
                if j < 2:
                    sp.wait_ge(s_xn, ln2(g, 0))
                    sp.wait_ge(s_end, TILES * g + FIN0)
                    sp.wait_ge(s_twice, TILES * g + 2)
                    load_gate(gt[b][:], 0, g, j, s_gt[b])
                else:
                    sp.wait_ge(s_gated, TILES * g + j - 1)
                    load_gate(gt[b][:], 0, g, j, s_gt[b])
                    sp.wait_ge(s_twice, TILES * g + j + 1)
                load_rows(xr[b][:], rows, g, j, s_xr[b])

            def load_fin(g, j):
                if j < FIN:
                    sp.wait_ge(s_twice, TILES * g + TILES + 2)
                else:
                    sp.wait_ge(s_end, TILES * g + j - FIN + 1 + FIN0)
                sp.wait_ge(s_stored[j % 2], 16 + 16 * (TILES * g + j // 2 + 1))
                load_rows(qT[:, j % FIN, :], rows, g, j, s_sum_here[j % FIN])
                load_gate(kT[:, j % FIN, :], 1, g, j, s_gate_here[j % FIN])

            def load_chunk(kind, g, q, c, last):
                n = (chunks_a if kind == "a" else chunks_f)(g, q) + c
                src, _, part = chunk(kind, g, q, c, last)
                slot = slot_of(kind, q, c)
                sp.wait_ge(s_w_lo, n - RAW + 1)
                sp.dma_start(raw[slot][:], src[:, 2 * part:2 * part + 2, :]).then_inc(s_raw[slot], 16)

            def body(kind, g, q, steps, at):
                if isinstance(g, int) and g < 0:
                    return
                last = at.get("last", False)
                if kind == "a" and last:
                    load_ln2(g, 0)
                    load_ln2(g, 1)
                more = not (isinstance(g, int) and g == GROUPS - 1)
                ahead = 2
                for c in range(ahead if kind == "f" and at.get("first") else 0, n_chunks(kind, last, more)):
                    if kind == "a" and c == 4:
                        sp.wait_ge(s_value_taken, tiles_a(g, q) + 1)
                        sp.dma_start(bv[:], qkv_b[bass.ds(2 * INNER + q * HQ * P, HQ * P)].partition_broadcast(P))\
                            .then_inc(s_bv, 16)
                    load_chunk(kind, g, q, c, last)
                if kind == "a" and last:
                    for c in range(ahead):
                        load_chunk("f", g, 0, c, False)
                if kind == "f" and last:
                    for j in range(FIN):
                        load_fin(g, j)
                for what, j in steps:
                    if what == "norm2":
                        if j + 2 < TILES:
                            load_ln2(g, j + 2)
                        sp.wait_ge(s_twice, TILES * g + j + 1 + 2)
                        sp.dma_start(rows[bass.ds((g * TILES + j) * P, P), :], st[j % 2][:]).then_inc(s_stored[j % 2], 16)
                    if what == "fin":
                        sp.wait_ge(s_end, TILES * g + j + 1 + FIN0)
                        sp.dma_start(out_rows[bass.ds((g * TILES + j) * P, P), :], st[j % 2][:]).then_inc(s_stored[j % 2], 16)
                        if j + FIN < TILES:
                            load_fin(g, j + FIN)
            groups(sp, body)
            for i in range(2):
                sp.wait_ge(s_stored[i], 16 + 16 * TILES * GROUPS)

        @block.gpsimd
        def _(pool):
            nc.gpsimd.memset(pr[:], 0.0).then_inc(s_fill, 1)
            pool.wait_ge(s_fill, 1)
            nc.gpsimd.memset(eps[:], EPS).then_inc(s_fill, 1)
            pool.wait_ge(s_fill, 2)
            nc.gpsimd.memset(mhalf[:], -0.5).then_inc(s_fill, 1)
            pool.wait_ge(s_fill, 3)
            pool.sem_inc(s_twice, 2)
            pool.sem_inc(s_end, FIN0)

            def body(kind, g, q, steps, at):
                for what, j in steps:
                    b = j % 2
                    if what == "norm2":
                        if j < HT:
                            pool.wait_ge(s_out_taken, outs_a(g, QUADS - 1) + j + 2)
                            pool.wait_ge(s_gt[b], 32 * (TILES // 2 * g + j // 2 + 1))
                            nc.gpsimd.tensor_tensor(y[:, j, :], y[:, j, :], gt[b][:], ALU.mult).then_inc(s_gated, 1)
                        pool.wait_ge(s_gated, TILES * g + j + 1)
                        pool.wait_ge(s_xr[b], xr_count(g, 1, j))
                        if j >= 2:
                            pool.wait_ge(s_xn, ln2(g, j) - 1)
                        nc.gpsimd.tensor_tensor(x2[b][:], y[:, j, :], xr[b][:], ALU.add).then_inc(s_x2, 1)
                    if what in ("norm1", "norm2"):
                        n = ln_of(kind, g, q, what, j)
                        pool.wait_ge(s_mv, n + 1)
                        nc.gpsimd.tensor_tensor(veps[:], mv[:, 1:2], eps[:], ALU.add).then_inc(s_veps, 1)
                        pool.wait_ge(s_veps, n + 1)
                        nc.gpsimd.tensor_tensor(rstd[:], veps[:], mhalf[:], ALU.pow).then_inc(s_rstd, 1)
                    if what == "norm2":
                        pool.wait_ge(s_x2, TILES * g + j + 1)
                        pool.wait_ge(s_stored[b], 16 * (TILES * g + j // 2 + 1))
                        nc.gpsimd.tensor_tensor(st[b][:], x2[b][:], xr[b][:], ALU.add).then_inc(s_twice, 1)
                    if what == "fin":
                        pool.wait_ge(s_out_taken, outs_f(g, q) + j + 2)
                        pool.wait_ge(s_gate_here[j % FIN], 32 * (TILES // FIN * g + j // FIN + 1))
                        pool.wait_ge(s_stored[b], 16 * (TILES * g + TILES // 2 + j // 2 + 1))
                        nc.gpsimd.tensor_tensor(st[b][:], y[:, j, :], kT[:, j % FIN, :], ALU.mult).then_inc(s_end_gated, 1)
                        pool.wait_ge(s_end_gated, TILES * g + j + 1)
                        pool.wait_ge(s_sum_here[j % FIN], 16 * (TILES // FIN * g + j // FIN + 1))
                        nc.gpsimd.tensor_tensor(st[b][:], st[b][:], qT[:, j % FIN, :], ALU.add).then_inc(s_end, 1)
            groups(pool, body)

        @block.scalar
        def _(act):
            act.sem_inc(s_proj_taken, 2)

            def load_rows(dst, src, g, j, s):
                act.dma_start(dst[:], src[bass.ds((g * TILES + j) * P, P), :]).then_inc(s, 16)

            def load_ln1(g, j):
                b = j % 2
                if isinstance(g, int) and g == 0:
                    wait(act, s_xn, j - 1)
                else:
                    if j < 2:
                        act.wait_ge(s_twice, TILES * g + 2)
                        act.wait_ge(s_xn, ln1(g, 0))
                    else:
                        act.wait_ge(s_xn, ln1(g, j) - 1)
                load_rows(xr[b], rows, g, j, s_xr[b])

            load_ln1(0, 0)
            load_ln1(0, 1)
            act.dma_start(qkvb[:], qkv_b.rearrange("(c p) -> p c", p=P), allow_slow_non_contiguous=True).then_inc(s_const, 16)
            act.dma_start(f1b[:], ffn_b1.rearrange("(c p) -> p c", p=P), allow_slow_non_contiguous=True).then_inc(s_const, 16)

            def body(kind, g, q, steps, at):
                last, first = at.get("last", False), at.get("first", False)
                for what, j in steps:
                    b = j % 2
                    if what == "split":
                        n = (chunks_a if kind == "a" else chunks_f)(g, q) + j
                        _, dst, part = chunk(kind, g, q, j, last)
                        s = slot_of(kind, q, j)
                        act.wait_ge(s_raw[s], raw_count(kind, g, q, j))
                        act.wait_ge(s_proj, region_free(kind, g, q, j, last))
                        if kind == "f" and last and j >= 4:
                            act.wait_ge(s_out, outs_f(g, q) + HT)
                        nc.scalar.copy(dst[0][:, 2 * part:2 * part + 2, :], raw[s][:]).then_inc(s_w_hi, 1)
                    if what == "proj":
                        n = proj_a(g, q) + j
                        hf, w, hd = j // 8, j // HQ % 2, j % HQ
                        act.wait_ge(s_proj, n + 1)
                        if first and j < 2 * HQ:
                            act.wait_ge(s_end, TILES * g - FIN + hd + 1 + FIN0)
                        nc.scalar.activation((qT, kT)[w][:, hd, :], ps_p[b][:], ACT.Identity,
                                             bias=qkvb[:, bass.ds(w * H + q * HQ + hd, 1)]).then_inc(s_proj_taken, 1)
                    if what == "fproj":
                        n = proj_f(g, q) + j
                        act.wait_ge(s_proj, n + 1)
                        act.wait_ge(s_hid_lo, hid(g, q) + j + 1)
                        nc.scalar.activation(v_sb[b][:], ps_p[b][:], ACT.Gelu,
                                             bias=f1b[:, bass.ds(q * HQ + j % HQ, 1)]).then_inc(s_proj_taken, 1)
                    if what == "soften":
                        act.wait_ge(s_score_taken, tiles_a(g, q) + j + 2)
                        nc.scalar.activation(ex[:], sc[:], ACT.Exp, scale=SCALE).then_inc(s_exp, 1)
                    if what == "turn":
                        act.wait_ge(s_turned, tiles_a(g, q) + j + 2)
                        nc.scalar.copy(pT[:], ps_pt[:]).then_inc(s_turned_taken, 1)
                    if what == "pv":
                        act.wait_ge(s_head, tiles_a(g, q) + j + 1)
                        nc.scalar.copy(at_hi[:, j % 4, :], ps_pv[:]).then_inc(s_head_hi, 1)
                    if what == "start":
                        act.wait_ge(s_raw[j], 16)
                        nc.scalar.copy(first_chunks[j][1][0][:, 2 * (j % 2):2 * (j % 2) + 2, :], raw[j][:]).then_inc(s_w_hi, 1)
                        if j == 3:
                            act.wait_ge(s_const, 32)
                    starting = isinstance(g, int) and g < 0
                    if what == ("norm1" if starting else "turn1") and j + 2 < TILES and not (kind == "f" and j + 2 >= 6):
                        load_ln1(group_of(kind, g, what), j + 2)
                    if what in ("shift1", "shift2"):
                        n = ln_of(kind, g, q, what, j)
                        act.wait_ge(s_aff, n + 1)
                        nc.scalar.copy(xT_hi[:, :, j * P:(j + 1) * P], tmp[:].rearrange("p (k t) -> p k t", k=KC)).then_inc(s_xhi, 1)
                    if kind == "f" and last and what == "fproj" and j == 0 and not (isinstance(g, int) and g == GROUPS - 1):
                        load_ln1(g + 1, 0)
                        load_ln1(g + 1, 1)
            groups(act, body)

        @block.vector
        def _(dve):
            for s, n in ((s_value_taken, 1), (s_score_taken, 1), (s_head_lo, 1), (s_out_taken, 1), (s_hid_lo, 2)):
                dve.sem_inc(s, n)

            def moments(src, lidx):
                nc.vector.bn_stats(stat[:], src[:]).then_inc(s_moments, 1)
                dve.wait_ge(s_moments, lidx + 1)
                dve.nop(nofuse=True)
                nc.vector.bn_aggr(mv[:], stat[:]).then_inc(s_mv, 1)

            def scale(src, lidx, b):
                dve.wait_ge(s_rstd, lidx + 1)
                wait(dve, s_lnT, lidx - 1)
                nc.vector.tensor_scalar(xn[b][:], src[:], mv[:, 0:1], rstd[:], ALU.subtract, ALU.mult).then_inc(s_xn, 1)

            def body(kind, g, q, steps, at):
                last, first = at.get("last", False), at.get("first", False)
                for what, j in steps:
                    b = j % 2
                    if what == "split":
                        n = (chunks_a if kind == "a" else chunks_f)(g, q) + j
                        _, dst, part = chunk(kind, g, q, j, last)
                        s = slot_of(kind, q, j)
                        dve.wait_ge(s_w_hi, n + 1)
                        nc.vector.tensor_tensor(dst[1][:, 2 * part:2 * part + 2, :], raw[s][:],
                                                dst[0][:, 2 * part:2 * part + 2, :].bitcast(F32), ALU.subtract).then_inc(s_w_lo, 1)
                    if what == "start":
                        dve.wait_ge(s_w_hi, j + 1)
                        _, dst, part = first_chunks[j]
                        nc.vector.tensor_tensor(dst[1][:, 2 * part:2 * part + 2, :], raw[j][:],
                                                dst[0][:, 2 * part:2 * part + 2, :].bitcast(F32), ALU.subtract).then_inc(s_w_lo, 1)
                    if what == "keep":
                        dve.wait_ge(s_value, tiles_a(g, q) + j + 1)
                        if j % HT >= 2:
                            dve.wait_ge(s_head, tiles_a(g, q) + j - 1)
                        if j == 0:
                            dve.wait_ge(s_bv, 16 * (QUADS * g + q + 1))
                        nc.vector.tensor_tensor(v_sb[b][:], (ps_v, ps_o)[b][:], bv[:], ALU.add).then_inc(s_value_taken, 1)
                    if what == "score":
                        n = tiles_a(g, q) + j
                        if first and j == 0:
                            dve.wait_ge(s_fill, 1)
                        dve.wait_ge(s_score, n + 1)
                        S = ps_s[:, 0:HQ * T].rearrange("p (h t) -> p h t", h=HQ)
                        nc.vector.tensor_reduce(row_max[:], S, AX.X, ALU.max).then_inc(s_max, 1)
                        dve.wait_ge(s_max, n + 1)
                        nc.vector.tensor_tensor(sc[:], S, row_max[:].unsqueeze(2).broadcast_to([P, HQ, T]), ALU.subtract).then_inc(s_score_taken, 1)
                    if what == "soften":
                        n = tiles_a(g, q) + j
                        dve.wait_ge(s_exp, n + 1)
                        nc.vector.tensor_reduce(row_sum[:], ex[:], AX.X, ALU.add).then_inc(s_sum, 1)
                        dve.wait_ge(s_sum, n + 1)
                        nc.vector.reciprocal(row_rec[:], row_sum[:]).then_inc(s_rec, 1)
                        dve.wait_ge(s_rec, n + 1)
                        dve.wait_ge(s_turned, n + 1)
                        for i in range(2):
                            r = slice(i * T, (i + 1) * T)
                            done = nc.vector.tensor_tensor(pr[r, :, i * T:(i + 1) * T], ex[r, :, :],
                                                             row_rec[r, :].unsqueeze(2).broadcast_to([T, HQ, T]), ALU.mult)
                        done.then_inc(s_prob, 1)
                    if what == "lower":
                        n = tiles_a(g, q) + j
                        dve.wait_ge(s_head_hi, n + 1)
                        nc.vector.tensor_tensor(at_lo[:, j % 4, :], ps_pv[:], at_hi[:, j % 4, :].bitcast(F32),
                                                ALU.subtract).then_inc(s_head_lo, 1)
                    if what == "out":
                        dve.wait_ge(s_out, outs_a(g, q) + j + 1)
                        if first and j == 0:
                            dve.wait_ge(s_const, 64)
                            dve.wait_ge(s_end, TILES * g + FIN0)
                        nc.vector.tensor_tensor(y[:, j, :], ps_out(j)[:], ob[:] if first else y[:, j, :], ALU.add).then_inc(s_out_taken, 1)
                        if last and j >= HT:
                            dve.wait_ge(s_out_taken, outs_a(g, q) + j + 2)
                            dve.wait_ge(s_gated, TILES * g + j)
                            dve.wait_ge(s_gt[b], 32 * (TILES // 2 * g + j // 2 + 1))
                            nc.vector.tensor_tensor(y[:, j, :], y[:, j, :], gt[b][:], ALU.mult).then_inc(s_gated, 1)
                    if what == "fproj":
                        n = hid(g, q) + j
                        dve.wait_ge(s_proj_taken, 2 + proj_f(g, q) + j + 1)
                        hi, lo = (wk, (at_hi, at_lo))[j // HQ]
                        nc.vector.tensor_copy(hi[:, j % HQ, :], v_sb[b][:]).then_inc(s_hid_hi, 1)
                        dve.wait_ge(s_hid_hi, n + 1)
                        nc.vector.tensor_tensor(lo[:, j % HQ, :], v_sb[b][:], hi[:, j % HQ, :].bitcast(F32), ALU.subtract).then_inc(s_hid_lo, 1)
                    if what == "fout":
                        dve.wait_ge(s_out, outs_f(g, q) + j + 1)
                        nc.vector.tensor_tensor(y[:, j, :], (ps_o, ps_v)[b][:], b2[:] if first else y[:, j, :], ALU.add).then_inc(s_out_taken, 1)
                    if what == "norm1":
                        n = ln_of(kind, g, q, what, j)
                        gg = g + 1 if kind == "f" else (0 if isinstance(g, int) and g < 0 else g)
                        dve.wait_ge(s_xr[b], xr_count(gg, 0, j))
                        moments(xr[b], n)
                    if what == "norm2":
                        n = ln_of(kind, g, q, what, j)
                        dve.wait_ge(s_x2, TILES * g + j + 1)
                        moments(x2[b], n)
                    if what in ("scale1", "scale2"):
                        scale((xr, x2)[what == "scale2"][b], ln_of(kind, g, q, what, j), b)
                    if what in ("shift1", "shift2"):
                        n = ln_of(kind, g, q, what, j)
                        two = 2 * (what == "shift2")
                        at_b = bass.ds(2 * (group_of(kind, g, what) * TILES + j), 2)
                        dve.wait_ge(s_lnT, n + 1)
                        wait(dve, s_xlo, n)
                        t4, p4 = (a[:].rearrange("p (k b t) -> p k b t", k=KC, b=2) for a in (tmp, ps_ln))
                        factor, term = (adaT[:, two + i, :, at_b].unsqueeze(3).broadcast_to([P, KC, 2, T]) for i in (1, 0))
                        nc.vector.tensor_tensor(t4, p4, factor, ALU.mult).then_inc(s_scaled, 1)
                        dve.wait_ge(s_scaled, n + 1)
                        nc.vector.tensor_tensor(t4, t4, term, ALU.add).then_inc(s_aff, 1)
                    if what in ("halve1", "halve2"):
                        n = ln_of(kind, g, q, what, j)
                        dve.wait_ge(s_xhi, n + 1)
                        nc.vector.tensor_tensor(xT_lo[:, :, j * P:(j + 1) * P], tmp[:].rearrange("p (k t) -> p k t", k=KC),
                                                xT_hi[:, :, j * P:(j + 1) * P].bitcast(F32), ALU.subtract).then_inc(s_xlo, 1)
            groups(dve, body)

        @block.tensor
        def _(pe):
            pe.sem_inc(s_turned, 1)

            def product(dst, a, w, ready=None):
                for k in range(KC):
                    if ready:
                        ready(k)
                    for i, (ha, hw) in enumerate(((0, 0), (0, 1), (1, 0))):
                        last = nc.tensor.matmul(dst, a(ha, k), w(hw, k), start=(k == 0 and i == 0), stop=(k == KC - 1 and i == 2))
                return last

            xT = (xT_hi, xT_lo)
            at = (at_hi, at_lo)

            def body(kind, g, q, steps, flags):
                last, first = flags.get("last", False), flags.get("first", False)
                for what, j in steps:
                    b = j % 2
                    if what == "proj":
                        hf, w, hd = j // 8, j // HQ % 2, j % HQ
                        if j == 0:
                            pe.wait_ge(s_w_lo, chunks_a(g, q) - 2)
                            pe.wait_ge(s_xlo, ln1(g, HT))
                        if j == HQ:
                            pe.wait_ge(s_w_lo, chunks_a(g, q))
                        if j == 8:
                            pe.wait_ge(s_xlo, ln1(g, TILES))
                        pe.wait_ge(s_proj_taken, proj_a(g, q) + j + 1)
                        W = (wq, wk)[w]
                        product(ps_p[b][:], lambda h, k: W[h][:, k, hd * P:(hd + 1) * P],
                                lambda h, k: xT[h][:, k, hf * HALF:(hf + 1) * HALF]).then_inc(s_proj, 1)
                    if what == "fproj":
                        hf, m = j // HQ, j % HQ
                        if j == 0:
                            pe.wait_ge(s_w_lo, chunks_f(g, q))
                            pe.wait_ge(s_xlo, ln2(g, HT))
                        if j == HQ:
                            pe.wait_ge(s_xlo, ln2(g, TILES))
                        pe.wait_ge(s_proj_taken, proj_f(g, q) + j + 1)
                        product(ps_p[b][:], lambda h, k: wq[h][:, k, m * P:(m + 1) * P],
                                lambda h, k: xT[h][:, k, hf * HALF:(hf + 1) * HALF]).then_inc(s_proj, 1)
                    if what == "value":
                        n = tiles_a(g, q) + j
                        if j == 0:
                            pe.wait_ge(s_w_lo, chunks_a(g, q) + 2)
                            pe.wait_ge(s_out_taken, outs_a(g, q) + 1)
                        if j == HT:
                            pe.wait_ge(s_out_taken, outs_a(g, q) + HT + 1)
                        pe.wait_ge(s_value_taken, n + (j == 0))
                        product((ps_v, ps_o)[b][:], lambda h, k: xT[h][:, k, j * P:(j + 1) * P],
                                lambda h, k: wv[h][:, k, :]).then_inc(s_value, 1)
                    if what == "score":
                        n = tiles_a(g, q) + j
                        pe.wait_ge(s_proj_taken, 2 + proj_a(g, q) + 8 * (j // HT + 1))
                        pe.wait_ge(s_score_taken, n + 1)
                        for hd in range(HQ):
                            for i in range(2):
                                c = (j % HT) * P + i * T
                                done = nc.tensor.matmul(ps_s[i * T:(i + 1) * T, hd * T:(hd + 1) * T], qT[:, hd, c:c + T],
                                                          kT[:, hd, c:c + T], start=True, stop=True)
                        done.then_inc(s_score, 1)
                    if what == "turn":
                        n = tiles_a(g, q) + j
                        pe.wait_ge(s_prob, n + 1)
                        for hd in range(HQ):
                            done = nc.tensor.transpose(ps_pt[:, hd * P:(hd + 1) * P], pr[:, hd, :], ident[:])
                        done.then_inc(s_turned, 1)
                    if what == "pv":
                        n = tiles_a(g, q) + j
                        pe.wait_ge(s_turned_taken, n + 1)
                        pe.wait_ge(s_value_taken, n + 2)
                        pe.wait_ge(s_head_lo, n + 1)
                        for hd in range(HQ):
                            done = nc.tensor.matmul(ps_pv[:, hd * P:(hd + 1) * P], v_sb[b][:, hd * P:(hd + 1) * P],
                                                      pT[:, hd * P:(hd + 1) * P], start=True, stop=True)
                        done.then_inc(s_head, 1)
                    if what == "out":
                        n = tiles_a(g, q) + j
                        if j == 0:
                            pe.wait_ge(s_w_lo, chunks_a(g, q) + 4)
                        pe.wait_ge(s_head_lo, n + 2)
                        if j == HT:
                            pe.wait_ge(s_value_taken, tiles_a(g, q) + TILES + 1)
                        pe.wait_ge(s_out_taken, outs_a(g, q) + j + (j <= HT))
                        product(ps_out(j)[:], lambda h, k: at[h][:, j % 4, k * P:(k + 1) * P],
                                lambda h, k: wo[h][:, k, :]).then_inc(s_out, 1)
                    if what == "fout":
                        hf = j // HT
                        if j == 0:
                            pe.wait_ge(s_w_lo, chunks_f(g, q) + 2)
                        pe.wait_ge(s_out_taken, outs_f(g, q) + (j if j else 1))
                        Hh = (wk, at)[hf]
                        c = (j % HT) * P
                        ready = (lambda k: pe.wait_ge(s_hid_lo, 2 + hid(g, q) + HQ * hf + k + 1)) if j % HT == 0 else None
                        product((ps_o, ps_v)[b][:], lambda h, k: Hh[h][:, k, c:c + P],
                                lambda h, k: wo[h][:, k, :], ready).then_inc(s_out, 1)
                    if what in ("turn1", "turn2"):
                        n = ln_of(kind, g, q, what, j)
                        pe.wait_ge(s_xn, n + 1)
                        wait(pe, s_aff, n)
                        for k in range(KC):
                            done = nc.tensor.transpose(ps_ln[:, k * P:(k + 1) * P], xn[b][:, k * P:(k + 1) * P], ident[:])
                        done.then_inc(s_lnT, 1)
            groups(pe, body)


_INS = ['x', 'cond_2048', 'L0_cond_W_ih', 'L0_cond_W_hh', 'L0_cond_b_ih', 'L0_cond_b_hh', 'L1_cond_ada_w',
        'L1_cond_ada_b', 'L1_cond_qkv_w', 'L1_cond_qkv_b', 'L1_cond_out_w', 'L1_cond_out_b', 'L1_cond_ffn_w1',
        'L1_cond_ffn_b1', 'L1_cond_ffn_w2', 'L1_cond_ffn_b2']
_OUTS = [((64, 64, 512), 'float32')]


def kernel(**inputs):
    import numpy as _np
    import concourse.bacc as _bacc
    from concourse import mybir as _mybir
    from concourse.bass_utils import run_bass_kernel_spmd as _run

    nc = _bacc.Bacc("TRN2", target_bir_lowering=False, num_devices=1)
    arrays, args = {}, []
    for name in _INS:
        a = _np.ascontiguousarray(inputs[name])
        arrays[f"in_{name}_dram"] = a
        args.append(nc.dram_tensor(f"in_{name}_dram", a.shape, _mybir.dt.from_np(a.dtype), kind="ExternalInput").ap())
    for i, (shape, dtype) in enumerate(_OUTS):
        dt = _mybir.dt.from_np(_np.dtype(dtype))
        args.append(nc.dram_tensor(f"out_{i}_dram", shape, dt, kind="ExternalOutput").ap())
    gru_then_transformer(nc, *args)
    r = _run(nc, [arrays], core_ids=[0])
    return r.results[0]["out_0_dram"]
```
